# Optimizing a Trainium2 kernel written in Bass

```python
import numpy as np
import jax
import jax.numpy as jnp

def _softmax(x, axis=-1):
    return jax.nn.softmax(x, axis=axis)

def _gelu(x):
    return jax.nn.gelu(x, approximate=True)

def _silu(x):
    return jax.nn.silu(x)

def _sigmoid(x):
    return jax.nn.sigmoid(x)

def _layernorm(x, axis=-1, eps=1e-05):
    m = jnp.mean(x, axis=axis, keepdims=True)
    v = jnp.var(x, axis=axis, keepdims=True)
    return (x - m) / jnp.sqrt(v + eps)

def _scatter_add(tgt, idx, src, axis=0):
    return tgt.at[idx].add(src)

def _segment_sum(src, seg, n):
    return jax.ops.segment_sum(src, seg, n)
kernel_name = 'mk_flamingo_gated_d2_seqx_r4_31cad4'

def setup_inputs(seed: int=0):
    np.random.seed(seed)
    _w = jnp.asarray

    def _rec_inputs():
        import jax
        import jax.numpy as jnp
        _rk = jax.random.key(seed)
        x = -7.109e-05 + 0.9999 * jax.random.normal(jax.random.fold_in(_rk, 1), (4, 512, 512), jnp.float32)
        _lenS = 512 - jax.random.randint(jax.random.fold_in(_rk, 7), (4,), 0, max(1, 512 // 4) + 1, jnp.int32)
        _lenS2 = 512 - jax.random.randint(jax.random.fold_in(_rk, 8), (4,), 0, max(1, 512 // 4) + 1, jnp.int32)
        _ctx_512P = jax.random.normal(jax.random.fold_in(_rk, 11), (4, 16, 128), jnp.float32)
        _ctx_512c = jax.random.dirichlet(jax.random.fold_in(_rk, 511), 0.3 * jnp.ones((16,), jnp.float32), (4, 512))
        _ctx_512t = jnp.einsum('bsk,bkd->bsd', _ctx_512c, _ctx_512P)
        _ctx_512t = _ctx_512t * jax.lax.rsqrt(jnp.mean(jnp.square(_ctx_512t)) + 1e-12) * 0.953939
        ctx_512 = 2.81802e-05 + 1.00001 * (_ctx_512t + 0.3 * jax.random.normal(jax.random.fold_in(_rk, 611), (4, 512, 128), jnp.float32))
        _g = jax.random.normal(jax.random.fold_in(_rk, 9001), (2, 2), jnp.float32)
        _g = jnp.sign(_g) * jnp.maximum(jnp.abs(_g), 1.0) + (_g == 0) * 1.0
        g_xattn = _g[0]
        g_ffn = _g[1]
        return (x, ctx_512, g_xattn, g_ffn)
    x, ctx_512, g_xattn, g_ffn = _rec_inputs()

    def _L0_xattn_setup():
        import jax, jax.numpy as jnp
        import numpy as np
        EPS = 1e-06
        IMAGE_DIMS = 512
        key = jax.random.key(seed)
        k1, k2, k3 = jax.random.split(key, 3)
        B, I, J, D = (16, 512, 512, 128)
        p = jax.random.normal(k1, (B, I, J), dtype=jnp.float32)
        k_v = jax.random.normal(k2, (B, J, D), dtype=jnp.float32)
        W_k = jax.random.normal(k3, (D, D), dtype=jnp.float32) * (1.0 / np.sqrt(D))
        b_k = jnp.zeros((D,), dtype=jnp.float32)
        ln_gamma = jnp.ones((J,), dtype=jnp.float32)
        ln_beta = jnp.zeros((J,), dtype=jnp.float32)
        return {'p': p, 'k_v': k_v, 'W_k': W_k, 'b_k': b_k, 'ln_gamma': ln_gamma, 'ln_beta': ln_beta}
    _L0_xattn_all = _L0_xattn_setup()
    _L0_xattn_in = {k: v for k, v in _L0_xattn_all.items() if k in ('W_k', 'b_k', 'ln_gamma', 'ln_beta')}
    del _L0_xattn_all

    def _L0_ffn_setup():
        import jax, jax.numpy as jnp
        import numpy as np
        TOP_K = 8
        NUM_EXPERTS = 32
        key = jax.random.key(seed)
        k1, k2, k3, k4, k5 = jax.random.split(key, 5)
        B, S, D, M, E = (4, 256, 512, 192, NUM_EXPERTS)
        return {'hidden_states': jax.random.normal(k1, (B, S, D), dtype=jnp.float32), 'gate_kernel': jax.random.normal(k2, (D, E), dtype=jnp.float32) * 0.02, 'gate_proj': jax.random.normal(k3, (E, D, M), dtype=jnp.float32) * 0.02, 'up_proj': jax.random.normal(k4, (E, D, M), dtype=jnp.float32) * 0.02, 'down_proj': jax.random.normal(k5, (E, M, D), dtype=jnp.float32) * 0.02}
    _L0_ffn_all = _L0_ffn_setup()
    _L0_ffn_in = {k: v for k, v in _L0_ffn_all.items() if k in ('gate_kernel', 'gate_proj', 'up_proj', 'down_proj')}
    del _L0_ffn_all

    def _L1_xattn_setup():
        import jax, jax.numpy as jnp
        import numpy as np
        B, S, L = (2, 256, 256)
        DIM_Q, H, K, D_C, D_CQ, R = (512, 16, 128, 128, 384, 64)

        def _rope_tables(length, dim):
            inv = 1.0 / 10000.0 ** (jnp.arange(0, dim, 2, dtype=jnp.float32) / dim)
            f = jnp.arange(length, dtype=jnp.float32)[:, None] * inv[None, :]
            sin = jnp.repeat(jnp.sin(f), 2, axis=-1)
            cos = jnp.repeat(jnp.cos(f), 2, axis=-1)
            return (sin, cos)

        def _rotate_half(x):
            half = x.shape[-1] // 2
            return jnp.concatenate([-x[..., half:], x[..., :half]], axis=-1)

        def _apply_rope(x, sin, cos):
            return x * cos + _rotate_half(x) * sin
        key = jax.random.key(seed)
        ks = jax.random.split(key, 8)
        return {'hidden_q': jax.random.normal(ks[0], (B, S, DIM_Q), jnp.float32), 'kv_c': jax.random.normal(ks[1], (B, L, D_C), jnp.float32), 'Wq': jax.random.normal(ks[2], (H * K, DIM_Q), jnp.float32) / np.sqrt(DIM_Q).astype(np.float32), 'w_kc_q': jax.random.normal(ks[3], (H, K, D_CQ), jnp.float32) / np.sqrt(K).astype(np.float32), 'w_kc_kv': jax.random.normal(ks[4], (H, K, D_C), jnp.float32) / np.sqrt(K).astype(np.float32), 'W_qr': jax.random.normal(ks[5], (H, D_CQ, R), jnp.float32) / np.float32(np.sqrt(D_CQ) * np.sqrt(R)), 'W_kr': jax.random.normal(ks[6], (H, D_C, R), jnp.float32) / np.sqrt(D_C).astype(np.float32), 'Wo': jax.random.normal(ks[7], (DIM_Q, H * K), jnp.float32) / np.sqrt(H * K).astype(np.float32)}
    _L1_xattn_all = _L1_xattn_setup()
    _L1_xattn_in = {k: v for k, v in _L1_xattn_all.items() if k in ('Wq', 'w_kc_q', 'w_kc_kv', 'W_qr', 'W_kr', 'Wo')}
    del _L1_xattn_all

    def _L1_ffn_setup():
        import jax, jax.numpy as jnp
        import numpy as np
        E = 16
        K = 2
        D = 512
        I = 352
        CAP = 256
        VOCAB = 32320
        key = jax.random.key(seed)
        ks = jax.random.split(key, 11)
        B, S = (4, 256)
        sd = 1.0 / np.sqrt(D)
        si = 1.0 / np.sqrt(I)
        return {'x': jax.random.normal(ks[0], (B, S, D), jnp.float32), 'input_ids': jax.random.randint(ks[1], (B, S), 0, VOCAB, dtype=jnp.int64), 'gate_w': jax.random.normal(ks[2], (E, D), jnp.float32) * sd, 'gate_b': jax.random.normal(ks[3], (E,), jnp.float32) * 0.01, 'W1': jax.random.normal(ks[4], (E, I, D), jnp.float32) * sd, 'W3': jax.random.normal(ks[5], (E, I, D), jnp.float32) * sd, 'W2': jax.random.normal(ks[6], (E, D, I), jnp.float32) * si, 'Ws1': jax.random.normal(ks[7], (I, D), jnp.float32) * sd, 'Ws3': jax.random.normal(ks[8], (I, D), jnp.float32) * sd, 'Ws2': jax.random.normal(ks[9], (D, I), jnp.float32) * si}
    _L1_ffn_all = _L1_ffn_setup()
    _L1_ffn_in = {k: v for k, v in _L1_ffn_all.items() if k in ('input_ids', 'gate_w', 'gate_b', 'W1', 'W3', 'W2', 'Ws1', 'Ws3', 'Ws2')}
    del _L1_ffn_all
    return {'x': x, 'ctx_512': ctx_512, 'g_xattn': g_xattn, 'g_ffn': g_ffn, 'L0_xattn_W_k': _L0_xattn_in['W_k'], 'L0_xattn_b_k': _L0_xattn_in['b_k'], 'L0_xattn_ln_gamma': _L0_xattn_in['ln_gamma'], 'L0_xattn_ln_beta': _L0_xattn_in['ln_beta'], 'L0_ffn_gate_kernel': _L0_ffn_in['gate_kernel'], 'L0_ffn_gate_proj': _L0_ffn_in['gate_proj'], 'L0_ffn_up_proj': _L0_ffn_in['up_proj'], 'L0_ffn_down_proj': _L0_ffn_in['down_proj'], 'L1_xattn_Wq': _L1_xattn_in['Wq'], 'L1_xattn_w_kc_q': _L1_xattn_in['w_kc_q'], 'L1_xattn_w_kc_kv': _L1_xattn_in['w_kc_kv'], 'L1_xattn_W_qr': _L1_xattn_in['W_qr'], 'L1_xattn_W_kr': _L1_xattn_in['W_kr'], 'L1_xattn_Wo': _L1_xattn_in['Wo'], 'L1_ffn_input_ids': _L1_ffn_in['input_ids'], 'L1_ffn_gate_w': _L1_ffn_in['gate_w'], 'L1_ffn_gate_b': _L1_ffn_in['gate_b'], 'L1_ffn_W1': _L1_ffn_in['W1'], 'L1_ffn_W3': _L1_ffn_in['W3'], 'L1_ffn_W2': _L1_ffn_in['W2'], 'L1_ffn_Ws1': _L1_ffn_in['Ws1'], 'L1_ffn_Ws3': _L1_ffn_in['Ws3'], 'L1_ffn_Ws2': _L1_ffn_in['Ws2']}

def reference(x, ctx_512, g_xattn, g_ffn, L0_xattn_W_k, L0_xattn_b_k, L0_xattn_ln_gamma, L0_xattn_ln_beta, L0_ffn_gate_kernel, L0_ffn_gate_proj, L0_ffn_up_proj, L0_ffn_down_proj, L1_xattn_Wq, L1_xattn_w_kc_q, L1_xattn_w_kc_kv, L1_xattn_W_qr, L1_xattn_W_kr, L1_xattn_Wo, L1_ffn_input_ids, L1_ffn_gate_w, L1_ffn_gate_b, L1_ffn_W1, L1_ffn_W3, L1_ffn_W2, L1_ffn_Ws1, L1_ffn_Ws3, L1_ffn_Ws2):
    import jax
    import jax.numpy as jnp

    def _L0_xattn_ref(p, k_v, W_k, b_k, ln_gamma, ln_beta):
        import jax, jax.numpy as jnp
        import numpy as np
        EPS = 1e-06
        IMAGE_DIMS = 512
        kv = k_v @ W_k.T + b_k
        out = jnp.einsum('bij,bjd->bid', p, kv)
        scale = IMAGE_DIMS ** (-0.5)
        sim = jnp.einsum('bid,bjd->bij', out, kv) * scale
        mu = jnp.mean(sim, axis=-1, keepdims=True)
        var = jnp.var(sim, axis=-1, keepdims=True)
        sim = (sim - mu) * jax.lax.rsqrt(var + EPS) * ln_gamma + ln_beta
        attn = jax.nn.softmax(sim, axis=-1)
        return attn

    def _L0_ffn_ref(hidden_states, gate_kernel, gate_proj, up_proj, down_proj):
        import jax, jax.numpy as jnp
        import numpy as np
        TOP_K = 8
        NUM_EXPERTS = 32
        B, S, D = hidden_states.shape
        T = B * S
        x2d = hidden_states.reshape(T, D)
        router_logits = x2d @ gate_kernel
        routing_weights = jax.nn.softmax(router_logits, axis=-1)
        routing_weights, selected_experts = jax.lax.top_k(routing_weights, TOP_K)
        routing_weights = routing_weights / jnp.sum(routing_weights, axis=-1, keepdims=True)
        flat_experts = selected_experts.reshape(-1)
        sort_idx = jnp.argsort(flat_experts)
        token_rows = sort_idx // TOP_K
        sorted_inputs = jnp.take(x2d, token_rows, axis=0)
        group_sizes = jnp.bincount(flat_experts, length=NUM_EXPERTS).astype(jnp.int32)
        w0 = jax.lax.ragged_dot(sorted_inputs, gate_proj, group_sizes, preferred_element_type=jnp.float32)
        w1 = jax.lax.ragged_dot(sorted_inputs, up_proj, group_sizes, preferred_element_type=jnp.float32)
        inter = jax.nn.silu(w0) * w1
        expert_out = jax.lax.ragged_dot(inter, down_proj, group_sizes, preferred_element_type=jnp.float32)
        unsorted = jnp.take(expert_out, jnp.argsort(sort_idx), axis=0)
        per_token = unsorted.reshape(T, TOP_K, D)
        output = jnp.einsum('BKE,BK->BE', per_token.astype(jnp.float32), routing_weights.astype(jnp.float32))
        return output.reshape(B, S, D)

    def _L1_xattn_ref(hidden_q, kv_c, Wq, w_kc_q, w_kc_kv, W_qr, W_kr, Wo):
        import jax, jax.numpy as jnp
        import numpy as np
        B, S, L = (2, 256, 256)
        DIM_Q, H, K, D_C, D_CQ, R = (512, 16, 128, 128, 384, 64)

        def _rope_tables(length, dim):
            inv = 1.0 / 10000.0 ** (jnp.arange(0, dim, 2, dtype=jnp.float32) / dim)
            f = jnp.arange(length, dtype=jnp.float32)[:, None] * inv[None, :]
            sin = jnp.repeat(jnp.sin(f), 2, axis=-1)
            cos = jnp.repeat(jnp.cos(f), 2, axis=-1)
            return (sin, cos)

        def _rotate_half(x):
            half = x.shape[-1] // 2
            return jnp.concatenate([-x[..., half:], x[..., :half]], axis=-1)

        def _apply_rope(x, sin, cos):
            return x * cos + _rotate_half(x) * sin
        Bv, Sv, _ = hidden_q.shape
        _, Lv, _ = kv_c.shape
        q_hk = (hidden_q @ Wq.T).reshape(Bv, Sv, H, K)
        q_big = jnp.einsum('bshk,hkq->bshq', q_hk, w_kc_q)
        sin_q, cos_q = _rope_tables(Sv, D_CQ)
        q_big = _apply_rope(q_big, sin_q[None, :, None, :], cos_q[None, :, None, :])
        sin_k, cos_k = _rope_tables(Lv, D_C)
        kv_r = _apply_rope(kv_c, sin_k[None], cos_k[None])
        q_r = jnp.einsum('bshq,hqr->bhsr', q_big, W_qr)
        k_r = jnp.einsum('bld,hdr->bhlr', kv_r, W_kr)
        scores = jnp.einsum('bhsr,bhlr->bhsl', q_r, k_r)
        attn = jax.nn.softmax(scores, axis=-1)
        ctx_c = jnp.einsum('bhsl,bld->bhsd', attn, kv_r)
        ctx_lat = jnp.einsum('bhsd,hkd->bhsk', ctx_c, w_kc_kv)
        ctx = ctx_lat.transpose(0, 2, 1, 3).reshape(Bv, Sv, H * K)
        return ctx @ Wo.T

    def _L1_ffn_ref(x, input_ids, gate_w, gate_b, W1, W3, W2, Ws1, Ws3, Ws2):
        import jax, jax.numpy as jnp
        import numpy as np
        E = 16
        K = 2
        D = 512
        I = 352
        CAP = 256
        VOCAB = 32320
        shape = x.shape
        xt = x.reshape(-1, D)
        T = xt.shape[0]
        logits = xt.astype(jnp.float32) @ gate_w.astype(jnp.float32).T
        scores = jnp.sqrt(jax.nn.softplus(logits))
        _, idx = jax.lax.top_k(scores + gate_b, K)
        w = jnp.take_along_axis(scores, idx, axis=1)
        w = w / jnp.sum(w, axis=1, keepdims=True)
        e = idx.reshape(-1)
        onehot = jax.nn.one_hot(e, E, dtype=jnp.int32)
        pos = jnp.sum(onehot * (jnp.cumsum(onehot, axis=0) - 1), axis=1)
        valid = pos < CAP
        posc = jnp.where(valid, pos, 0)
        x_pairs = jnp.repeat(xt, K, axis=0)
        x_pairs = jnp.where(valid[:, None], x_pairs, 0.0)
        buf = jnp.zeros((E, CAP, D), xt.dtype).at[e, posc].add(x_pairs)
        g = jnp.einsum('ecd,eid->eci', buf, W1).astype(jnp.float32)
        u = jnp.einsum('ecd,eid->eci', buf, W3).astype(jnp.float32)
        h = (jax.nn.silu(g) * u).astype(xt.dtype)
        out = jnp.einsum('eci,edi->ecd', h, W2)
        y_pairs = out[e, posc] * (w.reshape(-1) * valid)[:, None]
        y = y_pairs.reshape(T, K, D).sum(axis=1)
        gs = jax.nn.silu((xt @ Ws1.T).astype(jnp.float32))
        us = (xt @ Ws3.T).astype(jnp.float32)
        shared = (gs * us).astype(xt.dtype) @ Ws2.T
        return (y + shared).astype(x.dtype).reshape(shape)
    x = x + jnp.tanh(g_xattn[0]) * _L0_xattn_ref(_layernorm(x, axis=-1), ctx_512, L0_xattn_W_k, L0_xattn_b_k, L0_xattn_ln_gamma, L0_xattn_ln_beta)
    x = x + jnp.tanh(g_ffn[0]) * _L0_ffn_ref(_layernorm(x, axis=-1), L0_ffn_gate_kernel, L0_ffn_gate_proj, L0_ffn_up_proj, L0_ffn_down_proj)
    x = x + jnp.tanh(g_xattn[1]) * _L1_xattn_ref(_layernorm(x, axis=-1), ctx_512, L1_xattn_Wq, L1_xattn_w_kc_q, L1_xattn_w_kc_kv, L1_xattn_W_qr, L1_xattn_W_kr, L1_xattn_Wo)
    x = x + jnp.tanh(g_ffn[1]) * _L1_ffn_ref(_layernorm(x, axis=-1), L1_ffn_input_ids, L1_ffn_gate_w, L1_ffn_gate_b, L1_ffn_W1, L1_ffn_W3, L1_ffn_W2, L1_ffn_Ws1, L1_ffn_Ws3, L1_ffn_Ws2)
    return x

_drawn_inputs = setup_inputs


def setup_inputs(seed=0):
    import zlib

    import numpy as np

    out = dict(_drawn_inputs(seed))
    spreads = {'g_ffn': (-1.0, 0.2),
     'L0_xattn_b_k': (0.0, 2.0),
     'L0_xattn_ln_gamma': (1.0, 0.6),
     'L0_xattn_ln_beta': (0.0, 2.0)}
    factors = {'L0_xattn_W_k': 7.047}
    for name, (base, spread) in spreads.items():
        noise = np.random.default_rng([zlib.crc32(name.encode()), seed]).standard_normal(out[name].shape)
        drawn = base * np.exp(spread * noise) if base else spread * noise
        out[name] = jnp.asarray(drawn.astype(out[name].dtype))
    for name, factor in factors.items():
        out[name] = (out[name] * factor).astype(out[name].dtype)
    return out
```

```python
from contextlib import ExitStack

import concourse.bass as bass
from concourse import mybir

F32 = mybir.dt.float32
F32R = mybir.dt.float32r
I32 = mybir.dt.int32
U32 = mybir.dt.uint32
ALU = mybir.AluOpType
ACT = mybir.ActivationFunctionType
AX_X = mybir.AxisListType.X
ds = bass.ds

P = 128
B = 4
S = 512
T = B * S
D = 512
DC = D // P
NT = T // P
SJ = S // P
C = 128
LN_EPS = 1e-5
SIM_EPS = 1e-6
SIM_SCALE = 512 ** -0.5

DVE_A = 70

TILE = 256
SUB = TILE // P


passed = []


def until(eng, sem, value):
    eng.wait_ge(sem, value)
    if not isinstance(value, int):
        eng.sem_inc(passed[0], 1)


class Steps:

    def __init__(self, eng, sem, base=0):
        self.eng, self.sem, self.base, self.n = eng, sem, base, 0

    def __call__(self, ins):
        self.n += 1
        return ins.then_inc(self.sem, 1)

    def settle(self):
        until(self.eng, self.sem, self.base + self.n)


def over(ap, axis, n):
    ap = ap.unsqueeze(axis)
    shape = list(ap.shape)
    shape[axis] = n
    return ap.to_broadcast(shape)


def semaphores(nc, ctx, prefix):
    made = []

    def sem(name):
        made.append(nc.alloc_semaphore(name=prefix + name))
        return made[-1]

    def free():
        nc.clear_and_free_semaphores(made)
        nc.all_engine_barrier()

    ctx.callback(free)
    return sem


def constants(nc, mem, sem, g_in):
    ident = mem("ident", [P, P])
    ident_r = mem("ident_r", [P, P], F32R)
    ones = mem("ones", [P, P])
    before = mem("before", [P, P])
    mhalf = mem("mhalf", [P, NT])
    gates = mem("gates", [P, 4])
    tanhg = mem("tanhg", [P, 4])
    gates_in, filled, masked = sem("gates_in"), sem("consts_filled"), sem("consts_masked")
    ready = sem("consts_ready")
    passed[:] = [sem("waits_passed")]
    with nc.Block() as block:
        @block.sync
        def _(sp):
            sp.dma_start(gates[:], g_in.partition_broadcast(P)).then_inc(gates_in, 16)

        @block.gpsimd
        def _(pool):
            pool.memset(ident[:], 0.0).then_inc(filled, 1)
            pool.memset(before[:], 1.0).then_inc(filled, 1)
            pool.wait_ge(filled, 2)
            pool.affine_select(out=ident[:], in_=ident[:], compare_op=ALU.not_equal, fill=1.0, base=0,
                               pattern=[[-1, P]], channel_multiplier=1).then_inc(masked, 1)
            pool.affine_select(out=before[:], in_=before[:], compare_op=ALU.is_gt, fill=0.0, base=0,
                               pattern=[[1, P]], channel_multiplier=-1).then_inc(masked, 1)

        @block.vector
        def _(dve):
            dve.memset(ones[:], 1.0).then_inc(ready, 1)
            dve.memset(mhalf[:], -0.5).then_inc(ready, 1)
            dve.wait_ge(masked, 2)
            dve.tensor_copy(ident_r[:], ident[:]).then_inc(ready, 1)

        @block.scalar
        def _(act):
            act.wait_ge(gates_in, 16)
            act.activation(tanhg[:], gates[:], ACT.Tanh).then_inc(ready, 1)

        @block.tensor
        def _(pe):
            pe.wait_ge(ready, 4)
    return dict(ident=ident, ident_r=ident_r, ones=ones, before=before, mhalf=mhalf, tanhg=tanhg)


def first_layer_attention(nc, cst, X, x_in, ctxT_in, wkT_in, bk_in, gamma_in, beta_in, gk_in, xn_dram, tab_dram,
                          running, K=8, E=32):
    with ExitStack() as ctx:
        def mem(name, shape, dt=F32):
            return ctx.enter_context(nc.sbuf_tensor("a_" + name, shape, dt))

        def bank(name):
            return ctx.enter_context(nc.psum_tensor("a_" + name, [P, 512], F32))

        sem = semaphores(nc, ctx, "a_")

        M = SJ * K
        wkT, brow, bcol = mem("wkT", [P, C]), mem("brow", [P, C]), mem("bcol", [P, 1])
        gamma, beta = mem("gamma", [P, S]), mem("beta", [P, S])
        gk = mem("gk", [P, DC, E])
        ctxT = mem("ctxT", [P, S])
        N = mem("N", [P, SJ, D])
        NT_ = mem("NT", [P, DC, S])
        kv, kvT, outT = mem("kv", [P, SJ, C]), mem("kvT", [P, S]), mem("outT", [P, S])
        sim = mem("sim", [P, SJ, S])
        stats, mv = mem("stats", [P, SJ, 6]), mem("mv", [P, SJ, 2])
        ve, rstd, nbias = mem("ve", [P, SJ]), mem("rstd", [P, SJ]), mem("nbias", [P, SJ])
        top = mem("top", [P, SJ])
        esum, rsum = mem("esum", [P, SJ]), mem("rsum", [P, SJ])
        logit8, idx8 = mem("logit8", [P, SJ, 8]), mem("idx8", [P, SJ, 8], U32)
        lg = mem("lg", [P, SJ, E])
        w8, wsum = mem("w8", [P, SJ, 8]), mem("wsum", [P, SJ])
        idxf = mem("idxf", [P, M])
        iota_e, e16 = mem("iota_e", [P, E], I32), mem("e16", [P, SJ, E], I32)
        iota_ef = mem("iota_ef", [P, E])
        hot = mem("hot", [P, M, E])
        mask, pref = mem("mask", [P, SJ, E]), mem("pref", [P, SJ, E])
        pos_i, low = mem("pos_i", [P, SJ * E], I32), mem("low", [P, SJ * E], I32)
        addr = mem("addr", [P, SJ, E])
        slot_f, slot = mem("slot_f", [P, M]), mem("slot", [P, M], I32)
        ids = mem("ids", [P, SJ, K], I32)
        entry = mem("entry", [P, SJ, K, 2], I32)
        init, zeros = mem("init", [P, P * 4, 2], I32), mem("zeros", [P, D])

        tr = [bank("tr0"), bank("tr1")]
        kvp, kvTp = bank("kvp"), bank("kvTp")
        simp = [bank(f"simp{j}") for j in range(SJ)]
        outp, rt, posp = tr[0], kvp, kvTp

        consts_in, x_in_s, ctx_in = sem("consts_in"), sem("x_in"), sem("ctx_in")
        dve_s, act_s, pool_s = sem("dve"), sem("act"), sem("pool")
        var_r, rstd_r, nb_r = sem("var_ready"), sem("rstd_ready"), sem("nbias_ready")
        n_r, tr_r, trs_r = sem("rows_normal"), sem("transposed"), sem("transposes_kept")
        kvp_r, kv_r, kvTp_r, kvT_r = sem("kv_made"), sem("kv_kept"), sem("kvT_made"), sem("kvT_kept")
        outp_r, outT_r, simp_r = sem("out_made"), sem("out_kept"), sem("sim_made")
        sn_r, sg_r, top_r, e_r = sem("sim_normal"), sem("sim_scaled"), sem("top_ready"), sem("exp_ready")
        x_r = sem("x_updated")
        lg_r, d8_r, w8_r = sem("logits_made"), sem("logit8_shifted"), sem("exp8_ready")
        mask_r, pos_r, route_r = sem("mask_ready"), sem("pos_made"), sem("route_ready")
        rows_out, tab_init, tab_out, iota_r = sem("rows_out"), sem("tab_init"), cst["a_table_out"], sem("iota")
        init_r = sem("init_ready")
        zeros_r = sem("zeros")
        dve_tr, dve_pre, lg_done = sem("even_transposes_kept"), sem("dve_setup"), route_r

        xv = x_in.rearrange("(b j p) d -> b p j d", p=P, j=SJ)
        xnv = xn_dram[0:T, :].rearrange("(b j p) d -> b p j d", p=P, j=SJ)
        ident = cst["ident"]

        with nc.Block() as block:
            @block.sync
            def _(sp):
                sp.dma_start(X[:, 0:SJ, :], xv[0]).then_inc(x_in_s, 16)
                sp.dma_start(wkT[:], wkT_in).then_inc(consts_in, 16)
                sp.dma_start(brow[:], bk_in.partition_broadcast(P)).then_inc(consts_in, 16)
                sp.dma_start(bcol[:], bk_in.rearrange("(d a) -> d a", a=1)).then_inc(consts_in, 16)
                sp.dma_start(gamma[:], gamma_in.partition_broadcast(P)).then_inc(consts_in, 16)
                sp.dma_start(beta[:], beta_in.partition_broadcast(P)).then_inc(consts_in, 16)
                sp.dma_start(gk[:], gk_in).then_inc(consts_in, 16)
                for b in range(1, B):
                    sp.dma_start(X[:, SJ * b:SJ * (b + 1), :], xv[b]).then_inc(x_in_s, 16)
                sp.wait_ge(init_r, 2)
                sp.dma_start(tab_dram[0:E * T, :].rearrange("(p c) w -> p (c w)", p=P),
                             init[:].rearrange("p c w -> p (c w)")).then_inc(tab_init, 16)
                sp.wait_ge(zeros_r, 1)
                sp.dma_start(xn_dram[T:T + P, :], zeros[:]).then_inc(tab_init, 16)
                with sp.Fori(0, B) as b:
                    until(sp, kvTp_r, b)
                    until(sp, kvp_r, b)
                    sp.dma_start(ctxT[:], ctxT_in[ds(b, 1)].rearrange("a d l -> (a d) l")).then_inc(ctx_in, 16)
                    until(sp, n_r, 8 * b + 8)
                    sp.dma_start(xnv[ds(b, 1)].rearrange("a p j d -> (a p) j d"), N[:]).then_inc(rows_out, 16)
                sp.wait_ge(rows_out, 16 * B)
                sp.wait_ge(tab_init, 32)

            @block.scalar
            def _(act):
                act.wait_ge(consts_in, 96)

                with act.Fori(0, B) as b:
                    def normalise(half):
                        until(act, nb_r, 3 * b + (1 if half == 0 else 3))
                        if half == 0:
                            until(act, rows_out, 16 * b)
                            until(act, tr_r, 8 * b)
                        else:
                            until(act, tr_r, 8 * b + 4)
                        for j in range(SJ):
                            act.activation(N[:, j, :], X[:, ds(SJ * b + j, 1), :].rearrange("p a d -> p (a d)"),
                                           ACT.Identity, bias=nbias[:, j:j + 1],
                                           scale=rstd[:, j:j + 1]).then_inc(n_r, 1)

                    def keep_transposes(half):
                        if half == 1:
                            until(act, outp_r, b + 1)
                        else:
                            until(act, lg_r, b)
                        for c in (1, 3):
                            until(act, tr_r, 8 * b + 4 * half + c + 1)
                            act.activation(NT_[:, c, :], tr[1][:, :], ACT.Copy).then_inc(trs_r, 1)

                    normalise(0)
                    until(act, kvTp_r, b + 1)
                    act.activation(kvT[:], kvTp[:], ACT.Identity, bias=bcol[:, 0:1]).then_inc(kvT_r, 1)
                    keep_transposes(0)
                    until(act, outp_r, b + 1)
                    act.activation(outT[:], outp[:], ACT.Copy).then_inc(outT_r, 1)
                    until(act, nb_r, 3 * b + 2)
                    until(act, x_r, 4 * b)
                    for j in range(SJ):
                        act.activation(sim[:, j, :], simp[j][:], ACT.Identity, bias=nbias[:, j:j + 1],
                                       scale=rstd[:, j:j + 1]).then_inc(sn_r, 1)
                    for j in range(SJ):
                        until(act, top_r, 4 * b + j + 1)
                        act.activation(sim[:, j, :], sim[:, j, :], ACT.Exp, bias=top[:, j:j + 1],
                                       accum_out=esum[:, j:j + 1]).then_inc(e_r, 1)
                    normalise(1)
                    keep_transposes(1)
                    until(act, d8_r, b + 1)
                    act.activation(w8[:], w8[:], ACT.Exp).then_inc(w8_r, 1)

            @block.gpsimd
            def _(pool):
                pool.iota(iota_e[:], [[1, E]], base=0, channel_multiplier=0).then_inc(iota_r, 1)
                pool.iota(e16[:], [[0, SJ], [T // P, E]], base=0, channel_multiplier=0).then_inc(iota_r, 1)
                pool.iota(ids[:], [[P, SJ], [0, K]], base=0, channel_multiplier=1).then_inc(iota_r, 1)
                pool.iota(init[:, :, 0], [[0, P * 4]], base=T, channel_multiplier=1).then_inc(init_r, 1)
                pool.memset(init[:, :, 1], 0).then_inc(init_r, 1)
                with pool.Fori(0, B) as b:
                    def power(n):
                        until(pool, var_r, 3 * b + n)
                        pool.tensor_tensor(rstd[:], ve[:], cst["mhalf"][:, 0:SJ], ALU.pow).then_inc(rstd_r, 1)

                    power(1)
                    power(2)
                    for j in range(SJ):
                        until(pool, sn_r, 4 * b + j + 1)
                        pool.tensor_tensor(sim[:, j, :], sim[:, j, :], gamma[:], ALU.mult).then_inc(sg_r, 1)
                    power(3)
                    pool.wait_ge(tab_init, 32)
                    until(pool, route_r, b + 1)
                    pool.wait_ge(tab_init, 32)
                    for m in range(M):
                        j, k = divmod(m, K)
                        pool.indirect_dma_start(
                            out=tab_dram, out_offset=bass.IndirectOffsetOnAxis(ap=slot[:, m:m + 1], axis=0),
                            in_=entry[:, j, k, :], in_offset=None).then_inc(tab_out, 16)
                pool.wait_ge(tab_out, 16 * M * B)

            @block.tensor
            def _(pe):
                pe.wait_ge(consts_in, 96)
                with pe.Fori(0, B) as b:
                    def transposes(half):
                        until(pe, n_r, 8 * b + 4 * half + 4)
                        for c in range(DC):
                            if c >= 2:
                                until(pe, trs_r if c % 2 else dve_tr, 4 * b + 2 * half + 1)
                            elif half == 1 or c == 1:
                                pass
                            for j in range(SJ):
                                mm = pe.transpose(tr[c % 2][:, j * P:(j + 1) * P], N[:, j, c * P:(c + 1) * P], ident[:])
                            mm.then_inc(tr_r, 1)

                    until(pe, ctx_in, 16 * b + 16)
                    until(pe, lg_done, b)
                    until(pe, route_r, b)
                    for j in range(SJ):
                        mm = pe.matmul(kvp[:, j * C:(j + 1) * C], ctxT[:, j * P:(j + 1) * P], wkT[:],
                                       start=True, stop=True)
                    mm.then_inc(kvp_r, 1)
                    pe.matmul(kvTp[:], wkT[:], ctxT[:], start=True, stop=True).then_inc(kvTp_r, 1)
                    until(pe, dve_tr, 4 * b)
                    until(pe, trs_r, 4 * b)
                    transposes(0)
                    until(pe, kv_r, b + 1)
                    until(pe, trs_r, 4 * b + 2)
                    until(pe, dve_tr, 4 * b + 2)
                    for c in range(DC):
                        mm = pe.matmul(outp[:], kv[:, c, :], NT_[:, c, :], start=(c == 0), stop=(c == DC - 1))
                    mm.then_inc(outp_r, 1)
                    until(pe, outT_r, b + 1)
                    until(pe, kvT_r, b + 1)
                    until(pe, sn_r, 4 * b)
                    for j in range(SJ):
                        pe.matmul(simp[j][:], outT[:, j * P:(j + 1) * P], kvT[:], start=True,
                                  stop=True).then_inc(simp_r, 1)
                    transposes(1)
                    until(pe, trs_r, 4 * b + 4)
                    until(pe, dve_tr, 4 * b + 4)
                    for j in range(SJ):
                        for c in range(DC):
                            mm = pe.matmul(rt[:, j * E:(j + 1) * E], NT_[:, c, j * P:(j + 1) * P], gk[:, c, :],
                                           start=(c == 0), stop=(c == DC - 1))
                    mm.then_inc(lg_r, 1)
                    until(pe, mask_r, b + 1)
                    pe.matmul(posp[:, 0:SJ * E], cst["before"][:], mask[:].rearrange("p j e -> p (j e)"),
                              start=True, stop=False)
                    pe.matmul(posp[:, 0:SJ * E], cst["ones"][:], pref[:].rearrange("p j e -> p (j e)"),
                              start=False, stop=True).then_inc(pos_r, 1)

            @block.vector
            def _(dve):
                pre = Steps(dve, dve_pre)
                dve.memset(zeros[:], 0.0).then_inc(zeros_r, 1)
                pre(dve.memset(running[:], 0.0))
                dve.wait_ge(iota_r, 3)
                pre(dve.tensor_copy(iota_ef[:], iota_e[:]))
                pre.settle()
                dve.wait_ge(consts_in, 96)
                with dve.Fori(0, B) as b:
                    step = Steps(dve, dve_s, b * DVE_A)

                    def moments(half, src):
                        for j in range(SJ):
                            if half == 1:
                                until(dve, simp_r, 4 * b + j + 1)
                            step(dve.bn_stats(stats[:, j, :], src(j)))
                        step.settle()
                        for j in range(SJ):
                            step(dve.bn_aggr(mv[:, j, :], stats[:, j, :]))
                        step.settle()
                        if half == 1:
                            step(dve.tensor_scalar(ve[:], mv[:, :, 1], SIM_SCALE ** 2, SIM_EPS, ALU.mult, ALU.add))
                        else:
                            step(dve.tensor_scalar(ve[:], mv[:, :, 1], LN_EPS, None, ALU.add))
                        step.settle()
                        dve.engine_nop().then_inc(var_r, 1)
                        until(dve, rstd_r, 3 * b + half + 1)
                        if half == 1:
                            step(dve.tensor_scalar(rstd[:], rstd[:], SIM_SCALE, None, ALU.mult))
                            step.settle()
                        dve.scalar_tensor_tensor(nbias[:], mv[:, :, 0], -1.0, rstd[:], ALU.mult,
                                                 ALU.mult).then_inc(nb_r, 1)

                    def keep_transposes(half):
                        if half == 1:
                            until(dve, outp_r, b + 1)
                        else:
                            until(dve, lg_r, b)
                        for c in (0, 2):
                            until(dve, tr_r, 8 * b + 4 * half + c + 1)
                            dve.tensor_copy(NT_[:, c, :], tr[0][:]).then_inc(dve_tr, 1)

                    def rows(j):
                        return X[:, ds(SJ * b + j, 1), :].rearrange("p a d -> p (a d)")

                    until(dve, x_in_s, 16 * b + 16)
                    moments(0, rows)
                    until(dve, kvp_r, b + 1)
                    dve.tensor_tensor(kv[:], kvp[:].rearrange("p (j c) -> p j c", c=C), over(brow[:], 1, SJ),
                                      ALU.add).then_inc(kv_r, 1)
                    keep_transposes(0)
                    moments(1, lambda j: simp[j][:])
                    for j in range(SJ):
                        until(dve, sg_r, 4 * b + j + 1)
                        step(dve.tensor_tensor_reduce(sim[:, j, :], sim[:, j, :], beta[:], 1.0, -3.0e38, ALU.add,
                                                      ALU.max, top[:, j:j + 1]))
                        step.settle()
                        dve.tensor_scalar(top[:, j:j + 1], top[:, j:j + 1], -1.0, None, ALU.mult).then_inc(top_r, 1)
                    for j in range(SJ):
                        until(dve, e_r, 4 * b + j + 1)
                        step(dve.reciprocal(rsum[:, j:j + 1], esum[:, j:j + 1]))
                        step.settle()
                        step(dve.tensor_scalar(rsum[:, j:j + 1], rsum[:, j:j + 1], cst["tanhg"][:, 0:1], None,
                                               ALU.mult))
                        step.settle()
                        dve.scalar_tensor_tensor(rows(j), sim[:, j, :], rsum[:, j:j + 1], rows(j), ALU.mult,
                                                 ALU.add).then_inc(x_r, 1)
                    until(dve, x_r, 4 * b + 4)
                    moments(2, rows)
                    keep_transposes(1)

                    until(dve, lg_r, b + 1)
                    step(dve.tensor_copy(lg[:], rt[:, 0:SJ * E].rearrange("p (j e) -> p j e", e=E)))
                    step.settle()
                    for j in range(SJ):
                        step(dve.max(logit8[:, j, :], lg[:, j, :]))
                    step.settle()
                    for j in range(SJ):
                        step(dve.max_index(idx8[:, j, :], logit8[:, j, :], lg[:, j, :]))
                    dve.tensor_tensor(w8[:], logit8[:], logit8[:, :, 0:1].to_broadcast([P, SJ, 8]),
                                      ALU.subtract).then_inc(d8_r, 1)
                    step.settle()
                    step(dve.tensor_copy(idxf[:], idx8[:].rearrange("p j k -> p (j k)")))
                    step.settle()
                    step(dve.tensor_tensor(hot[:], over(idxf[:], 2, E), over(iota_ef[:], 1, M), ALU.is_equal))
                    step.settle()
                    step(dve.tensor_reduce(mask[:], hot[:].rearrange("p (j k) e -> p j e k", k=K), AX_X, ALU.add))
                    step(dve.tensor_copy(pref[:, 0, :], running[:]))
                    step.settle()
                    for j in range(SJ):
                        nxt = pref[:, j + 1, :] if j + 1 < SJ else running[:]
                        step(dve.tensor_tensor(nxt, pref[:, j, :], mask[:, j, :], ALU.add))
                        step.settle()
                    dve.engine_nop().then_inc(mask_r, 1)
                    until(dve, w8_r, b + 1)
                    step(dve.tensor_reduce(wsum[:], w8[:], AX_X, ALU.add))
                    step.settle()
                    step(dve.reciprocal(wsum[:], wsum[:]))
                    step.settle()
                    until(dve, tab_out, 16 * M * b)
                    step(dve.tensor_tensor(entry[:, :, :, 1].bitcast(F32), w8[:], over(wsum[:], 2, 8), ALU.mult))
                    step(dve.tensor_copy(entry[:, :, :, 0], ids[:]))
                    step.settle()
                    step(dve.tensor_scalar(ids[:], ids[:], float(S), None, ALU.add))
                    until(dve, pos_r, b + 1)
                    step(dve.tensor_copy(pos_i[:], posp[:, 0:SJ * E]))
                    step.settle()
                    step(dve.tensor_scalar(low[:], pos_i[:], P - 1, (E * T // P).bit_length() - 1, ALU.bitwise_and,
                                           ALU.logical_shift_left))
                    step(dve.tensor_scalar(pos_i[:], pos_i[:], 7, None, ALU.logical_shift_right))
                    step.settle()
                    step(dve.tensor_tensor(low[:], low[:], pos_i[:], ALU.add))
                    step.settle()
                    step(dve.tensor_tensor(addr[:].rearrange("p j e -> p (j e)"), low[:],
                                           e16[:].rearrange("p j e -> p (j e)"), ALU.add))
                    step.settle()
                    hot4 = hot[:].rearrange("p (j k) e -> p j k e", k=K)
                    step(dve.tensor_tensor(hot4, hot4, over(addr[:], 2, K), ALU.mult))
                    step.settle()
                    step(dve.tensor_reduce(slot_f[:], hot[:], AX_X, ALU.add))
                    step.settle()
                    step(dve.tensor_copy(slot[:], slot_f[:]))
                    step.settle()
                    dve.engine_nop().then_inc(route_r, 1)
                    assert step.n == DVE_A, step.n


def plan_tiles(nc, cst, running, bounds, cols, plan_dram, acc_dram, tab_dram, table, E=32):
    with ExitStack() as ctx:
        def mem(name, shape, dt=F32):
            return ctx.enter_context(nc.sbuf_tensor("p_" + name, shape, dt))

        sem = semaphores(nc, ctx, "p_")

        count, tiles, ntile = mem("count", [P, E], I32), mem("tiles", [P, E], I32), mem("ntile", [P, E])
        upto = mem("upto", [P, E + 1])
        upto_i = mem("upto_i", [P, E + 1], I32)
        tile_i, tile_f = mem("tile_i", [P, 1], I32), mem("tile_f", [P, 1])
        past, pastn = mem("past", [P, E]), mem("pastn", [P, E])
        expert, first, col = mem("expert", [P, 1]), mem("first", [P, 1]), mem("col", [P, 1])
        col_i = mem("col_i", [P, 1], I32)
        zeros = mem("zeros", [P, D])
        total = ctx.enter_context(nc.psum_tensor("p_total", [P, E], F32))
        dve_s, total_r, iota_r, plan_r, moved, cleared, zeros_r, tab_in = (sem(n) for n in (
            "dve", "total", "iota", "plan_ready", "moved", "cleared", "zeros", "tab_in"))
        with nc.Block() as block:
            @block.gpsimd
            def _(pool):
                pool.iota(tile_i[:], [[0, 1]], base=0, channel_multiplier=1).then_inc(iota_r, 1)

            @block.tensor
            def _(pe):
                pe.matmul(total[:], cst["ones"][:], running[:], start=True, stop=True).then_inc(total_r, 1)

            @block.vector
            def _(dve):
                step = Steps(dve, dve_s)
                dve.memset(zeros[:], 0.0).then_inc(zeros_r, 1)
                dve.wait_ge(total_r, 1)
                step(dve.tensor_copy(count[:], total[:]))
                step.settle()
                step(dve.tensor_scalar(count[:], count[:], TILE - 1, None, ALU.add))
                step.settle()
                step(dve.tensor_scalar(tiles[:], count[:], TILE.bit_length() - 1, None, ALU.logical_shift_right))
                step.settle()
                step(dve.tensor_scalar(ntile[:], tiles[:], 1.0, None, ALU.max))
                step(dve.memset(upto[:, 0:1], 0.0))
                step.settle()
                step(dve.tensor_tensor_scan(upto[:, 1:E + 1], cst["ones"][:, 0:E], ntile[:], 0.0, ALU.mult, ALU.add))
                step.settle()
                step(dve.tensor_copy(upto_i[:], upto[:]))
                dve.wait_ge(iota_r, 1)
                step(dve.tensor_copy(tile_f[:], tile_i[:]))
                step.settle()
                step(dve.tensor_scalar(past[:], upto[:, 1:E + 1], tile_f[:, 0:1], None, ALU.is_le))
                step(dve.tensor_copy(bounds[:], upto_i[0:1, :]))
                step.settle()
                step(dve.tensor_reduce(expert[:], past[:], AX_X, ALU.add))
                step(dve.tensor_tensor(pastn[:], past[:], ntile[:], ALU.mult))
                step.settle()
                step(dve.tensor_reduce(first[:], pastn[:], AX_X, ALU.add))
                step.settle()
                step(dve.tensor_tensor(first[:], tile_f[:], first[:], ALU.subtract))
                step(dve.tensor_scalar(expert[:], expert[:], float(T // P), None, ALU.mult))
                step.settle()
                step(dve.scalar_tensor_tensor(col[:], first[:], float(SUB), expert[:], ALU.mult, ALU.add))
                step.settle()
                step(dve.tensor_scalar(col_i[:], col[:], float(E * T // P - SUB), None, ALU.min))
                step.settle()
                dve.engine_nop().then_inc(plan_r, 1)

            @block.sync
            def _(sp):
                sp.wait_ge(zeros_r, 1)
                sp.dma_start(table[:], tab_dram.rearrange("(p c) w -> p c w", p=P)).then_inc(tab_in, 16)
                clear_rows(sp, zeros, acc_dram, cleared)
                sp.wait_ge(plan_r, 1)
                sp.dma_start(plan_dram.rearrange("a g -> g a"), col_i[:]).then_inc(moved, 16)
                sp.wait_ge(moved, 16)
                sp.dma_start(cols[:], plan_dram).then_inc(moved, 16)
                sp.wait_ge(moved, 32)
                sp.wait_ge(cleared, 16 * (NT + 1))
                sp.wait_ge(tab_in, 16)


def clear_rows(sp, zeros, acc_dram, cleared):
    for n in range(NT + 1):
        sp.dma_start(acc_dram[n * P:(n + 1) * P, :], zeros[:]).then_inc(cleared, 16)


def experts(nc, cst, name, xn_dram, acc_dram, table, gu_in, dn_in, chunks, pieces, bounds, cols, n_tiles, pairs, tail):
    with ExitStack() as ctx:
        def mem(nm, shape, dt=F32):
            return ctx.enter_context(nc.sbuf_tensor(name + nm, shape, dt))

        def bank(nm, dt=F32):
            return ctx.enter_context(nc.psum_tensor(name + nm, [P, 512], dt))

        sem = semaphores(nc, ctx, name)

        W, NQ, NC = chunks[-1][0] + chunks[-1][1], len(pieces), len(chunks)
        raw_gu, raw_dn = mem("raw_gu", [P, DC, W]), mem("raw_dn", [P, NQ, D])
        gu_hi = [mem(f"gu_hi{i}", [P, DC, W], F32R) for i in (0, 1)]
        gu_lo = [mem(f"gu_lo{i}", [P, DC, W], F32R) for i in (0, 1)]
        dn_hi = [mem(f"dn_hi{i}", [P, NQ, D], F32R) for i in (0, 1)]
        dn_lo = [mem(f"dn_lo{i}", [P, NQ, D], F32R) for i in (0, 1)]
        x = mem("x", [P, SUB, D], F32R)
        x_hi, x_lo = mem("x_hi", [P, DC, TILE], F32R), mem("x_lo", [P, DC, TILE], F32R)
        sg, h = mem("sg", [P, NQ, TILE]), mem("h", [P, NQ, TILE])
        h_hi, h_lo = mem("h_hi", [P, NQ, TILE], F32R), mem("h_lo", [P, NQ, TILE], F32R)
        y = mem("y", [P, SUB, D])
        gidx, sidx, sw = mem("gidx", [P, SUB], I32), mem("sidx", [P, SUB], I32), mem("sw", [P, SUB])
        gup = [bank(f"gu{i}") for i in range(4)]
        trp = [bank(f"tr{i}", F32R) for i in range(2)]
        dnp = [bank(f"dn{i}") for i in range(SUB)]
        raw_in, hi_r, lo_r = sem("raw_in"), sem("weights_hi"), sem("weights_lo")
        gidx_r, x_in, tr_r = sem("gidx"), cst[name + "rows_in"], sem("transposed")
        xhi_r, xlo_r = sem("x_hi"), sem("x_lo")
        chunk_r, sg_r, h_r, hs_r = sem("chunk_made"), sem("silu_made"), sem("h_made"), sem("h_split")
        dn_r, y_r = sem("down_made"), sem("y_ready")
        sidx_r, added = sem("sidx"), cst[name + "rows_added"]
        dve_s = sem("dve")
        dynamic = not isinstance(bounds, list)

        def span(eng, e):
            if not dynamic:
                return (bounds[e], bounds[e + 1]) if isinstance(e, int) else (e, e + 1)
            return (eng.value_load(bounds[0:1, ds(e, 1)], min_val=0, max_val=n_tiles - 1),
                    eng.value_load(bounds[0:1, ds(e + 1, 1)], min_val=1, max_val=n_tiles))

        def each_expert(eng, body):
            with eng.Fori(0, pairs) as i:
                body(2 * i, 0, False)
                body(2 * i + 1, 1, False)
            for e in tail:
                body(e, e % 2, e == tail[-1])

        def each_tile(eng, e, body):
            first, end = span(eng, e)
            if isinstance(first, int) and end == first + 1:
                body(first)
            elif not dynamic and not isinstance(e, int):
                body(first)
            else:
                with eng.Fori(first, end) as g:
                    body(g)

        with nc.Block() as block:
            @block.sync
            def _(sp):
                def load(e):
                    sp.dma_start(raw_gu[:], gu_in[ds(e, 1)].rearrange("a p c w -> (a p) c w")).then_inc(raw_in, 16)
                    sp.dma_start(raw_dn[:], dn_in[ds(e, 1)].rearrange("a p q d -> (a p) q d")).then_inc(raw_in, 16)

                def expert(e, parity, last):
                    if not last:
                        until(sp, lo_r, e + 1)
                        load(e + 1)

                load(0)
                each_expert(sp, expert)

            @block.gpsimd
            def _(pool):
                def column(g):
                    if dynamic:
                        return pool.value_load(cols[0:1, ds(g, 1)], min_val=0, max_val=table.shape[1] - SUB)
                    return g * SUB

                def gather(g, c):
                    pool.tensor_copy(gidx[:], table[:, ds(c, SUB), 0]).then_inc(gidx_r, 1)
                    until(pool, gidx_r, g + 1)
                    for s in range(SUB):
                        pool.indirect_dma_start(
                            out=x[:, s, :].bitcast(F32), out_offset=None, in_=xn_dram,
                            in_offset=bass.IndirectOffsetOnAxis(ap=gidx[:, s:s + 1], axis=0)).then_inc(x_in, 16)

                gather(0, column(0))
                pool.wait_ge(tr_r, 1)
                gather(1, column(1))

                end = n_tiles if not dynamic else span(pool, tail[-1])[1]
                with pool.Fori(0, end) as g:
                    c = column(g)
                    until(pool, added, 16 * SUB * g)
                    until(pool, y_r, SUB * g)
                    pool.tensor_copy(sidx[:], table[:, ds(c, SUB), 0]).then_inc(sidx_r, 1)
                    pool.tensor_copy(sw[:], table[:, ds(c, SUB), 1].bitcast(F32)).then_inc(sidx_r, 1)
                    until(pool, tr_r, g + 2)
                    gather(g + 2, column(g + 2))
                    until(pool, sidx_r, 2 * g + 2)
                    for s in range(SUB):
                        until(pool, y_r, SUB * g + s + 1)
                        until(pool, added, 16 * (SUB * g + s))
                        pool.indirect_dma_start(
                            out=acc_dram, out_offset=bass.IndirectOffsetOnAxis(ap=sidx[:, s:s + 1], axis=0),
                            in_=y[:, s, :], in_offset=None, compute_op=ALU.add).then_inc(added, 16)
                until(pool, x_in, 16 * SUB * (end + 2))
                until(pool, added, 16 * SUB * end)

            @block.scalar
            def _(act):
                def split_weights(e, parity, done=None):
                    until(act, raw_in, 32 * e + 32)
                    if done is not None:
                        until(act, dn_r, SUB * done)
                    act.activation(gu_hi[parity][:], raw_gu[:], ACT.Copy).then_inc(hi_r, 1)
                    act.activation(dn_hi[parity][:], raw_dn[:], ACT.Copy).then_inc(hi_r, 1)

                def keep_x(g):
                    until(act, tr_r, g + 1)
                    until(act, chunk_r, NC * g)
                    for i in (0, 1):
                        act.activation(x_hi[:, 2 * i:2 * i + 2, :], trp[i][:].bitcast(F32), ACT.Copy).then_inc(xhi_r, 1)

                def tile(g):
                    for q, (rows, gc, gp, uc, up) in enumerate(pieces):
                        until(act, chunk_r, NC * g + gc + 1)
                        act.activation(sg[up:up + rows, q, :], gup[chunks[gc][2]][gp:gp + rows, 0:TILE],
                                       ACT.Silu).then_inc(sg_r, 1)
                    keep_x(g + 1)
                    until(act, sidx_r, 2 * g + 2)
                    until(act, added, 16 * SUB * g)
                    for s in range(SUB):
                        until(act, dn_r, SUB * g + s + 1)
                        act.activation(y[:, s, :], dnp[s][:], ACT.Copy, scale=sw[:, s:s + 1]).then_inc(y_r, 1)

                def expert(e, parity, last):
                    if not last:
                        split_weights(e + 1, 1 - parity, span(act, e)[0])
                    each_tile(act, e, tile)

                split_weights(0, 0)
                keep_x(0)
                each_expert(act, expert)

            @block.vector
            def _(dve):
                def split_weights(e, parity):
                    until(dve, hi_r, 2 * e + 1)
                    dve.tensor_tensor(gu_lo[parity][:], raw_gu[:], gu_hi[parity][:].bitcast(F32), ALU.subtract)
                    until(dve, hi_r, 2 * e + 2)
                    dve.tensor_tensor(dn_lo[parity][:], raw_dn[:], dn_hi[parity][:].bitcast(F32),
                                      ALU.subtract).then_inc(lo_r, 1)

                def keep_x(g):
                    for i in (0, 1):
                        until(dve, xhi_r, 2 * g + i + 1)
                        dve.tensor_tensor(x_lo[:, 2 * i:2 * i + 2, :], trp[i][:].bitcast(F32),
                                          x_hi[:, 2 * i:2 * i + 2, :].bitcast(F32), ALU.subtract).then_inc(xlo_r, 1)

                def tile(g):
                    until(dve, dn_r, SUB * g)
                    for q, (rows, gc, gp, uc, up) in enumerate(pieces):
                        until(dve, sg_r, NQ * g + q + 1)
                        until(dve, chunk_r, NC * g + uc + 1)
                        dve.tensor_tensor(h[0:rows, q, :], gup[chunks[uc][2]][up:up + rows, 0:TILE],
                                          sg[up:up + rows, q, :], ALU.mult).then_inc(h_r, 1)
                        until(dve, h_r, NQ * g + q + 1)
                        dve.tensor_copy(h_hi[0:rows, q, :], h[0:rows, q, :]).then_inc(dve_s, 1)
                        until(dve, dve_s, NQ * g + q + 1)
                        dve.tensor_tensor(h_lo[0:rows, q, :], h[0:rows, q, :], h_hi[0:rows, q, :].bitcast(F32),
                                          ALU.subtract).then_inc(hs_r, 1)
                    keep_x(g + 1)

                def expert(e, parity, last):
                    if not last:
                        split_weights(e + 1, 1 - parity)
                    each_tile(dve, e, tile)

                split_weights(0, 0)
                keep_x(0)
                each_expert(dve, expert)

            @block.tensor
            def _(pe):
                def transposes(g):
                    until(pe, x_in, 16 * SUB * (g + 1))
                    until(pe, xlo_r, 2 * g)
                    for c in range(DC):
                        for s in range(SUB):
                            at = (c % 2) * TILE + s * P
                            mm = pe.transpose(trp[c // 2][:, at:at + P], x[:, s, c * P:(c + 1) * P], cst["ident_r"][:])
                    mm.then_inc(tr_r, 1)

                def tile(g, parity):
                    until(pe, xlo_r, 2 * g + 2)
                    owner = {}
                    for n, (at, cols_n, bk) in enumerate(chunks):
                        if bk in owner:
                            until(pe, h_r, NQ * g + owner[bk] + 1)
                        owner[bk] = piece_of[n]
                        for c in range(DC):
                            w_hi, w_lo = gu_hi[parity][:, c, at:at + cols_n], gu_lo[parity][:, c, at:at + cols_n]
                            out = gup[bk][0:cols_n, 0:TILE]
                            pe.matmul(out, w_hi, x_hi[:, c, :], start=(c == 0), stop=False)
                            pe.matmul(out, w_hi, x_lo[:, c, :], start=False, stop=False)
                            mm = pe.matmul(out, w_lo, x_hi[:, c, :], start=False, stop=(c == DC - 1))
                        mm.then_inc(chunk_r, 1)
                    transposes(g + 1)
                    until(pe, y_r, SUB * g)
                    for s in range(SUB):
                        for q, (rows, *_) in enumerate(pieces):
                            if s == 0:
                                until(pe, hs_r, NQ * g + q + 1)
                            a_hi = h_hi[0:rows, q, s * P:(s + 1) * P]
                            a_lo = h_lo[0:rows, q, s * P:(s + 1) * P]
                            w_hi, w_lo = dn_hi[parity][0:rows, q, :], dn_lo[parity][0:rows, q, :]
                            pe.matmul(dnp[s][:], a_hi, w_hi, start=(q == 0), stop=False)
                            pe.matmul(dnp[s][:], a_hi, w_lo, start=False, stop=False)
                            mm = pe.matmul(dnp[s][:], a_lo, w_hi, start=False, stop=(q == NQ - 1))
                        mm.then_inc(dn_r, 1)

                piece_of = {}
                for q, (_, gc, _, uc, _) in enumerate(pieces):
                    piece_of[gc] = piece_of[uc] = q

                def expert(e, parity, last):
                    until(pe, lo_r, e + 1)
                    each_tile(pe, e, lambda g: tile(g, parity))

                transposes(0)
                each_expert(pe, expert)


CHUNKS_A = [(0, 128, 0), (128, 128, 1), (256, 128, 2)]
PIECES_A = [(64, 0, 0, 0, 64), (128, 1, 0, 2, 0)]
CHUNKS_B = [(0, 128, 0), (128, 128, 1), (256, 128, 2), (384, 128, 3), (512, 96, 0), (608, 96, 1)]
PIECES_B = [(128, 0, 0, 1, 0), (128, 2, 0, 3, 0), (96, 4, 0, 5, 0)]

H = 16
R = 64
Q = 384
QC = Q // P
WS = DC * P + Q + P
WR = P + D


def add_and_transpose(nc, cst, X, acc_dram, ctx_in, cos_k, sin_k, xT_hi, xT_lo, kv, kvT_hi, kvT_lo):
    with ExitStack() as ctx:
        def mem(name, shape, dt=F32):
            return ctx.enter_context(nc.sbuf_tensor("t_" + name, shape, dt))

        sem = semaphores(nc, ctx, "t_")

        acc, N = mem("acc", [P, SJ, D]), mem("N", [P, SJ, D])
        stats, mv = mem("stats", [P, SJ, 6]), mem("mv", [P, SJ, 2])
        ve, rstd, nbias = mem("ve", [P, SJ]), mem("rstd", [P, SJ]), mem("nbias", [P, SJ])
        cos, sin, c_in = mem("cos", [P, SJ, C]), mem("sin", [P, SJ, C]), mem("ctx", [P, SJ, C])
        t1, t2 = mem("t1", [P, SJ, C]), mem("t2", [P, SJ, C])
        trp = [ctx.enter_context(nc.psum_tensor(f"t_tr{c}", [P, S], F32)) for c in range(DC)]
        kvp = ctx.enter_context(nc.psum_tensor("t_kv", [P, S], F32))
        tabs_in, acc_in, ctx_s, x_r, var_r, rstd_r, nb_r, n_r, tr_r, kv_r, kvp_r, hi_r, lo_r, khi_r, klo_r, dve_s = (
            sem(n) for n in ("tabs_in", "acc_in", "ctx_in", "x_added", "var", "rstd", "nbias", "rows_normal",
                             "transposed", "kv_rotated", "kv_transposed", "x_hi", "x_lo", "kv_hi", "kv_lo", "dve"))
        av = acc_dram[0:T, :].rearrange("(b j p) d -> b p j d", p=P, j=SJ)
        cv = ctx_in.rearrange("(b j p) c -> b p j c", p=P, j=SJ)
        STEPS = 12

        with nc.Block() as block:
            @block.sync
            def _(sp):
                sp.dma_start(cos[:], cos_k).then_inc(tabs_in, 16)
                sp.dma_start(sin[:], sin_k).then_inc(tabs_in, 16)
                with sp.Fori(0, B) as b:
                    until(sp, x_r, b)
                    sp.dma_start(acc[:], av[ds(b, 1)].rearrange("a p j d -> (a p) j d")).then_inc(acc_in, 16)
                    until(sp, kv_r, b)
                    sp.dma_start(c_in[:], cv[ds(b, 1)].rearrange("a p j c -> (a p) j c")).then_inc(ctx_s, 16)

            @block.gpsimd
            def _(pool):
                with pool.Fori(0, B) as b:
                    until(pool, var_r, b + 1)
                    pool.tensor_tensor(rstd[:], ve[:], cst["mhalf"][:, 0:SJ], ALU.pow).then_inc(rstd_r, 1)

            @block.scalar
            def _(act):
                with act.Fori(0, B) as b:
                    until(act, nb_r, b + 1)
                    until(act, tr_r, DC * b)
                    for j in range(SJ):
                        act.activation(N[:, j, :], X[:, ds(SJ * b + j, 1), :].rearrange("p a d -> p (a d)"),
                                       ACT.Identity, bias=nbias[:, j:j + 1], scale=rstd[:, j:j + 1]).then_inc(n_r, 1)
                    until(act, kvp_r, b + 1)
                    act.activation(kvT_hi[:, ds(S * b, S)], kvp[:], ACT.Copy).then_inc(khi_r, 1)
                    for c in range(DC):
                        until(act, tr_r, DC * b + c + 1)
                        act.activation(xT_hi[:, c, ds(S * b, S)], trp[c][:], ACT.Copy).then_inc(hi_r, 1)

            @block.tensor
            def _(pe):
                with pe.Fori(0, B) as b:
                    until(pe, kv_r, b + 1)
                    until(pe, klo_r, b)
                    for j in range(SJ):
                        mm = pe.transpose(kvp[:, j * P:(j + 1) * P], t1[:, j, :], cst["ident"][:])
                    mm.then_inc(kvp_r, 1)
                    until(pe, n_r, SJ * b + SJ)
                    until(pe, lo_r, DC * b)
                    for c in range(DC):
                        for j in range(SJ):
                            mm = pe.transpose(trp[c][:, j * P:(j + 1) * P], N[:, j, c * P:(c + 1) * P], cst["ident"][:])
                        mm.then_inc(tr_r, 1)

            @block.vector
            def _(dve):
                dve.wait_ge(tabs_in, 32)
                with dve.Fori(0, B) as b:
                    step = Steps(dve, dve_s, STEPS * b)
                    until(dve, acc_in, 16 * b + 16)
                    xs = X[:, ds(SJ * b, SJ), :]
                    dve.scalar_tensor_tensor(xs, acc[:], cst["tanhg"][:, 2:3], xs, ALU.mult, ALU.add).then_inc(x_r, 1)
                    until(dve, x_r, b + 1)
                    for j in range(SJ):
                        step(dve.bn_stats(stats[:, j, :], X[:, ds(SJ * b + j, 1), :].rearrange("p a d -> p (a d)")))
                    step.settle()
                    for j in range(SJ):
                        step(dve.bn_aggr(mv[:, j, :], stats[:, j, :]))
                    step.settle()
                    dve.tensor_scalar(ve[:], mv[:, :, 1], LN_EPS, None, ALU.add).then_inc(var_r, 1)
                    until(dve, ctx_s, 16 * b + 16)
                    until(dve, kvp_r, b)
                    step(dve.tensor_tensor(t1[:], c_in[:], cos[:], ALU.mult))
                    step(dve.tensor_tensor(t2[:, :, 0:C // 2], c_in[:, :, C // 2:C], sin[:, :, 0:C // 2], ALU.mult))
                    step(dve.tensor_tensor(t2[:, :, C // 2:C], c_in[:, :, 0:C // 2], sin[:, :, C // 2:C], ALU.mult))
                    step.settle()
                    step(dve.tensor_tensor(t1[:], t1[:], t2[:], ALU.add))
                    step.settle()
                    dve.tensor_copy(kv[:, ds(SJ * b, SJ), :], t1[:]).then_inc(kv_r, 1)
                    until(dve, rstd_r, b + 1)
                    dve.scalar_tensor_tensor(nbias[:], mv[:, :, 0], -1.0, rstd[:], ALU.mult, ALU.mult).then_inc(nb_r, 1)
                    until(dve, khi_r, b + 1)
                    dve.tensor_tensor(kvT_lo[:, ds(S * b, S)], kvp[:], kvT_hi[:, ds(S * b, S)].bitcast(F32),
                                      ALU.subtract).then_inc(klo_r, 1)
                    for c in range(DC):
                        until(dve, hi_r, DC * b + c + 1)
                        dve.tensor_tensor(xT_lo[:, c, ds(S * b, S)], trp[c][:], xT_hi[:, c, ds(S * b, S)].bitcast(F32),
                                          ALU.subtract).then_inc(lo_r, 1)
                    assert step.n == STEPS


def second_layer_attention(nc, cst, X, ws_in, wqr_in, wr_in, cosT_in, sinT_in, xT_hi, xT_lo, kv, kvT_hi, kvT_lo):
    with ExitStack() as ctx:
        def mem(name, shape, dt=F32):
            return ctx.enter_context(nc.sbuf_tensor("s_" + name, shape, dt))

        sem = semaphores(nc, ctx, "s_")

        cosT, sinT = mem("cosT", [P, QC, S]), mem("sinT", [P, QC, S])
        raw, rawv = mem("raw", [P, WS]), mem("rawv", [P, WR])
        w_hi, w_lo = [[mem(f"w_{n}{i}", [P, WS], F32R) for i in (0, 1)] for n in ("hi", "lo")]
        v_hi, v_lo = [[mem(f"v_{n}{i}", [P, D], F32R) for i in (0, 1)] for n in ("hi", "lo")]
        wqr = [mem(f"wqr{i}", [P, QC, R]) for i in (0, 1)]
        qh_hi, qh_lo = mem("qh_hi", [P, S], F32R), mem("qh_lo", [P, S], F32R)
        q, t = mem("q", [P, QC, S]), mem("t", [P, QC, S])
        q2, q3 = mem("q2", [P, S], F32R), mem("q3", [R + 1, S], F32R)
        k2, k3 = mem("k2", [P, S], F32R), mem("k3", [R + 1, S], F32R)
        top = mem("top", [P, SJ])
        pT = mem("pT", [P, SJ, S])
        s4 = mem("s4", [P, S])
        gsum = mem("gsum", [P, SJ])
        c_hi, c_lo = mem("c_hi", [P, S], F32R), mem("c_lo", [P, S], F32R)
        ap = ctx.enter_context(nc.psum_tensor("s_a", [P, 4, S], F32))
        bp = ctx.enter_context(nc.psum_tensor("s_b", [P, 4, S], F32))
        names = ("tabs_in", "raw_in", "wqr_in", "w_hi", "w_lo", "v_made", "v_hi", "v_lo", "qh_made", "qh_hi", "qh_lo",
                 "big_made", "dve", "rotated", "q_made", "q2_hi", "q3_hi", "q_lo", "k_made", "k_hi", "k_lo",
                 "smax_made", "top", "top_rows", "top_kept", "scores", "exp", "pairs_added", "sum_in", "ctx_made",
                 "sum_made", "recip", "c_hi", "c_lo", "out_made", "x_added", "ones_row")
        (tabs_in, raw_in, wqr_s, whi_r, wlo_r, vp_r, vhi_r, vlo_r, qh_r, qhhi_r, qhlo_r, big_r, dve_s, rot_r, q_r,
         q2_r, q3_r, qlo_r, k_r, khi_r, klo_r, smax_r, top_r, row_r, m_r, sc_r, e_r, pair_r, s4_r, ctx_r, sum_r, rec_r,
         chi_r, clo_r, out_r, x_r, one_r) = (sem(n) for n in names)
        KQ, KB, KK = 0, DC * P, DC * P + Q

        def heads(eng, step):
            def pair(h0, last):
                for hp in (0, 1):
                    for b in range(B):
                        n = B * (h0 + hp) + b
                        step(n, h0 + hp, b, hp, last and hp == 1 and b == B - 1, last and hp == 1)

            with eng.Fori(0, H // 2 - 1) as i:
                pair(2 * i, False)
            pair(H - 2, True)

        def nxt(b, parity):
            return (b + 1, parity) if b + 1 < B else (0, 1 - parity)

        with nc.Block() as block:
            @block.sync
            def _(sp):
                sp.dma_start(cosT[:], cosT_in).then_inc(tabs_in, 16)
                sp.dma_start(sinT[:], sinT_in).then_inc(tabs_in, 16)

                def load(h, parity):
                    sp.dma_start(raw[:], ws_in[ds(h, 1)].rearrange("a p w -> (a p) w")).then_inc(raw_in, 16)
                    sp.dma_start(rawv[:], wr_in[ds(h, 1)].rearrange("a p w -> (a p) w")).then_inc(raw_in, 16)
                    sp.dma_start(wqr[parity][:], wqr_in[ds(h, 1)].rearrange("a p c r -> (a p) c r")).then_inc(wqr_s, 16)

                def step(n, h, b, parity, last, last_head):
                    if b == 0 and not last_head:
                        until(sp, wlo_r, h + 1)
                        until(sp, vp_r, h + 1)
                        load(h + 1, 1 - parity)

                load(0, 0)
                heads(sp, step)

            @block.gpsimd
            def _(pool):
                def step(n, h, b, parity, last, last_head):
                    until(pool, e_r, SJ * n + 2)
                    until(pool, sum_r, n)
                    pool.tensor_tensor(s4[:], pT[:, 0, :], pT[:, 1, :], ALU.add).then_inc(pair_r, 1)
                    for j in (2, 3):
                        until(pool, e_r, SJ * n + j + 1)
                        until(pool, pair_r, 2 * n + j - 1)
                        pool.tensor_tensor(s4[:], s4[:], pT[:, j, :], ALU.add).then_inc(s4_r if j == 3 else pair_r, 1)
                heads(pool, step)

            @block.scalar
            def _(act):
                def split_w(h, parity):
                    until(act, raw_in, 32 * h + 32)
                    act.activation(w_hi[parity][:], raw[:], ACT.Copy).then_inc(whi_r, 1)

                def split_v(h, parity):
                    until(act, vp_r, h + 1)
                    act.activation(v_hi[parity][:], ap[:, 3, :], ACT.Copy).then_inc(vhi_r, 1)

                def queries(n):
                    until(act, qh_r, n + 1)
                    act.activation(qh_hi[:], bp[:, 0, :], ACT.Copy).then_inc(qhhi_r, 1)

                def keys(n):
                    until(act, q_r, n + 1)
                    act.activation(q3[0:R, :], ap[0:R, 1, :], ACT.Copy).then_inc(q3_r, 1)
                    act.activation(q2[0:R, :], ap[0:R, 1, :], ACT.Copy).then_inc(q2_r, 1)
                    until(act, k_r, n + 1)
                    act.activation(k2[:], ap[:, 2, :], ACT.Copy).then_inc(khi_r, 1)

                def step(n, h, b, parity, last, last_head):
                    if not last:
                        queries(n + 1)
                    until(act, row_r, n + 1)
                    act.activation(q3[R:R + 1, :], bp[0:1, 1, :], ACT.Copy, scale=-1.0).then_inc(m_r, 1)
                    for j in range(SJ):
                        until(act, sc_r, SJ * n + j + 1)
                        act.activation(pT[:, j, :], ap[:, j, :], ACT.Exp).then_inc(e_r, 1)
                    if b == B - 2 and not last_head:
                        split_w(h + 1, 1 - parity)
                    if b == B - 1 and not last_head:
                        split_v(h + 1, 1 - parity)
                    until(act, ctx_r, n + 1)
                    act.activation(c_hi[:], bp[:, 0, :], ACT.Copy).then_inc(chi_r, 1)
                    if not last:
                        keys(n + 1)

                split_w(0, 0)
                split_v(0, 0)
                queries(0)
                keys(0)
                heads(act, step)

            @block.vector
            def _(dve):
                def split_w(h, parity):
                    until(dve, whi_r, h + 1)
                    dve.tensor_tensor(w_lo[parity][:], raw[:], w_hi[parity][:].bitcast(F32),
                                      ALU.subtract).then_inc(wlo_r, 1)

                def split_v(h, parity):
                    until(dve, vhi_r, h + 1)
                    dve.tensor_tensor(v_lo[parity][:], ap[:, 3, :], v_hi[parity][:].bitcast(F32),
                                      ALU.subtract).then_inc(vlo_r, 1)

                def queries(n):
                    until(dve, qhhi_r, n + 1)
                    dve.tensor_tensor(qh_lo[:], bp[:, 0, :], qh_hi[:].bitcast(F32), ALU.subtract).then_inc(qhlo_r, 1)

                def rotate(n):
                    done = 8 * n
                    until(dve, big_r, QC * n + 2)
                    until(dve, q_r, n)
                    dve.tensor_tensor(q[:, 0, :], bp[:, 1, :], cosT[:, 0, :], ALU.mult).then_inc(dve_s, 1)
                    dve.tensor_tensor(t[:, 0, :], bp[:, 2, :], sinT[:, 0, :], ALU.mult).then_inc(dve_s, 1)
                    dve.tensor_tensor(q[:, 1, :], bp[:, 2, :], cosT[:, 1, :], ALU.mult).then_inc(dve_s, 1)
                    dve.tensor_tensor(t[:, 1, :], bp[:, 1, :], sinT[:, 1, :], ALU.mult).then_inc(dve_s, 1)
                    until(dve, dve_s, done + 2)
                    dve.tensor_tensor(q[:, 0, :], q[:, 0, :], t[:, 0, :], ALU.add).then_inc(rot_r, 1)
                    until(dve, dve_s, done + 4)
                    dve.tensor_tensor(q[:, 1, :], q[:, 1, :], t[:, 1, :], ALU.add).then_inc(rot_r, 1)
                    until(dve, big_r, QC * n + 3)
                    half = P // 2
                    dve.tensor_tensor(q[:, 2, :], bp[:, 3, :], cosT[:, 2, :], ALU.mult).then_inc(dve_s, 1)
                    dve.tensor_tensor(t[0:half, 2, :], bp[half:P, 3, :], sinT[half:P, 2, :], ALU.mult).then_inc(dve_s, 1)
                    dve.tensor_tensor(t[half:P, 2, :], bp[0:half, 3, :], sinT[0:half, 2, :], ALU.mult).then_inc(dve_s, 1)
                    until(dve, dve_s, done + 7)
                    dve.tensor_tensor(q[:, 2, :], q[:, 2, :], t[:, 2, :], ALU.add).then_inc(rot_r, 1)
                    dve.engine_nop().then_inc(dve_s, 1)

                def keys(n):
                    until(dve, q3_r, n + 1)
                    until(dve, q2_r, n + 1)
                    dve.tensor_tensor(q2[R:2 * R, :], ap[0:R, 1, :], q3[0:R, :].bitcast(F32),
                                      ALU.subtract).then_inc(qlo_r, 1)
                    until(dve, khi_r, n + 1)
                    dve.tensor_tensor(k3[0:R, :], ap[0:R, 2, :], k2[0:R, :].bitcast(F32),
                                      ALU.subtract).then_inc(klo_r, 1)

                def step(n, h, b, parity, last, last_head):
                    for j in range(SJ):
                        until(dve, smax_r, SJ * n + j + 1)
                        dve.tensor_reduce(top[:, j:j + 1], ap[:, j, :], AX_X, ALU.max).then_inc(top_r, 1)
                    if not last:
                        queries(n + 1)
                        if b == B - 2 and not last_head:
                            split_w(h + 1, 1 - parity)
                        rotate(n + 1)
                    until(dve, chi_r, n + 1)
                    dve.tensor_tensor(c_lo[:], bp[:, 0, :], c_hi[:].bitcast(F32), ALU.subtract).then_inc(clo_r, 1)
                    until(dve, sum_r, n + 1)
                    dve.reciprocal(gsum[:], ap[:, 0, 0:SJ]).then_inc(rec_r, 1)
                    until(dve, rec_r, 2 * n + 1)
                    dve.tensor_scalar(gsum[:], gsum[:], cst["tanhg"][:, 1:2], None, ALU.mult).then_inc(rec_r, 1)
                    if not last:
                        keys(n + 1)
                    if b == B - 1 and not last_head:
                        split_v(h + 1, 1 - parity)
                    until(dve, rec_r, 2 * n + 2)
                    for j in range(SJ):
                        until(dve, out_r, SJ * n + j + 1)
                        rows = X[:, SJ * b + j, :]
                        dve.scalar_tensor_tensor(rows, bp[:, j, :], gsum[:, j:j + 1], rows, ALU.mult,
                                                 ALU.add).then_inc(x_r, 1)

                dve.wait_ge(tabs_in, 32)
                dve.memset(k3[R:R + 1, :].bitcast(F32), 1.0).then_inc(one_r, 1)
                split_w(0, 0)
                split_v(0, 0)
                queries(0)
                rotate(0)
                keys(0)
                heads(dve, step)

            @block.tensor
            def _(pe):
                def three(out, a_hi, a_lo, b_hi, b_lo, start=True, stop=True):
                    pe.matmul(out, a_hi, b_hi, start=start, stop=False)
                    pe.matmul(out, a_hi, b_lo, start=False, stop=False)
                    return pe.matmul(out, a_lo, b_hi, start=False, stop=stop)

                def queries(n, b, parity):
                    for c in range(DC):
                        w = slice(KQ + c * P, KQ + (c + 1) * P)
                        mm = three(bp[:, 0, :], w_hi[parity][:, w], w_lo[parity][:, w],
                                   xT_hi[:, c, b * S:(b + 1) * S], xT_lo[:, c, b * S:(b + 1) * S], c == 0, c == DC - 1)
                    mm.then_inc(qh_r, 1)

                def big(n, parity):
                    until(pe, qhlo_r, n + 1)
                    for c in range(QC):
                        w = slice(KB + c * P, KB + (c + 1) * P)
                        three(bp[:, 1 + c, :], w_hi[parity][:, w], w_lo[parity][:, w], qh_hi[:],
                              qh_lo[:]).then_inc(big_r, 1)

                def keys(n, b, parity):
                    for c in range(QC):
                        until(pe, rot_r, QC * n + c + 1)
                        mm = pe.matmul(ap[0:R, 1, :], wqr[parity][:, c, :], q[:, c, :], start=(c == 0),
                                       stop=(c == QC - 1))
                    mm.then_inc(q_r, 1)
                    w = slice(KK, KK + P)
                    three(ap[:, 2, :], w_hi[parity][:, w], w_lo[parity][:, w], kvT_hi[:, b * S:(b + 1) * S],
                          kvT_lo[:, b * S:(b + 1) * S]).then_inc(k_r, 1)

                def values(h):
                    until(pe, raw_in, 32 * h + 32)
                    pe.matmul(ap[:, 3, :], rawv[:, 0:P], rawv[:, P:P + D], start=True, stop=True).then_inc(vp_r, 1)

                def step(n, h, b, parity, last, last_head):
                    until(pe, klo_r, n + 1)
                    until(pe, qlo_r, n + 1)
                    if b == 0:
                        until(pe, vlo_r, h + 1)
                    for j in range(SJ):
                        pe.matmul(ap[:, j, :], q3[0:R, j * P:(j + 1) * P], k2[0:R, :], start=True,
                                  stop=True).then_inc(smax_r, 1)
                    nb, np_ = nxt(b, parity)
                    until(pe, x_r, SJ * n)
                    if not last:
                        if b == B - 1:
                            until(pe, wlo_r, h + 2)
                            until(pe, wqr_s, 16 * h + 32)
                        queries(n + 1, nb, np_)
                    until(pe, top_r, SJ * n + SJ)
                    for j in range(SJ):
                        mm = pe.transpose(bp[0:1, 1, j * P:(j + 1) * P], top[:, j:j + 1], cst["ident"][:])
                    mm.then_inc(row_r, 1)
                    until(pe, m_r, n + 1)
                    for j in range(SJ):
                        pe.matmul(ap[:, j, :], k2[:, j * P:(j + 1) * P], q2[:], start=True, stop=False)
                        pe.matmul(ap[:, j, :], k3[:, j * P:(j + 1) * P], q3[:], start=False, stop=True).then_inc(sc_r, 1)
                    if not last:
                        big(n + 1, np_)
                    for j in range(SJ):
                        until(pe, e_r, SJ * n + j + 1)
                        mm = pe.matmul(bp[:, 0, :], kv[:, SJ * b + j, :], pT[:, j, :], start=(j == 0), stop=(j == SJ - 1))
                    mm.then_inc(ctx_r, 1)
                    until(pe, s4_r, n + 1)
                    for j in range(SJ):
                        mm = pe.matmul(ap[:, 0, j:j + 1], s4[:, j * P:(j + 1) * P], cst["ones"][:, 0:1], start=True,
                                       stop=True)
                    mm.then_inc(sum_r, 1)
                    if b == B - 1 and not last_head:
                        values(h + 1)
                    if not last:
                        keys(n + 1, nb, np_)
                    until(pe, clo_r, n + 1)
                    for j in range(SJ):
                        rows = slice(j * P, (j + 1) * P)
                        three(bp[:, j, :], c_hi[:, rows], c_lo[:, rows], v_hi[parity][:], v_lo[parity][:]).then_inc(out_r, 1)

                pe.wait_ge(wqr_s, 16)
                values(0)
                pe.wait_ge(one_r, 1)
                pe.wait_ge(wlo_r, 1)
                queries(0, 0, 0)
                big(0, 0)
                keys(0, 0, 0)
                heads(pe, step)


def second_attention_all(nc, cst, X, acc_dram, ctx_in, cos_k, sin_k, ws_in, wqr_in, wr_in, cosT_in, sinT_in):
    with ExitStack() as ctx:
        def mem(name, shape, dt=F32):
            return ctx.enter_context(nc.sbuf_tensor(name, shape, dt))

        xT_hi, xT_lo = mem("xT_hi", [P, DC, T], F32R), mem("xT_lo", [P, DC, T], F32R)
        kvT_hi, kvT_lo = mem("kvT_hi", [P, T], F32R), mem("kvT_lo", [P, T], F32R)
        kv = mem("kv", [P, NT, C])
        add_and_transpose(nc, cst, X, acc_dram, ctx_in, cos_k, sin_k, xT_hi, xT_lo, kv, kvT_hi, kvT_lo)
        second_layer_attention(nc, cst, X, ws_in, wqr_in, wr_in, cosT_in, sinT_in, xT_hi, xT_lo, kv, kvT_hi, kvT_lo)

E2, K2, CAP = 16, 2, 256
COLS2 = E2 * CAP // P
TILES2 = E2 * CAP // TILE + T // TILE


def second_layer_routing(nc, cst, X, gw_in, bias_in, xn_dram, tab_dram, acc_dram, table):
    with ExitStack() as ctx:
        def mem(name, shape, dt=F32):
            return ctx.enter_context(nc.sbuf_tensor("r_" + name, shape, dt))

        sem = semaphores(nc, ctx, "r_")

        M = NT * K2
        gw, bias = mem("gw", [P, DC, E2]), mem("bias", [P, E2])
        N, NTr = mem("N", [P, SJ, D]), mem("NT", [P, DC, S])
        stats, mv = mem("stats", [P, SJ, 6]), mem("mv", [P, SJ, 2])
        ve, rstd, nbias = mem("ve", [P, SJ]), mem("rstd", [P, SJ]), mem("nbias", [P, SJ])
        lg, score, pick = mem("lg", [P, NT, E2]), mem("score", [P, NT, E2]), mem("pick", [P, NT, E2])
        u, w1, d, dz = mem("u", [P, NT, E2]), mem("w1", [P, NT, E2]), mem("d", [P, NT, E2]), mem("dz", [P, NT, E2])
        ln = mem("ln", [P, NT, E2])
        top8, idx8 = mem("top8", [P, NT, 8]), mem("idx8", [P, NT, 8], U32)
        idxf = mem("idxf", [P, NT, K2])
        hot, tmp = mem("hot", [P, M, E2]), mem("tmp", [P, M, E2])
        mask, pref = mem("mask", [P, NT, E2]), mem("pref", [P, NT, E2])
        pos, low, pos_i = mem("pos", [P, NT * E2]), mem("low", [P, NT * E2], I32), mem("pos_i", [P, NT * E2], I32)
        addr = mem("addr", [P, NT * E2])
        s_k, p_k, a_k, valid = mem("s_k", [P, M]), mem("p_k", [P, M]), mem("a_k", [P, M]), mem("valid", [P, M])
        wsum, slot = mem("wsum", [P, NT]), mem("slot", [P, M], I32)
        entry = mem("entry", [P, NT, K2, 2], I32)
        iota_e, e2, ids, spare = (mem("iota_e", [P, E2], I32), mem("e2", [P, NT, E2], I32),
                                  mem("ids", [P, NT, K2], I32), mem("spare", [P, NT, K2], I32))
        iota_ef, spare_f, weight1 = mem("iota_ef", [P, E2]), mem("spare_f", [P, M]), mem("weight1", [P, NT + SUB * 2])
        init, zeros = mem("init", [P, COLS2, 2], I32), mem("zeros", [P, D])
        trp = [ctx.enter_context(nc.psum_tensor(f"r_tr{c}", [P, S], F32)) for c in range(DC)]
        lgp = ctx.enter_context(nc.psum_tensor("r_logits_sum", [P, SJ, E2], F32))
        posp = ctx.enter_context(nc.psum_tensor("r_place_sum", [P, NT * E2], F32))
        (c_in, var_r, rstd_r, nb_r, n_r, tr_r, keep_a, keep_v, lg_r, lgk_r, dve_s, rows_out, cleared, iota_r, init_s,
         zeros_r, abs_r, u_r, w1_r, ln_r, sp_r, score_r, mask_r, pos_r, route_r, tab_in) = (sem(n) for n in (
             "consts_in", "var", "rstd", "nbias", "rows_normal", "transposed", "kept_by_act", "kept_by_dve",
             "logits_made", "logits_kept", "dve", "rows_out", "cleared", "iota", "tab_init", "zeros", "abs", "exp",
             "one_plus", "ln", "softplus", "score", "mask", "pos", "route", "tab_in"))
        tab_out = cst["b_table_out"]
        xnv = xn_dram[0:T, :].rearrange("(b j p) d -> b p j d", p=P, j=SJ)
        STEPS = 8

        with nc.Block() as block:
            @block.sync
            def _(sp):
                sp.dma_start(gw[:], gw_in).then_inc(c_in, 16)
                sp.dma_start(bias[:], bias_in.partition_broadcast(P)).then_inc(c_in, 16)
                sp.wait_ge(iota_r, 7)
                sp.dma_start(tab_dram[0:E2 * CAP, :].rearrange("(p c) w -> p c w", p=P), init[:]).then_inc(init_s, 16)
                sp.wait_ge(zeros_r, 1)
                sp.dma_start(xn_dram[T:T + P, :], zeros[:]).then_inc(init_s, 16)
                clear_rows(sp, zeros, acc_dram, cleared)
                with sp.Fori(0, B) as b:
                    until(sp, n_r, SJ * b + SJ)
                    sp.dma_start(xnv[ds(b, 1)].rearrange("a p j d -> (a p) j d"), N[:]).then_inc(rows_out, 16)
                sp.wait_ge(rows_out, 16 * B)
                sp.wait_ge(cleared, 16 * (NT + 1))
                sp.wait_ge(init_s, 32)
                sp.wait_ge(tab_out, 16 * M)
                sp.dma_start(table[:, 0:COLS2, :],
                             tab_dram[0:E2 * CAP, :].rearrange("(p c) w -> p c w", p=P)).then_inc(tab_in, 16)
                sp.wait_ge(tab_in, 16)

            @block.gpsimd
            def _(pool):
                pool.iota(iota_e[:], [[1, E2]], base=0, channel_multiplier=0).then_inc(iota_r, 1)
                pool.iota(e2[:], [[0, NT], [CAP // P, E2]], base=0, channel_multiplier=0).then_inc(iota_r, 1)
                pool.iota(ids[:], [[P, NT], [0, K2]], base=0, channel_multiplier=1).then_inc(iota_r, 1)
                pool.iota(spare[:], [[P, NT], [T, K2]], base=E2 * CAP, channel_multiplier=1).then_inc(iota_r, 1)
                pool.iota(init[:, :, 0], [[0, COLS2]], base=T, channel_multiplier=1).then_inc(iota_r, 1)
                pool.memset(init[:, :, 1], 0).then_inc(iota_r, 1)
                pool.iota(table[:, COLS2:COLS2 + NT, 0], [[P, NT]], base=0, channel_multiplier=1).then_inc(iota_r, 1)
                pool.memset(table[:, COLS2 + NT:COLS2 + NT + 2 * SUB, 0], 0).then_inc(iota_r, 1)
                with pool.Fori(0, B) as b:
                    until(pool, var_r, b + 1)
                    pool.tensor_tensor(rstd[:], ve[:], cst["mhalf"][:, 0:SJ], ALU.pow).then_inc(rstd_r, 1)
                pool.wait_ge(init_s, 32)
                pool.wait_ge(route_r, 1)
                for m in range(M):
                    j, k = divmod(m, K2)
                    pool.indirect_dma_start(
                        out=tab_dram, out_offset=bass.IndirectOffsetOnAxis(ap=slot[:, m:m + 1], axis=0),
                        in_=entry[:, j, k, :], in_offset=None).then_inc(tab_out, 16)
                pool.wait_ge(tab_out, 16 * M)

            @block.scalar
            def _(act):
                with act.Fori(0, B) as b:
                    until(act, nb_r, b + 1)
                    until(act, tr_r, DC * b)
                    until(act, rows_out, 16 * b)
                    for j in range(SJ):
                        act.activation(N[:, j, :], X[:, ds(SJ * b + j, 1), :].rearrange("p a d -> p (a d)"),
                                       ACT.Identity, bias=nbias[:, j:j + 1], scale=rstd[:, j:j + 1]).then_inc(n_r, 1)
                    until(act, lg_r, b)
                    for c in (0, 1):
                        until(act, tr_r, DC * b + c + 1)
                        act.activation(NTr[:, c, :], trp[c][:], ACT.Copy).then_inc(keep_a, 1)
                act.wait_ge(abs_r, 1)
                act.activation(u[:], u[:], ACT.Exp).then_inc(u_r, 1)
                act.wait_ge(w1_r, 1)
                act.activation(ln[:], w1[:], ACT.Ln).then_inc(ln_r, 1)
                act.wait_ge(sp_r, 1)
                act.activation(score[:], score[:], ACT.Sqrt).then_inc(score_r, 1)

            @block.tensor
            def _(pe):
                pe.wait_ge(c_in, 32)
                with pe.Fori(0, B) as b:
                    until(pe, n_r, SJ * b + SJ)
                    until(pe, keep_v, 2 * b)
                    until(pe, keep_a, 2 * b)
                    for c in range(DC):
                        for j in range(SJ):
                            mm = pe.transpose(trp[c][:, j * P:(j + 1) * P], N[:, j, c * P:(c + 1) * P], cst["ident"][:])
                        mm.then_inc(tr_r, 1)
                    until(pe, keep_a, 2 * b + 2)
                    until(pe, keep_v, 2 * b + 2)
                    until(pe, lgk_r, b)
                    for j in range(SJ):
                        for c in range(DC):
                            mm = pe.matmul(lgp[:, j, :], NTr[:, c, j * P:(j + 1) * P], gw[:, c, :],
                                           start=(c == 0), stop=(c == DC - 1))
                    mm.then_inc(lg_r, 1)
                pe.wait_ge(mask_r, 1)
                pe.matmul(posp[:], cst["before"][:], mask[:].rearrange("p j e -> p (j e)"), start=True, stop=False)
                pe.matmul(posp[:], cst["ones"][:], pref[:].rearrange("p j e -> p (j e)"), start=False,
                          stop=True).then_inc(pos_r, 1)

            @block.vector
            def _(dve):
                dve.memset(zeros[:], 0.0).then_inc(zeros_r, 1)
                with dve.Fori(0, B) as b:
                    step = Steps(dve, dve_s, STEPS * b)
                    for j in range(SJ):
                        step(dve.bn_stats(stats[:, j, :], X[:, ds(SJ * b + j, 1), :].rearrange("p a d -> p (a d)")))
                    step.settle()
                    for j in range(SJ):
                        step(dve.bn_aggr(mv[:, j, :], stats[:, j, :]))
                    step.settle()
                    dve.tensor_scalar(ve[:], mv[:, :, 1], LN_EPS, None, ALU.add).then_inc(var_r, 1)
                    until(dve, rstd_r, b + 1)
                    dve.scalar_tensor_tensor(nbias[:], mv[:, :, 0], -1.0, rstd[:], ALU.mult, ALU.mult).then_inc(nb_r, 1)
                    until(dve, lg_r, b)
                    for c in (2, 3):
                        until(dve, tr_r, DC * b + c + 1)
                        dve.tensor_copy(NTr[:, c, :], trp[c][:]).then_inc(keep_v, 1)
                    until(dve, lg_r, b + 1)
                    dve.tensor_copy(lg[:, ds(SJ * b, SJ), :], lgp[:]).then_inc(lgk_r, 1)
                    assert step.n == STEPS
                step = Steps(dve, dve_s, STEPS * B)
                dve.wait_ge(lgk_r, B)
                dve.wait_ge(iota_r, 8)
                dve.scalar_tensor_tensor(u[:], lg[:], -1.0, lg[:], ALU.mult, ALU.min).then_inc(abs_r, 1)
                dve.wait_ge(u_r, 1)
                dve.tensor_scalar(w1[:], u[:], 1.0, None, ALU.add).then_inc(w1_r, 1)
                dve.wait_ge(w1_r, 1)
                step(dve.tensor_scalar(d[:], w1[:], -1.0, None, ALU.add))
                step.settle()
                step(dve.tensor_scalar(dz[:], d[:], 0.0, None, ALU.is_equal))
                step.settle()
                step(dve.tensor_tensor(d[:], d[:], dz[:], ALU.add))
                step.settle()
                step(dve.reciprocal(d[:], d[:]))
                step(dve.tensor_tensor(dz[:], dz[:], u[:], ALU.mult))
                dve.wait_ge(ln_r, 1)
                step(dve.tensor_tensor(ln[:], ln[:], u[:], ALU.mult))
                step.settle()
                step(dve.tensor_tensor(ln[:], ln[:], d[:], ALU.mult))
                step.settle()
                step(dve.tensor_tensor(ln[:], ln[:], dz[:], ALU.add))
                step.settle()
                dve.scalar_tensor_tensor(score[:], lg[:], 0.0, ln[:], ALU.max, ALU.add).then_inc(sp_r, 1)
                dve.wait_ge(c_in, 32)
                dve.wait_ge(score_r, 1)
                step(dve.tensor_tensor(pick[:], score[:], over(bias[:], 1, NT), ALU.add))
                step.settle()
                for j in range(NT):
                    step(dve.max(top8[:, j, :], pick[:, j, :]))
                step.settle()
                for j in range(NT):
                    step(dve.max_index(idx8[:, j, :], top8[:, j, :], pick[:, j, :]))
                step(dve.tensor_copy(iota_ef[:], iota_e[:]))
                step(dve.tensor_copy(spare_f[:], spare[:].rearrange("p j k -> p (j k)")))
                step(dve.memset(weight1[:], 1.0))
                step.settle()
                step(dve.tensor_copy(idxf[:], idx8[:, :, 0:K2]))
                step(dve.tensor_copy(table[:, COLS2:, 1].bitcast(F32), weight1[:]))
                step.settle()
                step(dve.tensor_tensor(hot[:], over(idxf[:].rearrange("p j k -> p (j k)"), 2, E2),
                                       over(iota_ef[:], 1, M), ALU.is_equal))
                step.settle()
                step(dve.tensor_reduce(mask[:], hot[:].rearrange("p (j k) e -> p j e k", k=K2), AX_X, ALU.add))
                step(dve.memset(pref[:, 0, :], 0.0))
                step.settle()
                for j in range(NT - 1):
                    step(dve.tensor_tensor(pref[:, j + 1, :], pref[:, j, :], mask[:, j, :], ALU.add))
                    step.settle()
                dve.engine_nop().then_inc(mask_r, 1)

                def chosen(out, values):
                    step(dve.tensor_tensor(tmp[:].rearrange("p (j k) e -> p j k e", k=K2),
                                           hot[:].rearrange("p (j k) e -> p j k e", k=K2), over(values, 2, K2),
                                           ALU.mult))
                    step.settle()
                    step(dve.tensor_reduce(out, tmp[:], AX_X, ALU.add))
                    step.settle()

                def per_expert(ap):
                    return ap[:].rearrange("p (j e) -> p j e", e=E2)

                chosen(s_k[:], score[:])
                step(dve.tensor_reduce(wsum[:], s_k[:].rearrange("p (j k) -> p j k", k=K2), AX_X, ALU.add))
                step.settle()
                step(dve.reciprocal(wsum[:], wsum[:]))
                dve.wait_ge(pos_r, 1)
                step(dve.tensor_copy(pos[:], posp[:]))
                step.settle()
                step(dve.tensor_copy(pos_i[:], pos[:]))
                chosen(p_k[:], per_expert(pos))
                step(dve.tensor_scalar(valid[:], p_k[:], float(CAP), None, ALU.is_lt))
                step(dve.tensor_scalar(low[:], pos_i[:], P - 1, COLS2.bit_length() - 1, ALU.bitwise_and,
                                       ALU.logical_shift_left))
                step(dve.tensor_scalar(pos_i[:], pos_i[:], P.bit_length() - 1, None, ALU.logical_shift_right))
                step.settle()
                step(dve.tensor_tensor(low[:], low[:], pos_i[:], ALU.add))
                step.settle()
                step(dve.tensor_tensor(addr[:], low[:], e2[:].rearrange("p j e -> p (j e)"), ALU.add))
                step.settle()
                chosen(a_k[:], per_expert(addr))
                step(dve.tensor_tensor(a_k[:], a_k[:], spare_f[:], ALU.subtract))
                step.settle()
                step(dve.tensor_tensor(a_k[:], a_k[:], valid[:], ALU.mult))
                step(dve.tensor_tensor(s_k[:], s_k[:], valid[:], ALU.mult))
                step.settle()
                step(dve.tensor_tensor(slot[:], a_k[:], spare_f[:], ALU.add))
                step(dve.tensor_tensor(entry[:, :, :, 1].bitcast(F32), s_k[:].rearrange("p (j k) -> p j k", k=K2),
                                       over(wsum[:], 2, K2), ALU.mult))
                step(dve.tensor_copy(entry[:, :, :, 0], ids[:]))
                step.settle()
                dve.engine_nop().then_inc(route_r, 1)


def add_and_store(nc, cst, X, acc_dram, out):
    with ExitStack() as ctx:
        acc = ctx.enter_context(nc.sbuf_tensor("o_acc", [P, NT, D], F32))
        acc_in = [ctx.enter_context(nc.semaphore(f"o_acc_in{b}")) for b in range(B)]
        sum_r, out_s = ctx.enter_context(nc.semaphore("o_sum")), ctx.enter_context(nc.semaphore("o_out"))
        av = acc_dram[0:T, :].rearrange("(b j p) d -> b p j d", p=P, j=SJ)
        ov = out.rearrange("(b j p) d -> b p j d", p=P, j=SJ)
        with nc.Block() as block:
            @block.sync
            def _(sp):
                for b in range(B):
                    sp.dma_start(acc[:, SJ * b:SJ * (b + 1), :], av[b]).then_inc(acc_in[b], 16)
                for b in range(B):
                    sp.wait_ge(sum_r, b + 1)
                    sp.dma_start(ov[b], X[:, SJ * b:SJ * (b + 1), :]).then_inc(out_s, 16)
                sp.wait_ge(out_s, 16 * B)

            @block.vector
            def _(dve):
                for b in range(B):
                    dve.wait_ge(acc_in[b], 16)
                    rows = slice(SJ * b, SJ * (b + 1))
                    dve.scalar_tensor_tensor(X[:, rows, :], acc[:, rows, :], cst["tanhg"][:, 3:4], X[:, rows, :],
                                             ALU.mult, ALU.add).then_inc(sum_r, 1)


def two_layers(nc, a, out):
    with ExitStack() as ctx:
        def mem(name, shape, dt=F32):
            return ctx.enter_context(nc.sbuf_tensor(name, shape, dt))

        def sem(name):
            return ctx.enter_context(nc.semaphore(name))

        def dram(name, shape, dt=F32):
            return nc.dram_tensor(name, shape, dt, kind="Internal").ap()

        cst = constants(nc, mem, sem, a["gates"])
        for name in ("a_table_out", "b_table_out", "e_rows_in", "e_rows_added", "f_rows_in", "f_rows_added"):
            cst[name] = sem(name)
        X = mem("X", [P, NT, D])
        rows_a, rows_b = dram("rows_a", (T + P, D)), dram("rows_b", (T + P, D))
        sum_a, sum_b = dram("sum_a", (T + P, D)), dram("sum_b", (T + P, D))
        tab_a, tab_b = dram("tab_a", (32 * T, 2), I32), dram("tab_b", (E2 * CAP + K2 * T, 2), I32)
        plan = dram("plan", (1, P), I32)
        with ExitStack() as first:
            def mem1(name, shape, dt=F32):
                return first.enter_context(nc.sbuf_tensor(name, shape, dt))

            running = mem1("running", [P, 32])
            first_layer_attention(nc, cst, X, a["x"], a["ctxT"], a["wkT"], a["b_k"], a["gamma"], a["beta"],
                                  a["gate_kernel"], rows_a, tab_a, running)
            bounds, cols = mem1("bounds", [1, 33], I32), mem1("cols", [1, P], I32)
            table = mem1("table_a", [P, 32 * T // P, 2], I32)
            plan_tiles(nc, cst, running, bounds, cols, plan, sum_a, tab_a, table)
            experts(nc, cst, "e_", rows_a, sum_a, table, a["gu_a"], a["dn_a"], CHUNKS_A, PIECES_A, bounds, cols,
                    97, 15, [30, 31])
        second_attention_all(nc, cst, X, sum_a, a["ctx"], a["cos_k"], a["sin_k"], a["heads"], a["heads_qr"],
                             a["heads_v"], a["cos_q"], a["sin_q"])
        table = mem("table_b", [P, COLS2 + NT + 2 * SUB, 2], I32)
        second_layer_routing(nc, cst, X, a["gate_w"], a["gate_b"], rows_b, tab_b, sum_b, table)
        experts(nc, cst, "f_", rows_b, sum_b, table, a["gu_b"], a["dn_b"], CHUNKS_B, PIECES_B,
                list(range(E2 + 1)) + [TILES2], None, TILES2, E2 // 2, [E2])
        add_and_store(nc, cst, X, sum_b, out)


def rope(np, length, dim):
    inv = (1.0 / 10000.0 ** (np.arange(0, dim, 2, dtype=np.float32) / np.float32(dim))).astype(np.float32)
    f = np.arange(length, dtype=np.float32)[:, None] * inv[None]
    return np.repeat(np.sin(f), 2, -1).astype(np.float32), np.repeat(np.cos(f), 2, -1).astype(np.float32)


def rope_tables(np, order):
    s, c = rope(np, S, Q)
    s, c = s.T[order].reshape(QC, P, S).copy(), c.T[order].reshape(QC, P, S)
    s[0] *= -1
    low = s[2, :P // 2].copy()
    s[2, :P // 2], s[2, P // 2:] = s[2, P // 2:], -low
    sk, ck = rope(np, S, C)
    sk[:, :C // 2] *= -1
    return (np.ascontiguousarray(c.transpose(1, 0, 2)), np.ascontiguousarray(s.transpose(1, 0, 2)),
            np.ascontiguousarray(ck.reshape(SJ, P, C).transpose(1, 0, 2)),
            np.ascontiguousarray(sk.reshape(SJ, P, C).transpose(1, 0, 2)))


def kernel(**inputs):
    import numpy as np
    import concourse.bacc as bacc
    from concourse.bass_utils import run_bass_kernel_spmd as run

    v = {k: np.asarray(a) for k, a in inputs.items()}

    def lay(a):
        return np.ascontiguousarray(a)

    def chunked(a):
        return lay(np.moveaxis(a.reshape(*a.shape[:-2], DC, P, a.shape[-1]), -3, -2))

    h = 192 - P
    order = np.concatenate([np.arange(0, P), np.arange(Q // 2, Q // 2 + P), np.arange(P, Q // 2),
                            np.arange(Q // 2 + P, Q)])
    g, u, d = v["L0_ffn_gate_proj"], v["L0_ffn_up_proj"], v["L0_ffn_down_proj"]
    dn_a = np.zeros((32, P, 2, D), np.float32)
    dn_a[:, :h, 0], dn_a[:, :, 1] = d[:, P:], d[:, :P]
    g1 = np.concatenate([v["L1_ffn_W1"], v["L1_ffn_Ws1"][None]]).transpose(0, 2, 1)
    u1 = np.concatenate([v["L1_ffn_W3"], v["L1_ffn_Ws3"][None]]).transpose(0, 2, 1)
    d1 = np.concatenate([v["L1_ffn_W2"], v["L1_ffn_Ws2"][None]]).transpose(0, 2, 1)
    dn_b = np.zeros((E2 + 1, 3 * P, D), np.float32)
    dn_b[:, :d1.shape[1]] = d1
    wq = v["L1_xattn_Wq"].reshape(H, P, DC, P).transpose(0, 3, 2, 1).reshape(H, P, D)
    wkr = v["L1_xattn_W_kr"]
    wo = v["L1_xattn_Wo"].reshape(D, H, P).transpose(1, 2, 0)
    cos_q, sin_q, cos_k, sin_k = rope_tables(np, order)
    arrays = {
        "x": lay(v["x"].reshape(T, D)),
        "ctx": lay(v["ctx_512"].reshape(T, C)),
        "ctxT": lay(v["ctx_512"].transpose(0, 2, 1)),
        "gates": lay(np.concatenate([v["g_xattn"], v["g_ffn"]])),
        "wkT": lay(v["L0_xattn_W_k"].T),
        "b_k": lay(v["L0_xattn_b_k"]),
        "gamma": lay(v["L0_xattn_ln_gamma"]),
        "beta": lay(v["L0_xattn_ln_beta"]),
        "gate_kernel": chunked(v["L0_ffn_gate_kernel"]),
        "gu_a": chunked(np.concatenate([g[..., P:], u[..., P:], g[..., :P], u[..., :P]], -1)),
        "dn_a": dn_a,
        "heads": lay(np.concatenate([wq, v["L1_xattn_w_kc_q"][..., order], wkr, wkr], 2)),
        "heads_qr": lay(v["L1_xattn_W_qr"][:, order].reshape(H, QC, P, R).transpose(0, 2, 1, 3)),
        "heads_v": lay(np.concatenate([v["L1_xattn_w_kc_kv"], wo], 2)),
        "cos_q": cos_q, "sin_q": sin_q, "cos_k": cos_k, "sin_k": sin_k,
        "gate_w": chunked(v["L1_ffn_gate_w"].T),
        "gate_b": lay(v["L1_ffn_gate_b"]),
        "gu_b": chunked(np.concatenate([m[..., i * P:(i + 1) * P] for i in range(3) for m in (g1, u1)], -1)),
        "dn_b": lay(dn_b.reshape(E2 + 1, 3, P, D).transpose(0, 2, 1, 3)),
    }
    nc = bacc.Bacc("TRN2", target_bir_lowering=False, num_devices=1)
    ins = {k: nc.dram_tensor("in_" + k, a.shape, mybir.dt.from_np(a.dtype), kind="ExternalInput").ap()
           for k, a in arrays.items()}
    out = nc.dram_tensor("out", (T, D), F32, kind="ExternalOutput").ap()
    two_layers(nc, ins, out)
    got = run(nc, [{"in_" + k: a for k, a in arrays.items()}], core_ids=[0])
    return got.results[0]["out"].reshape(B, S, D)
```

```python
from contextlib import ExitStack

import concourse.bass as bass
from concourse import mybir

F32 = mybir.dt.float32
F32R = mybir.dt.float32r
I32 = mybir.dt.int32
U32 = mybir.dt.uint32
ALU = mybir.AluOpType
ACT = mybir.ActivationFunctionType
AX_X = mybir.AxisListType.X
ds = bass.ds

P = 128
B = 4
S = 512
T = B * S
D = 512
DC = D // P
NT = T // P
SJ = S // P
C = 128
LN_EPS = 1e-5
SIM_EPS = 1e-6
SIM_SCALE = 512 ** -0.5

DVE_A = 58

TILE = 256
SUB = TILE // P


passed = []


def until(eng, sem, value):
    eng.wait_ge(sem, value)
    if not isinstance(value, int):
        eng.sem_inc(passed[0], 1)


class Steps:

    def __init__(self, eng, sem, base=0):
        self.eng, self.sem, self.base, self.n = eng, sem, base, 0

    def __call__(self, ins):
        self.n += 1
        return ins.then_inc(self.sem, 1)

    def settle(self):
        until(self.eng, self.sem, self.base + self.n)


def over(ap, axis, n):
    ap = ap.unsqueeze(axis)
    shape = list(ap.shape)
    shape[axis] = n
    return ap.to_broadcast(shape)


def semaphores(nc, ctx, prefix):
    made = []

    def sem(name):
        made.append(nc.alloc_semaphore(name=prefix + name))
        return made[-1]

    def free():
        nc.clear_and_free_semaphores(made)
        nc.all_engine_barrier()

    ctx.callback(free)
    return sem


def constants(nc, mem, sem, g_in):
    ident = mem("ident", [P, P])
    ident_r = mem("ident_r", [P, P], F32R)
    ones = mem("ones", [P, P])
    before = mem("before", [P, P])
    mhalf = mem("mhalf", [P, NT])
    gates = mem("gates", [P, 4])
    tanhg = mem("tanhg", [P, 4])
    gates_in, filled, masked = sem("gates_in"), sem("consts_filled"), sem("consts_masked")
    ready = sem("consts_ready")
    passed[:] = [sem("waits_passed")]
    with nc.Block() as block:
        @block.sync
        def _(sp):
            sp.dma_start(gates[:], g_in.partition_broadcast(P)).then_inc(gates_in, 16)

        @block.gpsimd
        def _(pool):
            pool.memset(ident[:], 0.0).then_inc(filled, 1)
            pool.memset(before[:], 1.0).then_inc(filled, 1)
            pool.wait_ge(filled, 2)
            pool.affine_select(out=ident[:], in_=ident[:], compare_op=ALU.not_equal, fill=1.0, base=0,
                               pattern=[[-1, P]], channel_multiplier=1).then_inc(masked, 1)
            pool.affine_select(out=before[:], in_=before[:], compare_op=ALU.is_gt, fill=0.0, base=0,
                               pattern=[[1, P]], channel_multiplier=-1).then_inc(masked, 1)

        @block.vector
        def _(dve):
            dve.memset(ones[:], 1.0).then_inc(ready, 1)
            dve.memset(mhalf[:], -0.5).then_inc(ready, 1)
            dve.wait_ge(masked, 2)
            dve.tensor_copy(ident_r[:], ident[:]).then_inc(ready, 1)

        @block.scalar
        def _(act):
            act.wait_ge(gates_in, 16)
            act.activation(tanhg[:], gates[:], ACT.Tanh).then_inc(ready, 1)

        @block.tensor
        def _(pe):
            pe.wait_ge(ready, 4)
    return dict(ident=ident, ident_r=ident_r, ones=ones, before=before, mhalf=mhalf, tanhg=tanhg)


def first_layer_attention(nc, cst, X, x_in, ctxT_in, wkT_in, bk_in, gamma_in, beta_in, gk_in, xn_dram, tab_dram,
                          running, accs, weights, K=8, E=32):
    with ExitStack() as ctx:
        def mem(name, shape, dt=F32):
            return ctx.enter_context(nc.sbuf_tensor("a_" + name, shape, dt))

        def bank(name):
            return ctx.enter_context(nc.psum_tensor("a_" + name, [P, 512], F32))

        sem = semaphores(nc, ctx, "a_")

        M = SJ * K
        wkT, brow, bcol = mem("wkT", [P, C]), mem("brow", [P, C]), mem("bcol", [P, 1])
        gamma, beta = mem("gamma", [P, S]), mem("beta", [P, S])
        gk = mem("gk", [P, DC, E])
        ctxT = mem("ctxT", [P, S])
        N1, N2, NT1, NT2 = mem("N1", [P, SJ, D]), mem("N2", [P, SJ, D]), mem("NT1", [P, DC, S]), mem("NT2", [P, DC, S])
        kv, kvT, outT = mem("kv", [P, SJ, C]), mem("kvT", [P, S]), mem("outT", [P, S])
        sim = mem("sim", [P, SJ, S])
        stats, mv = mem("stats", [P, SJ, 6]), mem("mv", [P, SJ, 2])
        mean1, ve1, rstd1, nb1 = (mem(n, [P, NT]) for n in ("mean1", "ve1", "rstd1", "nb1"))
        ve_s, rstd_s, nb_s, ve2, rstd2, nb2 = (mem(n, [P, SJ]) for n in ("ve_s", "rstd_s", "nb_s", "ve2", "rstd2", "nb2"))
        top = mem("top", [P, SJ])
        esum, rsum = mem("esum", [P, SJ]), mem("rsum", [P, SJ])
        logit8, idx8 = mem("logit8", [P, SJ, 8]), mem("idx8", [P, SJ, 8], U32)
        lg = mem("lg", [P, SJ, E])
        w8, wsum = mem("w8", [P, SJ, 8]), mem("wsum", [P, SJ])
        idxf = mem("idxf", [P, M])
        iota_e, e16 = mem("iota_e", [P, E], I32), mem("e16", [P, SJ, E], I32)
        iota_ef = mem("iota_ef", [P, E])
        hot = mem("hot", [P, M, E])
        mask, pref = mem("mask", [P, SJ, E]), mem("pref", [P, SJ, E])
        pos_i, low = mem("pos_i", [P, SJ * E], I32), mem("low", [P, SJ * E], I32)
        addr = mem("addr", [P, SJ, E])
        slot_f, slot = mem("slot_f", [P, M]), mem("slot", [P, M], I32)
        ids = mem("ids", [P, SJ, K], I32)
        entry = mem("entry", [P, SJ, K, 2], I32)
        init, zeros = mem("init", [P, P * 4, 2], I32), mem("zeros", [P, D])

        tr = [bank("tr0"), bank("tr1")]
        kvp, kvTp = bank("kvp"), bank("kvTp")
        simp = [bank(f"simp{j}") for j in range(SJ)]
        outp, rt, posp = tr[0], kvp, kvTp

        consts_in, ctx_in = sem("consts_in"), sem("ctx_in")
        x_in_s = [sem(f"x_in{b}") for b in range(B)]
        dve_s, dve_pre, dve_post = sem("dve"), sem("dve_setup"), sem("dve_moments")
        var1_r, rstd1_r, nb1_r = sem("var_x"), sem("rstd_x"), sem("nbias_x")
        var_s_r, rstd_s_r, nb_s_r = sem("var_sim"), sem("rstd_sim"), sem("nbias_sim")
        var2_r, rstd2_r, nb2_r = sem("var_new"), sem("rstd_new"), sem("nbias_new")
        n1_r, t1_r, k1_r = sem("rows_normal"), sem("transposed"), sem("chunks_kept")
        n2_r, t2_r, k2_r = sem("new_rows_normal"), sem("new_transposed"), sem("new_chunks_kept")
        kvp_r, kv_r, kvTp_r, kvT_r = sem("kv_made"), sem("kv_kept"), sem("kvT_made"), sem("kvT_kept")
        outp_r, outT_r, simp_r = sem("out_made"), sem("out_kept"), sem("sim_made")
        sn_r, sg_r, top_r, e_r = sem("sim_normal"), sem("sim_scaled"), sem("top_ready"), sem("exp_ready")
        x_r = sem("x_updated")
        lg_r, lgk_r, d8_r, w8_r = sem("logits_made"), sem("logits_kept"), sem("logit8_shifted"), sem("exp8_ready")
        mask_r, pos_r, posk_r, route_r = sem("mask_ready"), sem("pos_made"), sem("pos_kept"), sem("route_ready")
        rows_out, tab_init, tab_out, iota_r = sem("rows_out"), sem("tab_init"), cst["a_table_out"], sem("iota")
        init_r, zeros_r, cleared = sem("init_ready"), sem("zeros"), sem("cleared")

        xv = x_in.rearrange("(b j p) d -> b p j d", p=P, j=SJ)
        xnv = xn_dram[0:T, :].rearrange("(b j p) d -> b p j d", p=P, j=SJ)
        x0v = accs[0][0:T, :].rearrange("(b j p) d -> b p j d", p=P, j=SJ)
        ident = cst["ident"]

        def sequences(eng, body):
            with eng.Fori(0, B - 1) as b:
                body(b, True)
            body(B - 1, False)

        with nc.Block() as block:
            @block.sync
            def _(sp):
                def context(b):
                    sp.dma_start(ctxT[:], ctxT_in[ds(b, 1)].rearrange("a d l -> (a d) l")).then_inc(ctx_in, 16)

                sp.dma_start(X[:, 0:SJ, :], xv[0]).then_inc(x_in_s[0], 16)
                sp.dma_start(wkT[:], wkT_in).then_inc(consts_in, 16)
                sp.dma_start(brow[:], bk_in.partition_broadcast(P)).then_inc(consts_in, 16)
                sp.dma_start(bcol[:], bk_in.rearrange("(d a) -> d a", a=1)).then_inc(consts_in, 16)
                sp.dma_start(gamma[:], gamma_in.partition_broadcast(P)).then_inc(consts_in, 16)
                sp.dma_start(beta[:], beta_in.partition_broadcast(P)).then_inc(consts_in, 16)
                sp.dma_start(gk[:], gk_in).then_inc(consts_in, 16)
                context(0)
                for b in range(1, B):
                    sp.dma_start(X[:, SJ * b:SJ * (b + 1), :], xv[b]).then_inc(x_in_s[b], 16)
                sp.wait_ge(init_r, 2)
                sp.dma_start(tab_dram[0:E * T, :].rearrange("(p c) w -> p (c w)", p=P),
                             init[:].rearrange("p c w -> p (c w)")).then_inc(tab_init, 16)
                sp.wait_ge(zeros_r, 1)
                sp.dma_start(xn_dram[T:T + P, :], zeros[:]).then_inc(tab_init, 16)

                def step(b, more):
                    if more:
                        until(sp, kvTp_r, b + 1)
                        until(sp, kvp_r, b + 1)
                        context(b + 1)
                    for j in range(SJ):
                        sp.dma_start(accs[1][0:T, :].rearrange("(n p) d -> n p d", p=P)[ds(SJ * b + j, 1)].rearrange(
                            "a p d -> (a p) d"), zeros[:]).then_inc(cleared, 16)
                    until(sp, x_r, SJ * b + SJ)
                    sp.dma_start(x0v[ds(b, 1)].rearrange("a p j d -> (a p) j d"), X[:, ds(SJ * b, SJ), :]).then_inc(
                        cleared, 16)
                    until(sp, n2_r, SJ * b + SJ)
                    sp.dma_start(xnv[ds(b, 1)].rearrange("a p j d -> (a p) j d"), N2[:]).then_inc(rows_out, 16)

                sequences(sp, step)
                for e in (0, 1):
                    weights.load(sp, e, e)
                for rows in accs:
                    sp.dma_start(rows[T:T + P, :], zeros[:]).then_inc(cleared, 16)
                sp.wait_ge(rows_out, 16 * B)
                sp.wait_ge(tab_init, 32)
                sp.wait_ge(cleared, 16 * (NT + B + len(accs)))

            @block.scalar
            def _(act):
                act.wait_ge(consts_in, 96)

                def row(b, j):
                    return X[:, ds(SJ * b + j, 1), :].rearrange("p a d -> p (a d)")

                def rows1(b):
                    until(act, t1_r, DC * b)
                    for j in range(SJ):
                        tile = ds(SJ * b + j, 1)
                        act.activation(N1[:, j, :], row(b, j), ACT.Identity, bias=nb1[:, tile],
                                       scale=rstd1[:, tile]).then_inc(n1_r, 1)

                def keys(b):
                    until(act, kvTp_r, b + 1)
                    act.activation(kvT[:], kvTp[:], ACT.Identity, bias=bcol[:, 0:1]).then_inc(kvT_r, 1)

                def keep1(b):
                    until(act, outp_r, b)
                    for c in range(DC):
                        until(act, t1_r, DC * b + c + 1)
                        act.activation(NT1[:, c, :], tr[c % 2][:], ACT.Copy).then_inc(k1_r, 1)

                def keep_out(b):
                    until(act, outp_r, b + 1)
                    act.activation(outT[:], outp[:], ACT.Copy).then_inc(outT_r, 1)

                def normal_sim(b):
                    until(act, nb_s_r, b + 1)
                    until(act, x_r, SJ * b)
                    for j in range(SJ):
                        act.activation(sim[:, j, :], simp[j][:], ACT.Identity, bias=nb_s[:, j:j + 1],
                                       scale=rstd_s[:, j:j + 1]).then_inc(sn_r, 1)

                act.wait_ge(nb1_r, 1)
                rows1(0)
                keys(0)
                keep1(0)
                keep_out(0)
                normal_sim(0)
                act.wait_ge(nb1_r, 2)

                def step(b, more):
                    if more:
                        rows1(b + 1)
                        keys(b + 1)
                    for j in range(SJ):
                        until(act, top_r, SJ * b + j + 1)
                        act.activation(sim[:, j, :], sim[:, j, :], ACT.Exp, bias=top[:, j:j + 1],
                                       accum_out=esum[:, j:j + 1]).then_inc(e_r, 1)
                    if more:
                        keep1(b + 1)
                        keep_out(b + 1)
                    until(act, nb2_r, b + 1)
                    until(act, rows_out, 16 * b)
                    until(act, t2_r, DC * b)
                    for j in range(SJ):
                        act.activation(N2[:, j, :], row(b, j), ACT.Identity, bias=nb2[:, j:j + 1],
                                       scale=rstd2[:, j:j + 1]).then_inc(n2_r, 1)
                    until(act, lg_r, b)
                    for c in range(DC):
                        until(act, t2_r, DC * b + c + 1)
                        act.activation(NT2[:, c, :], tr[c % 2][:], ACT.Copy).then_inc(k2_r, 1)
                    if more:
                        normal_sim(b + 1)
                    until(act, d8_r, b + 1)
                    act.activation(w8[:], w8[:], ACT.Exp).then_inc(w8_r, 1)

                sequences(act, step)

            @block.gpsimd
            def _(pool):
                pool.iota(iota_e[:], [[1, E]], base=0, channel_multiplier=0).then_inc(iota_r, 1)
                pool.iota(e16[:], [[0, SJ], [T // P, E]], base=0, channel_multiplier=0).then_inc(iota_r, 1)
                pool.iota(ids[:], [[P, SJ], [0, K]], base=0, channel_multiplier=1).then_inc(iota_r, 1)
                pool.iota(init[:, :, 0], [[0, P * 4]], base=T, channel_multiplier=1).then_inc(init_r, 1)
                pool.memset(init[:, :, 1], 0).then_inc(init_r, 1)

                def power(out, base, made, ready, n):
                    until(pool, made, n)
                    pool.tensor_tensor(out, base, cst["mhalf"][:, 0:out.shape[1]], ALU.pow).then_inc(ready, 1)

                def scatter(b, some):
                    until(pool, route_r, b + 1)
                    for m in some:
                        j, k = divmod(m, K)
                        pool.indirect_dma_start(
                            out=tab_dram, out_offset=bass.IndirectOffsetOnAxis(ap=slot[:, m:m + 1], axis=0),
                            in_=entry[:, j, k, :], in_offset=None).then_inc(tab_out, 16)

                def gammas(b):
                    for j in range(SJ):
                        until(pool, sn_r, SJ * b + j + 1)
                        pool.tensor_tensor(sim[:, j, :], sim[:, j, :], gamma[:], ALU.mult).then_inc(sg_r, 1)

                power(rstd1[:, 0:SJ], ve1[:, 0:SJ], var1_r, rstd1_r, 1)
                power(rstd1[:, SJ:NT], ve1[:, SJ:NT], var1_r, rstd1_r, 2)
                def power_s(b):
                    power(rstd_s[:], ve_s[:], var_s_r, rstd_s_r, b + 1)

                def power2(b):
                    power(rstd2[:], ve2[:], var2_r, rstd2_r, b + 1)

                power_s(0)
                gammas(0)
                power2(0)
                power_s(1)
                gammas(1)
                pool.wait_ge(tab_init, 32)
                with pool.Fori(1, B - 1) as b:
                    scatter(b - 1, range(0, 13))
                    power2(b)
                    scatter(b - 1, range(13, 15))
                    power_s(b + 1)
                    scatter(b - 1, range(15, 24))
                    gammas(b + 1)
                    scatter(b - 1, range(24, M))
                scatter(B - 2, range(0, 13))
                power2(B - 1)
                scatter(B - 2, range(13, M))
                scatter(B - 1, range(M))
                pool.wait_ge(tab_out, 16 * M * B)

            @block.tensor
            def _(pe):
                pe.wait_ge(consts_in, 96)

                def front(b):
                    until(pe, ctx_in, 16 * b + 16)
                    for j in range(SJ):
                        mm = pe.matmul(kvp[:, j * C:(j + 1) * C], ctxT[:, j * P:(j + 1) * P], wkT[:],
                                       start=True, stop=True)
                    mm.then_inc(kvp_r, 1)
                    pe.matmul(kvTp[:], wkT[:], ctxT[:], start=True, stop=True).then_inc(kvTp_r, 1)
                    until(pe, n1_r, SJ * b + SJ)
                    for c in range(DC):
                        if c >= 2:
                            until(pe, k1_r, DC * b + c - 1)
                        for j in range(SJ):
                            mm = pe.transpose(tr[c % 2][:, j * P:(j + 1) * P], N1[:, j, c * P:(c + 1) * P], ident[:])
                        mm.then_inc(t1_r, 1)
                    until(pe, kv_r, b + 1)
                    until(pe, k1_r, DC * b + DC)
                    for c in range(DC):
                        mm = pe.matmul(outp[:], kv[:, c, :], NT1[:, c, :], start=(c == 0), stop=(c == DC - 1))
                    mm.then_inc(outp_r, 1)

                def similarity(b):
                    until(pe, outT_r, b + 1)
                    until(pe, kvT_r, b + 1)
                    until(pe, sn_r, SJ * b)
                    for j in range(SJ):
                        pe.matmul(simp[j][:], outT[:, j * P:(j + 1) * P], kvT[:], start=True,
                                  stop=True).then_inc(simp_r, 1)

                def step(b, more):
                    if more:
                        front(b + 1)
                        similarity(b + 1)
                    until(pe, n2_r, SJ * b + SJ)
                    for c in range(DC):
                        if c >= 2:
                            until(pe, k2_r, DC * b + c - 1)
                        for j in range(SJ):
                            mm = pe.transpose(tr[c % 2][:, j * P:(j + 1) * P], N2[:, j, c * P:(c + 1) * P], ident[:])
                        mm.then_inc(t2_r, 1)
                    until(pe, k2_r, DC * b + DC)
                    for j in range(SJ):
                        for c in range(DC):
                            mm = pe.matmul(rt[:, j * E:(j + 1) * E], NT2[:, c, j * P:(j + 1) * P], gk[:, c, :],
                                           start=(c == 0), stop=(c == DC - 1))
                    mm.then_inc(lg_r, 1)
                    until(pe, mask_r, b + 1)
                    pe.matmul(posp[:, 0:SJ * E], cst["before"][:], mask[:].rearrange("p j e -> p (j e)"),
                              start=True, stop=False)
                    pe.matmul(posp[:, 0:SJ * E], cst["ones"][:], pref[:].rearrange("p j e -> p (j e)"),
                              start=False, stop=True).then_inc(pos_r, 1)
                    until(pe, posk_r, b + 1)

                front(0)
                similarity(0)
                sequences(pe, step)

            @block.vector
            def _(dve):
                pre = Steps(dve, dve_pre)
                dve.memset(zeros[:], 0.0).then_inc(zeros_r, 1)
                pre(dve.memset(running[:], 0.0))
                dve.wait_ge(iota_r, 3)
                pre(dve.tensor_copy(iota_ef[:], iota_e[:]))
                pre.settle()
                dve.wait_ge(consts_in, 96)

                def moments(step, src):
                    for j in range(SJ):
                        step(dve.bn_stats(stats[:, j, :], src(j)))
                    step.settle()
                    for j in range(SJ):
                        step(dve.bn_aggr(mv[:, j, :], stats[:, j, :]))
                    step.settle()

                def moments1(b):
                    dve.wait_ge(x_in_s[b], 16)
                    moments(pre, lambda j: X[:, SJ * b + j, :])
                    tiles = slice(SJ * b, SJ * (b + 1))
                    pre(dve.tensor_copy(mean1[:, tiles], mv[:, :, 0]))
                    return dve.tensor_scalar(ve1[:, tiles], mv[:, :, 1], LN_EPS, None, ALU.add)

                def nbias1(n, tiles):
                    dve.wait_ge(rstd1_r, n)
                    dve.scalar_tensor_tensor(nb1[:, tiles], mean1[:, tiles], -1.0, rstd1[:, tiles], ALU.mult,
                                             ALU.mult).then_inc(nb1_r, 1)

                def keys(b):
                    until(dve, kvp_r, b + 1)
                    until(dve, outp_r, b)
                    dve.tensor_tensor(kv[:], kvp[:].rearrange("p (j c) -> p j c", c=C), over(brow[:], 1, SJ),
                                      ALU.add).then_inc(kv_r, 1)

                def row(b, j):
                    return X[:, ds(SJ * b + j, 1), :].rearrange("p a d -> p (a d)")

                moments1(0).then_inc(var1_r, 1)
                pre.settle()
                nbias1(1, slice(0, SJ))
                keys(0)
                for b in range(1, B):
                    last = moments1(b)
                    if b < B - 1:
                        pre(last)
                        pre.settle()
                pre.settle()
                last.then_inc(var1_r, 1)
                nbias1(2, slice(SJ, NT))

                def moments_sim(step, b):
                    for j in range(SJ):
                        until(dve, simp_r, SJ * b + j + 1)
                        step(dve.bn_stats(stats[:, j, :], simp[j][:]))
                    step.settle()
                    for j in range(SJ):
                        step(dve.bn_aggr(mv[:, j, :], stats[:, j, :]))
                    step.settle()
                    dve.tensor_scalar(ve_s[:], mv[:, :, 1], SIM_SCALE ** 2, SIM_EPS, ALU.mult, ALU.add).then_inc(var_s_r, 1)
                    until(dve, rstd_s_r, b + 1)
                    step(dve.tensor_scalar(rstd_s[:], rstd_s[:], SIM_SCALE, None, ALU.mult))
                    step.settle()
                    dve.scalar_tensor_tensor(nb_s[:], mv[:, :, 0], -1.0, rstd_s[:], ALU.mult,
                                             ALU.mult).then_inc(nb_s_r, 1)

                moments_sim(pre, 0)

                def step(b, more):
                    step = Steps(dve, dve_s, b * DVE_A)
                    if more:
                        keys(b + 1)
                    for j in range(SJ):
                        until(dve, sg_r, SJ * b + j + 1)
                        step(dve.tensor_tensor_reduce(sim[:, j, :], sim[:, j, :], beta[:], 1.0, -3.0e38, ALU.add,
                                                      ALU.max, top[:, j:j + 1]))
                        step.settle()
                        dve.tensor_scalar(top[:, j:j + 1], top[:, j:j + 1], -1.0, None, ALU.mult).then_inc(top_r, 1)
                    for j in range(SJ):
                        until(dve, e_r, SJ * b + j + 1)
                        step(dve.reciprocal(rsum[:, j:j + 1], esum[:, j:j + 1]))
                        step.settle()
                        step(dve.tensor_scalar(rsum[:, j:j + 1], rsum[:, j:j + 1], cst["tanhg"][:, 0:1], None,
                                               ALU.mult))
                        step.settle()
                        dve.scalar_tensor_tensor(row(b, j), sim[:, j, :], rsum[:, j:j + 1], row(b, j), ALU.mult,
                                                 ALU.add).then_inc(x_r, 1)
                    until(dve, x_r, SJ * b + SJ)
                    moments(step, lambda j: row(b, j))
                    dve.tensor_scalar(ve2[:], mv[:, :, 1], LN_EPS, None, ALU.add).then_inc(var2_r, 1)
                    until(dve, rstd2_r, b + 1)
                    dve.scalar_tensor_tensor(nb2[:], mv[:, :, 0], -1.0, rstd2[:], ALU.mult, ALU.mult).then_inc(nb2_r, 1)
                    if more:
                        moments_sim(step, b + 1)

                    until(dve, lg_r, b + 1)
                    dve.tensor_copy(lg[:], rt[:, 0:SJ * E].rearrange("p (j e) -> p j e", e=E)).then_inc(lgk_r, 1)
                    until(dve, lgk_r, b + 1)
                    for j in range(SJ):
                        step(dve.max(logit8[:, j, :], lg[:, j, :]))
                    step.settle()
                    for j in range(SJ):
                        step(dve.max_index(idx8[:, j, :], logit8[:, j, :], lg[:, j, :]))
                    dve.tensor_tensor(w8[:], logit8[:], logit8[:, :, 0:1].to_broadcast([P, SJ, 8]),
                                      ALU.subtract).then_inc(d8_r, 1)
                    step.settle()
                    step(dve.tensor_copy(idxf[:], idx8[:].rearrange("p j k -> p (j k)")))
                    step.settle()
                    step(dve.tensor_tensor(hot[:], over(idxf[:], 2, E), over(iota_ef[:], 1, M), ALU.is_equal))
                    step.settle()
                    step(dve.tensor_reduce(mask[:], hot[:].rearrange("p (j k) e -> p j e k", k=K), AX_X, ALU.add))
                    step(dve.tensor_copy(pref[:, 0, :], running[:]))
                    step.settle()
                    for j in range(SJ):
                        nxt = pref[:, j + 1, :] if j + 1 < SJ else running[:]
                        step(dve.tensor_tensor(nxt, pref[:, j, :], mask[:, j, :], ALU.add))
                        step.settle()
                    dve.engine_nop().then_inc(mask_r, 1)
                    until(dve, w8_r, b + 1)
                    step(dve.tensor_reduce(wsum[:], w8[:], AX_X, ALU.add))
                    step.settle()
                    step(dve.reciprocal(wsum[:], wsum[:]))
                    step.settle()
                    step(dve.tensor_scalar(wsum[:], wsum[:], cst["tanhg"][:, 2:3], None, ALU.mult))
                    step.settle()
                    until(dve, tab_out, 16 * M * b)
                    step(dve.tensor_tensor(entry[:, :, :, 1].bitcast(F32), w8[:], over(wsum[:], 2, 8), ALU.mult))
                    step(dve.tensor_copy(entry[:, :, :, 0], ids[:]))
                    step.settle()
                    step(dve.tensor_scalar(ids[:], ids[:], float(S), None, ALU.add))
                    until(dve, pos_r, b + 1)
                    dve.tensor_copy(pos_i[:], posp[:, 0:SJ * E]).then_inc(posk_r, 1)
                    until(dve, posk_r, b + 1)
                    step(dve.tensor_scalar(low[:], pos_i[:], P - 1, (E * T // P).bit_length() - 1, ALU.bitwise_and,
                                           ALU.logical_shift_left))
                    step(dve.tensor_scalar(pos_i[:], pos_i[:], 7, None, ALU.logical_shift_right))
                    step.settle()
                    step(dve.tensor_tensor(low[:], low[:], pos_i[:], ALU.add))
                    step.settle()
                    step(dve.tensor_tensor(addr[:].rearrange("p j e -> p (j e)"), low[:],
                                           e16[:].rearrange("p j e -> p (j e)"), ALU.add))
                    step.settle()
                    hot4 = hot[:].rearrange("p (j k) e -> p j k e", k=K)
                    step(dve.tensor_tensor(hot4, hot4, over(addr[:], 2, K), ALU.mult))
                    step.settle()
                    step(dve.tensor_reduce(slot_f[:], hot[:], AX_X, ALU.add))
                    step.settle()
                    step(dve.tensor_copy(slot[:], slot_f[:]))
                    step.settle()
                    dve.engine_nop().then_inc(route_r, 1)
                    assert step.n == DVE_A or not more, step.n

                sequences(dve, step)


def plan_tiles(nc, cst, running, bounds, cols, plan_dram, tab_dram, table, E=32):
    with ExitStack() as ctx:
        def mem(name, shape, dt=F32):
            return ctx.enter_context(nc.sbuf_tensor("p_" + name, shape, dt))

        sem = semaphores(nc, ctx, "p_")

        count, tiles, ntile = mem("count", [P, E], I32), mem("tiles", [P, E], I32), mem("ntile", [P, E])
        upto = mem("upto", [P, E + 1])
        upto_i = mem("upto_i", [P, E + 1], I32)
        tile_i, tile_f = mem("tile_i", [P, 1], I32), mem("tile_f", [P, 1])
        past, pastn = mem("past", [P, E]), mem("pastn", [P, E])
        expert, first, col = mem("expert", [P, 1]), mem("first", [P, 1]), mem("col", [P, 1])
        col_i = mem("col_i", [P, 1], I32)
        total = ctx.enter_context(nc.psum_tensor("p_total", [P, E], F32))
        dve_s, total_r, iota_r, plan_r, moved, tab_in = (sem(n) for n in (
            "dve", "total", "iota", "plan_ready", "moved", "tab_in"))
        with nc.Block() as block:
            @block.gpsimd
            def _(pool):
                pool.iota(tile_i[:], [[0, 1]], base=0, channel_multiplier=1).then_inc(iota_r, 1)

            @block.tensor
            def _(pe):
                pe.matmul(total[:], cst["ones"][:], running[:], start=True, stop=True).then_inc(total_r, 1)

            @block.vector
            def _(dve):
                step = Steps(dve, dve_s)
                dve.wait_ge(total_r, 1)
                step(dve.tensor_copy(count[:], total[:]))
                step.settle()
                step(dve.tensor_scalar(count[:], count[:], TILE - 1, None, ALU.add))
                step.settle()
                step(dve.tensor_scalar(tiles[:], count[:], TILE.bit_length() - 1, None, ALU.logical_shift_right))
                step.settle()
                step(dve.tensor_scalar(ntile[:], tiles[:], 1.0, None, ALU.max))
                step(dve.memset(upto[:, 0:1], 0.0))
                step.settle()
                step(dve.tensor_tensor_scan(upto[:, 1:E + 1], cst["ones"][:, 0:E], ntile[:], 0.0, ALU.mult, ALU.add))
                step.settle()
                step(dve.tensor_copy(upto_i[:], upto[:]))
                dve.wait_ge(iota_r, 1)
                step(dve.tensor_copy(tile_f[:], tile_i[:]))
                step.settle()
                step(dve.tensor_scalar(past[:], upto[:, 1:E + 1], tile_f[:, 0:1], None, ALU.is_le))
                step(dve.tensor_copy(bounds[:], upto_i[0:1, :]))
                step.settle()
                step(dve.tensor_reduce(expert[:], past[:], AX_X, ALU.add))
                step(dve.tensor_tensor(pastn[:], past[:], ntile[:], ALU.mult))
                step.settle()
                step(dve.tensor_reduce(first[:], pastn[:], AX_X, ALU.add))
                step.settle()
                step(dve.tensor_tensor(first[:], tile_f[:], first[:], ALU.subtract))
                step(dve.tensor_scalar(expert[:], expert[:], float(T // P), None, ALU.mult))
                step.settle()
                step(dve.scalar_tensor_tensor(col[:], first[:], float(SUB), expert[:], ALU.mult, ALU.add))
                step.settle()
                step(dve.tensor_scalar(col_i[:], col[:], float(E * T // P - SUB), None, ALU.min))
                step.settle()
                dve.engine_nop().then_inc(plan_r, 1)

            @block.sync
            def _(sp):
                sp.dma_start(table[:], tab_dram.rearrange("(p c) w -> p c w", p=P)).then_inc(tab_in, 16)
                sp.wait_ge(plan_r, 1)
                sp.dma_start(plan_dram.rearrange("a g -> g a"), col_i[:]).then_inc(moved, 16)
                sp.wait_ge(moved, 16)
                sp.dma_start(cols[:], plan_dram).then_inc(moved, 16)
                sp.wait_ge(moved, 32)
                sp.wait_ge(tab_in, 16)


class Weights:

    def __init__(self, mem, sem, name, gu_in, dn_in):
        self.gu_in, self.dn_in = gu_in, dn_in
        self.raw_gu = [mem(f"{name}raw_gu{i}", list(gu_in.shape[1:])) for i in (0, 1)]
        self.raw_dn = [mem(f"{name}raw_dn{i}", list(dn_in.shape[1:])) for i in (0, 1)]
        self.gu_s = [sem(f"{name}gu_in{i}") for i in (0, 1)]
        self.dn_s = [sem(f"{name}dn_in{i}") for i in (0, 1)]

    def load(self, sp, e, parity):
        sp.dma_start(self.raw_gu[parity][:],
                     self.gu_in[ds(e, 1)].rearrange("a p c w -> (a p) c w")).then_inc(self.gu_s[parity], 16)
        sp.dma_start(self.raw_dn[parity][:],
                     self.dn_in[ds(e, 1)].rearrange("a p q d -> (a p) q d")).then_inc(self.dn_s[parity], 16)


def experts(nc, cst, name, xn_dram, accs, table, weights, chunks, pieces, bounds, cols, n_tiles, head, pairs, tail,
            late=None):
    with ExitStack() as ctx:
        def mem(nm, shape, dt=F32):
            return ctx.enter_context(nc.sbuf_tensor(name + nm, shape, dt))

        def bank(nm, dt=F32):
            return ctx.enter_context(nc.psum_tensor(name + nm, [P, 512], dt))

        sem = semaphores(nc, ctx, name)

        W, NQ, NC = chunks[-1][0] + chunks[-1][1], len(pieces), len(chunks)
        raw_gu, raw_dn, gu_s, dn_s = weights.raw_gu, weights.raw_dn, weights.gu_s, weights.dn_s
        gu_hi = [mem(f"gu_hi{i}", [P, DC, W], F32R) for i in (0, 1)]
        gu_lo = [mem(f"gu_lo{i}", [P, DC, W], F32R) for i in (0, 1)]
        dn_hi = [mem(f"dn_hi{i}", [P, NQ, D], F32R) for i in (0, 1)]
        dn_lo = [mem(f"dn_lo{i}", [P, NQ, D], F32R) for i in (0, 1)]
        x = mem("x", [P, SUB, D], F32R)
        x_hi, x_lo = mem("x_hi", [P, DC, TILE], F32R), mem("x_lo", [P, DC, TILE], F32R)
        sg, h = mem("sg", [P, NQ, TILE]), mem("h", [P, NQ, TILE])
        h_hi, h_lo = mem("h_hi", [P, NQ, TILE], F32R), mem("h_lo", [P, NQ, TILE], F32R)
        y, warm = mem("y", [P, SUB, D]), mem("warm", [1, 1])
        gidx, sidx = mem("gidx", [P, SUB], I32), mem("sidx", [P, SUB], I32)
        idx, sw = mem("idx", [P, (n_tiles + 2) * SUB], I32), mem("sw", [P, (n_tiles + 2) * SUB])
        gup = [bank(f"gu{i}") for i in range(4)]
        trp = [bank(f"tr{i}", F32R) for i in range(2)]
        dnp = [bank(f"dn{i}") for i in range(SUB)]
        hi_r, gulo_r, dnlo_r = sem("weights_hi"), sem("gu_lo"), sem("dn_lo")
        idx_r, x_in, tr_r = sem("indices"), cst[name + "rows_in"], sem("transposed")
        xhi_r, xlo_r = sem("x_hi"), sem("x_lo")
        chunk_r, sg_r, h_r, hs_r = sem("chunk_made"), sem("silu_made"), sem("h_made"), sem("h_split")
        dn_r, y_r = sem("down_made"), sem("y_ready")
        sidx_r, added = sem("sidx"), [cst[f"{name}rows_added{s}"] for s in range(SUB)]
        dve_s = sem("dve")
        dynamic = not isinstance(bounds, list)
        late_in = sem("table_in")
        spread = not dynamic

        def borders(eng, e, n):
            if dynamic:
                return [eng.value_load(bounds[0:1, ds(e + k, 1)], min_val=0 if k == 0 else 1,
                                       max_val=n_tiles - 1 if k == 0 else n_tiles) for k in range(n + 1)]
            at = bounds[len(head)] - len(head)
            return [bounds[e + k] if isinstance(e, int) else e + at + k for k in range(n + 1)]

        def each_expert(eng, body):
            n = len(head)
            for e in head:
                body(e, e, False, e, *borders(eng, e, 1))
            with eng.Fori(0, pairs) as i:
                at = borders(eng, 2 * i + n, 2)
                body(2 * i + n, n, False, i, at[0], at[1])
                body(2 * i + 1 + n, 1 - n, False, i + n, at[1], at[2])
            at = borders(eng, tail[0], len(tail))
            for k, e in enumerate(tail):
                body(e, e % 2, e == tail[-1], e // 2, at[k], at[k + 1])

        def each_tile(eng, first, end, body):
            body(first, True)
            if dynamic or isinstance(first, int) and end > first + 1:
                with eng.Fori(first + 1, end) as g:
                    body(g, False)

        with nc.Block() as block:
            @block.sync
            def _(sp):
                def expert(e, parity, last, half, first, end):
                    if not isinstance(e, int) or e + 2 <= tail[-1]:
                        until(sp, gulo_r, 2 * e + 2)
                        until(sp, dnlo_r, e + 1)
                        weights.load(sp, e + 2, parity)

                if late is not None:
                    slot, entry, tab_dram, before = late
                    rows = (table.shape[1] - before - 2 * SUB) * P
                    sp.wait_ge(cst["b_table_out"], 16 * slot.shape[1])
                    sp.dma_start(table[:, before:before + rows // P, :],
                                 tab_dram[0:rows, :].rearrange("(p c) w -> p c w", p=P)).then_inc(late_in, 16)
                each_expert(sp, expert)

            @block.gpsimd
            def _(pool):
                def column(g):
                    if dynamic:
                        return pool.value_load(cols[0:1, ds(g, 1)], min_val=0, max_val=table.shape[1] - SUB)
                    return g * SUB

                def gather(g, c):
                    pool.tensor_copy(idx[:, ds(SUB * g, SUB)], table[:, ds(c, SUB), 0]).then_inc(idx_r, 1)
                    pool.tensor_copy(sw[:, ds(SUB * g, SUB)], table[:, ds(c, SUB), 1].bitcast(F32)).then_inc(idx_r, 1)
                    pool.tensor_copy(gidx[:], table[:, ds(c, SUB), 0]).then_inc(idx_r, 1)
                    until(pool, idx_r, 3 * g + 3)
                    for s in range(SUB):
                        pool.indirect_dma_start(
                            out=x[:, s, :].bitcast(F32), out_offset=None, in_=xn_dram,
                            in_offset=bass.IndirectOffsetOnAxis(ap=gidx[:, s:s + 1], axis=0)).then_inc(x_in, 16)

                gather(0, column(0))
                pool.wait_ge(tr_r, 1)
                gather(1, column(1))

                end = n_tiles if not dynamic else borders(pool, tail[-1], 1)[1]
                def scatter(some):
                    for m in some:
                        pool.indirect_dma_start(
                            out=late[2], out_offset=bass.IndirectOffsetOnAxis(ap=late[0][:, m:m + 1], axis=0),
                            in_=late[1][:, m // K2, m % K2, :], in_offset=None).then_inc(cst["b_table_out"], 16)

                def tile(g, entries=()):
                    until(pool, tr_r, g + 2)
                    gather(g + 2, column(g + 2))
                    for s in range(SUB):
                        until(pool, added[s], 16 * g)
                    pool.tensor_copy(sidx[:], idx[:, ds(SUB * g, SUB)]).then_inc(sidx_r, 1)
                    until(pool, sidx_r, g + 1)
                    for s in range(SUB):
                        until(pool, y_r, SUB * g + s + 1)
                        if s > 0:
                            scatter(entries[:3])
                        if s > 0 and accs[s] is accs[s - 1]:
                            until(pool, added[s - 1], 16 * g + 16)
                        pool.indirect_dma_start(
                            out=accs[s], out_offset=bass.IndirectOffsetOnAxis(ap=sidx[:, s:s + 1], axis=0),
                            in_=y[:, s, :], in_offset=None, compute_op=ALU.add).then_inc(added[s], 16)

                began = 0
                if late is not None:
                    M = late[0].shape[1]
                    began = late[3] // SUB - 2
                    for g in range(began):
                        entries = range(M * g // (began - 1), min(M, M * (g + 1) // (began - 1)))
                        tile(g, entries)
                        scatter(entries[3:])
                    pool.wait_ge(late_in, 16)
                with pool.Fori(began, end) as g:
                    tile(g)
                until(pool, x_in, 16 * SUB * (end + 2))
                for s in range(SUB):
                    until(pool, added[s], 16 * end)

            @block.scalar
            def _(act):
                def split_part(e, parity, half, part):
                    until(act, (gu_s if part < 2 else dn_s)[parity], 16 * half + 16)
                    if part < 2:
                        cs = slice(part * DC // 2, (part + 1) * DC // 2)
                        act.activation(gu_hi[parity][:, cs, :], raw_gu[parity][:, cs, :], ACT.Copy).then_inc(hi_r, 1)
                    else:
                        act.activation(dn_hi[parity][:], raw_dn[parity][:], ACT.Copy).then_inc(hi_r, 1)

                def keep_x(g):
                    until(act, tr_r, g + 1)
                    until(act, chunk_r, NC * g)
                    for i in (0, 1):
                        act.activation(x_hi[:, 2 * i:2 * i + 2, :], trp[i][:].bitcast(F32), ACT.Copy).then_inc(xhi_r, 1)

                def tile(g, split):
                    parts = [0, 1, 2] if split is not None else []
                    if parts:
                        until(act, dn_r, SUB * g)
                    for q, (rows, gc, gp, uc, up) in enumerate(pieces):
                        if parts and q < NQ - 1 and spread:
                            split_part(*split, parts.pop(0))
                        until(act, chunk_r, NC * g + gc + 1)
                        act.activation(sg[up:up + rows, q, :], gup[chunks[gc][2]][gp:gp + rows, 0:TILE],
                                       ACT.Silu).then_inc(sg_r, 1)
                    keep_x(g + 1)
                    for part in parts:
                        split_part(*split, part)
                    until(act, idx_r, 3 * g + 3)
                    for s in range(SUB):
                        until(act, added[s], 16 * g)
                        until(act, dn_r, SUB * g + s + 1)
                        act.activation(y[:, s, :], dnp[s][:], ACT.Copy, scale=sw[:, ds(SUB * g + s, 1)]).then_inc(y_r, 1)

                def expert(e, parity, last, half, first, end):
                    nxt = None if last else (e + 1, 1 - parity, half + parity)
                    each_tile(act, first, end, lambda g, new: tile(g, nxt if new else None))

                act.activation(warm[0:1, 0:1], cst["ones"][0:1, 0:1], ACT.Silu)
                for part in range(3):
                    split_part(0, 0, 0, part)
                keep_x(0)
                each_expert(act, expert)

            @block.vector
            def _(dve):
                def split_part(e, parity, part):
                    until(dve, hi_r, 3 * e + part + 1)
                    if part < 2:
                        half = slice(part * DC // 2, (part + 1) * DC // 2)
                        dve.tensor_tensor(gu_lo[parity][:, half, :], raw_gu[parity][:, half, :],
                                          gu_hi[parity][:, half, :].bitcast(F32), ALU.subtract).then_inc(gulo_r, 1)
                    else:
                        dve.tensor_tensor(dn_lo[parity][:], raw_dn[parity][:], dn_hi[parity][:].bitcast(F32),
                                          ALU.subtract).then_inc(dnlo_r, 1)

                def keep_x(g):
                    for i in (0, 1):
                        until(dve, xhi_r, 2 * g + i + 1)
                        dve.tensor_tensor(x_lo[:, 2 * i:2 * i + 2, :], trp[i][:].bitcast(F32),
                                          x_hi[:, 2 * i:2 * i + 2, :].bitcast(F32), ALU.subtract).then_inc(xlo_r, 1)

                def tile(g, split):
                    until(dve, dn_r, SUB * g)
                    parts = [0, 1, 2] if split is not None else []
                    for q, (rows, gc, gp, uc, up) in enumerate(pieces):
                        until(dve, sg_r, NQ * g + q + 1)
                        until(dve, chunk_r, NC * g + uc + 1)
                        dve.tensor_tensor(h[0:rows, q, :], gup[chunks[uc][2]][up:up + rows, 0:TILE],
                                          sg[up:up + rows, q, :], ALU.mult).then_inc(h_r, 1)
                        until(dve, h_r, NQ * g + q + 1)
                        dve.tensor_copy(h_hi[0:rows, q, :], h[0:rows, q, :]).then_inc(dve_s, 1)
                        until(dve, dve_s, NQ * g + q + 1)
                        dve.tensor_tensor(h_lo[0:rows, q, :], h[0:rows, q, :], h_hi[0:rows, q, :].bitcast(F32),
                                          ALU.subtract).then_inc(hs_r, 1)
                        if parts and q < NQ - 1 and spread:
                            split_part(*split, parts.pop(0))
                    keep_x(g + 1)
                    for part in parts:
                        split_part(*split, part)

                def expert(e, parity, last, half, first, end):
                    nxt = None if last else (e + 1, 1 - parity)
                    each_tile(dve, first, end, lambda g, new: tile(g, nxt if new else None))

                for part in range(3):
                    split_part(0, 0, part)
                keep_x(0)
                each_expert(dve, expert)

            @block.tensor
            def _(pe):
                def transposes(g):
                    until(pe, x_in, 16 * SUB * (g + 1))
                    until(pe, xlo_r, 2 * g)
                    for c in range(DC):
                        for s in range(SUB):
                            at = (c % 2) * TILE + s * P
                            mm = pe.transpose(trp[c // 2][:, at:at + P], x[:, s, c * P:(c + 1) * P], cst["ident_r"][:])
                    mm.then_inc(tr_r, 1)

                def tile(g, e, parity, first):
                    until(pe, xlo_r, 2 * g + 2)
                    owner = {}
                    for n, (at, cols_n, bk) in enumerate(chunks):
                        if bk in owner:
                            until(pe, h_r, NQ * g + owner[bk] + 1)
                        owner[bk] = piece_of[n]
                        for c in range(DC):
                            w_hi, w_lo = gu_hi[parity][:, c, at:at + cols_n], gu_lo[parity][:, c, at:at + cols_n]
                            out = gup[bk][0:cols_n, 0:TILE]
                            pe.matmul(out, w_hi, x_hi[:, c, :], start=(c == 0), stop=False)
                            pe.matmul(out, w_hi, x_lo[:, c, :], start=False, stop=False)
                            mm = pe.matmul(out, w_lo, x_hi[:, c, :], start=False, stop=(c == DC - 1))
                        mm.then_inc(chunk_r, 1)
                    transposes(g + 1)
                    until(pe, y_r, SUB * g)
                    if first:
                        until(pe, dnlo_r, e + 1)
                    for q, (rows, *_) in enumerate(pieces):
                        until(pe, hs_r, NQ * g + q + 1)
                        for s in range(SUB):
                            a_hi = h_hi[0:rows, q, s * P:(s + 1) * P]
                            a_lo = h_lo[0:rows, q, s * P:(s + 1) * P]
                            w_hi, w_lo = dn_hi[parity][0:rows, q, :], dn_lo[parity][0:rows, q, :]
                            pe.matmul(dnp[s][:], a_hi, w_hi, start=(q == 0), stop=False)
                            pe.matmul(dnp[s][:], a_hi, w_lo, start=False, stop=False)
                            mm = pe.matmul(dnp[s][:], a_lo, w_hi, start=False, stop=(q == NQ - 1))
                            if q == NQ - 1:
                                mm.then_inc(dn_r, 1)

                piece_of = {}
                for q, (_, gc, _, uc, _) in enumerate(pieces):
                    piece_of[gc] = piece_of[uc] = q

                def expert(e, parity, last, half, first, end):
                    until(pe, gulo_r, 2 * e + 2)
                    each_tile(pe, first, end, lambda g, new: tile(g, e, parity, new))

                transposes(0)
                each_expert(pe, expert)


CHUNKS_A = [(0, 128, 0), (128, 128, 1), (256, 128, 2)]
PIECES_A = [(64, 0, 0, 0, 64), (128, 1, 0, 2, 0)]
CHUNKS_B = [(0, 128, 0), (128, 128, 1), (256, 128, 2), (384, 128, 3), (512, 96, 0), (608, 96, 1)]
PIECES_B = [(128, 0, 0, 1, 0), (128, 2, 0, 3, 0), (96, 4, 0, 5, 0)]

H = 16
R = 64
Q = 384
QC = Q // P
WS = DC * P + Q + P
WR = P + D


def add_and_transpose(nc, cst, X, accs, ctx_in, cos_k, sin_k, xT_hi, xT_lo, kv, kvT_hi, kvT_lo):
    with ExitStack() as ctx:
        def mem(name, shape, dt=F32):
            return ctx.enter_context(nc.sbuf_tensor("t_" + name, shape, dt))

        sem = semaphores(nc, ctx, "t_")

        acc, N = mem("acc", [P, SUB, SJ, D]), mem("N", [P, SJ, D])
        stats, mv = mem("stats", [P, SJ, 6]), mem("mv", [P, SJ, 2])
        ve, rstd, nbias = mem("ve", [P, SJ]), mem("rstd", [P, SJ]), mem("nbias", [P, SJ])
        cos, sin, c_in = mem("cos", [P, SJ, C]), mem("sin", [P, SJ, C]), mem("ctx", [P, SJ, C])
        t1, t2 = mem("t1", [P, SJ, C]), mem("t2", [P, SJ, C])
        trp = [ctx.enter_context(nc.psum_tensor(f"t_tr{c}", [P, S], F32)) for c in range(DC)]
        kvp = ctx.enter_context(nc.psum_tensor("t_kv", [P, S], F32))
        tabs_in, acc_in, ctx_s, x_r, var_r, rstd_r, nb_r, n_r, tr_r, kv_r, kvp_r, hi_r, lo_r, khi_r, klo_r, dve_s, pool_s = (
            sem(n) for n in ("tabs_in", "acc_in", "ctx_in", "x_added", "var", "rstd", "nbias", "rows_normal",
                             "transposed", "kv_rotated", "kv_transposed", "x_hi", "x_lo", "kv_hi", "kv_lo", "dve", "pool"))
        av = [rows[0:T, :].rearrange("(b j p) d -> b p j d", p=P, j=SJ) for rows in accs]
        cv = ctx_in.rearrange("(b j p) c -> b p j c", p=P, j=SJ)
        STEPS = 8

        with nc.Block() as block:
            @block.sync
            def _(sp):
                def load(b):
                    for s in range(SUB):
                        sp.dma_start(acc[:, s, :, :],
                                     av[s][ds(b, 1)].rearrange("a p j d -> (a p) j d")).then_inc(acc_in, 16)

                def context(b):
                    sp.dma_start(c_in[:], cv[ds(b, 1)].rearrange("a p j c -> (a p) j c")).then_inc(ctx_s, 16)

                load(0)
                context(0)
                sp.dma_start(cos[:], cos_k).then_inc(tabs_in, 16)
                sp.dma_start(sin[:], sin_k).then_inc(tabs_in, 16)
                with sp.Fori(1, B) as b:
                    until(sp, x_r, b)
                    load(b)
                    until(sp, kv_r, b)
                    context(b)

            @block.gpsimd
            def _(pool):
                def rotate(b):
                    step = Steps(pool, pool_s, 4 * b)
                    until(pool, ctx_s, 16 * b + 16)
                    until(pool, kvp_r, b)
                    step(pool.tensor_tensor(t1[:], c_in[:], cos[:], ALU.mult))
                    step(pool.tensor_tensor(t2[:, :, 0:C // 2], c_in[:, :, C // 2:C], sin[:, :, 0:C // 2], ALU.mult))
                    step(pool.tensor_tensor(t2[:, :, C // 2:C], c_in[:, :, 0:C // 2], sin[:, :, C // 2:C], ALU.mult))
                    step.settle()
                    step(pool.tensor_tensor(t1[:], t1[:], t2[:], ALU.add))
                    step.settle()
                    pool.tensor_copy(kv[:, ds(SJ * b, SJ), :], t1[:]).then_inc(kv_r, 1)

                def power(b):
                    until(pool, var_r, b + 1)
                    until(pool, n_r, SJ * b)
                    pool.tensor_tensor(rstd[:], ve[:], cst["mhalf"][:, 0:SJ], ALU.pow).then_inc(rstd_r, 1)

                pool.wait_ge(tabs_in, 32)
                rotate(0)
                with pool.Fori(0, B - 1) as b:
                    power(b)
                    rotate(b + 1)
                power(B - 1)

            @block.scalar
            def _(act):
                with act.Fori(0, B) as b:
                    until(act, nb_r, b + 1)
                    until(act, tr_r, DC * b)
                    for j in range(SJ):
                        act.activation(N[:, j, :], X[:, ds(SJ * b + j, 1), :].rearrange("p a d -> p (a d)"),
                                       ACT.Identity, bias=nbias[:, j:j + 1], scale=rstd[:, j:j + 1]).then_inc(n_r, 1)
                    until(act, kvp_r, b + 1)
                    act.activation(kvT_hi[:, ds(S * b, S)], kvp[:], ACT.Copy).then_inc(khi_r, 1)
                    for c in range(DC):
                        until(act, tr_r, DC * b + c + 1)
                        act.activation(xT_hi[:, c, ds(S * b, S)], trp[c][:], ACT.Copy).then_inc(hi_r, 1)

            @block.tensor
            def _(pe):
                with pe.Fori(0, B) as b:
                    until(pe, kv_r, b + 1)
                    until(pe, klo_r, b)
                    for j in range(SJ):
                        mm = pe.transpose(kvp[:, j * P:(j + 1) * P], t1[:, j, :], cst["ident"][:])
                    mm.then_inc(kvp_r, 1)
                    until(pe, n_r, SJ * b + SJ)
                    until(pe, lo_r, DC * b)
                    for c in range(DC):
                        for j in range(SJ):
                            mm = pe.transpose(trp[c][:, j * P:(j + 1) * P], N[:, j, c * P:(c + 1) * P], cst["ident"][:])
                        mm.then_inc(tr_r, 1)

            @block.vector
            def _(dve):
                def add(b):
                    step = Steps(dve, dve_s, STEPS * b)
                    until(dve, acc_in, 16 * SUB * (b + 1))
                    xs = X[:, ds(SJ * b, SJ), :]
                    dve.tensor_tensor(xs, acc[:, 0, :, :], acc[:, 1, :, :], ALU.add).then_inc(x_r, 1)
                    until(dve, x_r, b + 1)
                    for j in range(SJ):
                        step(dve.bn_stats(stats[:, j, :], X[:, ds(SJ * b + j, 1), :].rearrange("p a d -> p (a d)")))
                    step.settle()
                    for j in range(SJ):
                        step(dve.bn_aggr(mv[:, j, :], stats[:, j, :]))
                    step.settle()
                    dve.tensor_scalar(ve[:], mv[:, :, 1], LN_EPS, None, ALU.add).then_inc(var_r, 1)
                    until(dve, rstd_r, b + 1)
                    until(dve, n_r, SJ * b)
                    dve.scalar_tensor_tensor(nbias[:], mv[:, :, 0], -1.0, rstd[:], ALU.mult, ALU.mult).then_inc(nb_r, 1)
                    assert step.n == STEPS

                def low_parts(b):
                    until(dve, khi_r, b + 1)
                    dve.tensor_tensor(kvT_lo[:, ds(S * b, S)], kvp[:], kvT_hi[:, ds(S * b, S)].bitcast(F32),
                                      ALU.subtract).then_inc(klo_r, 1)
                    for c in range(DC):
                        until(dve, hi_r, DC * b + c + 1)
                        dve.tensor_tensor(xT_lo[:, c, ds(S * b, S)], trp[c][:], xT_hi[:, c, ds(S * b, S)].bitcast(F32),
                                          ALU.subtract).then_inc(lo_r, 1)

                add(0)
                with dve.Fori(0, B - 1) as b:
                    add(b + 1)
                    low_parts(b)
                low_parts(B - 1)


def second_layer_attention(nc, cst, X, ws_in, wqr_in, wr_in, cosT_in, sinT_in, xT_hi, xT_lo, kv, kvT_hi, kvT_lo):
    with ExitStack() as ctx:
        def mem(name, shape, dt=F32):
            return ctx.enter_context(nc.sbuf_tensor("s_" + name, shape, dt))

        sem = semaphores(nc, ctx, "s_")

        cosT, sinT = mem("cosT", [P, QC, S]), mem("sinT", [P, QC, S])
        raw, rawv = mem("raw", [P, WS]), mem("rawv", [P, WR])
        w_hi, w_lo = [[mem(f"w_{n}{i}", [P, WS], F32R) for i in (0, 1)] for n in ("hi", "lo")]
        v_hi, v_lo = [[mem(f"v_{n}{i}", [P, D], F32R) for i in (0, 1)] for n in ("hi", "lo")]
        wqr = [mem(f"wqr{i}", [P, QC, R]) for i in (0, 1)]
        qh_hi, qh_lo = mem("qh_hi", [P, S], F32R), mem("qh_lo", [P, S], F32R)
        q, t = mem("q", [P, QC, S]), mem("t", [P, QC, S])
        q2, q3 = mem("q2", [P, S], F32R), mem("q3", [R + 1, S], F32R)
        k2, k3 = mem("k2", [P, S], F32R), mem("k3", [R + 1, S], F32R)
        top, warm = mem("top", [P, SJ]), mem("warm", [1, 1])
        pT = mem("pT", [P, SJ, S])
        s4 = mem("s4", [P, S])
        gsum = mem("gsum", [P, SJ])
        c_hi, c_lo = mem("c_hi", [P, S], F32R), mem("c_lo", [P, S], F32R)
        y = pT
        ap = ctx.enter_context(nc.psum_tensor("s_a", [P, 4, S], F32))
        bp = ctx.enter_context(nc.psum_tensor("s_b", [P, 4, S], F32))
        names = ("tabs_in", "raw_in", "wqr_in", "w_hi", "w_lo", "v_made", "v_hi", "v_lo", "qh_made", "qh_hi", "qh_lo",
                 "big_made", "dve", "rotated", "q_made", "q2_hi", "q3_hi", "q_lo", "k_made", "k_hi", "k_lo",
                 "smax_made", "top", "top_rows", "top_kept", "scores", "exp", "pairs_added", "sum_in", "ctx_made",
                 "sum_made", "recip", "c_hi", "c_lo", "out_made", "out_kept", "x_added", "ones_row")
        (tabs_in, raw_in, wqr_s, whi_r, wlo_r, vp_r, vhi_r, vlo_r, qh_r, qhhi_r, qhlo_r, big_r, dve_s, rot_r, q_r,
         q2_r, q3_r, qlo_r, k_r, khi_r, klo_r, smax_r, top_r, row_r, m_r, sc_r, e_r, pair_r, s4_r, ctx_r, sum_r, rec_r,
         chi_r, clo_r, out_r, y_r, x_r, one_r) = (sem(n) for n in names)
        KQ, KB, KK = 0, DC * P, DC * P + Q

        def heads(eng, step):
            def pair(h0, last):
                for hp in (0, 1):
                    for b in range(B):
                        n = B * (h0 + hp) + b
                        step(n, h0 + hp, b, hp, last and hp == 1 and b == B - 1, last and hp == 1)

            with eng.Fori(0, H // 2 - 1) as i:
                pair(2 * i, False)
            pair(H - 2, True)

        def nxt(b, parity):
            return (b + 1, parity) if b + 1 < B else (0, 1 - parity)

        with nc.Block() as block:
            @block.sync
            def _(sp):
                sp.dma_start(cosT[:], cosT_in).then_inc(tabs_in, 16)
                sp.dma_start(sinT[:], sinT_in).then_inc(tabs_in, 16)

                def load(h, parity):
                    sp.dma_start(raw[:], ws_in[ds(h, 1)].rearrange("a p w -> (a p) w")).then_inc(raw_in, 16)
                    sp.dma_start(rawv[:], wr_in[ds(h, 1)].rearrange("a p w -> (a p) w")).then_inc(raw_in, 16)
                    sp.dma_start(wqr[parity][:], wqr_in[ds(h, 1)].rearrange("a p c r -> (a p) c r")).then_inc(wqr_s, 16)

                def step(n, h, b, parity, last, last_head):
                    if b == 0 and not last_head:
                        until(sp, wlo_r, h + 1)
                        until(sp, vp_r, h + 1)
                        load(h + 1, 1 - parity)

                load(0, 0)
                heads(sp, step)

            @block.gpsimd
            def _(pool):
                def step(n, h, b, parity, last, last_head):
                    until(pool, e_r, SJ * n + 2)
                    until(pool, sum_r, n)
                    pool.tensor_tensor(s4[:], pT[:, 0, :], pT[:, 1, :], ALU.add).then_inc(pair_r, 1)
                    for j in (2, 3):
                        until(pool, e_r, SJ * n + j + 1)
                        until(pool, pair_r, 2 * n + j - 1)
                        pool.tensor_tensor(s4[:], s4[:], pT[:, j, :], ALU.add).then_inc(s4_r if j == 3 else pair_r, 1)
                    for j in range(SJ):
                        until(pool, y_r, SJ * n + j + SJ)
                        rows = X[:, SJ * b + j, :]
                        pool.tensor_tensor(rows, rows, y[:, j, :], ALU.add).then_inc(x_r, 1)
                heads(pool, step)

            @block.scalar
            def _(act):
                def split_w(h, parity):
                    until(act, raw_in, 32 * h + 32)
                    act.activation(w_hi[parity][:], raw[:], ACT.Copy).then_inc(whi_r, 1)

                def split_v(h, parity):
                    until(act, vp_r, h + 1)
                    act.activation(v_hi[parity][:], ap[:, 3, :], ACT.Copy).then_inc(vhi_r, 1)

                def queries(n):
                    until(act, qh_r, n + 1)
                    act.activation(qh_hi[:], bp[:, 0, :], ACT.Copy).then_inc(qhhi_r, 1)

                def keys(n):
                    until(act, k_r, n + 1)
                    act.activation(k2[:], ap[:, 2, :], ACT.Copy).then_inc(khi_r, 1)
                    until(act, q_r, n + 1)
                    act.activation(q3[0:R, :], ap[0:R, 1, :], ACT.Copy).then_inc(q3_r, 1)
                    act.activation(q2[0:R, :], ap[0:R, 1, :], ACT.Copy).then_inc(q2_r, 1)

                def step(n, h, b, parity, last, last_head):
                    until(act, row_r, n + 1)
                    act.activation(q3[R:R + 1, :], bp[0:1, 1, :], ACT.Copy, scale=-1.0).then_inc(m_r, 1)
                    if not last:
                        queries(n + 1)
                    until(act, x_r, SJ * n)
                    for j in range(SJ):
                        until(act, sc_r, SJ * n + j + 1)
                        act.activation(pT[:, j, :], ap[:, j, :], ACT.Exp).then_inc(e_r, 1)
                    until(act, ctx_r, n + 1)
                    act.activation(c_hi[:], bp[:, 0, :], ACT.Copy).then_inc(chi_r, 1)
                    if b == B - 1 and not last_head:
                        split_v(h + 1, 1 - parity)
                    if not last:
                        keys(n + 1)
                    until(act, rec_r, 2 * n + 2)
                    for j in range(SJ):
                        until(act, out_r, SJ * n + j + 1)
                        act.activation(y[:, j, :], bp[:, j, :], ACT.Copy, scale=gsum[:, j:j + 1]).then_inc(y_r, 1)
                    if b == 1 and not last_head:
                        split_w(h + 1, 1 - parity)

                act.activation(warm[0:1, 0:1], cst["ones"][0:1, 0:1], ACT.Exp).then_inc(y_r, SJ - 1)
                split_w(0, 0)
                split_v(0, 0)
                queries(0)
                keys(0)
                heads(act, step)

            @block.vector
            def _(dve):
                def split_w(h, parity):
                    until(dve, whi_r, h + 1)
                    dve.tensor_tensor(w_lo[parity][:], raw[:], w_hi[parity][:].bitcast(F32),
                                      ALU.subtract).then_inc(wlo_r, 1)

                def split_v(h, parity):
                    until(dve, vhi_r, h + 1)
                    dve.tensor_tensor(v_lo[parity][:], ap[:, 3, :], v_hi[parity][:].bitcast(F32),
                                      ALU.subtract).then_inc(vlo_r, 1)

                def queries(n):
                    until(dve, qhhi_r, n + 1)
                    dve.tensor_tensor(qh_lo[:], bp[:, 0, :], qh_hi[:].bitcast(F32), ALU.subtract).then_inc(qhlo_r, 1)

                def rotate(n):
                    done = 8 * n
                    until(dve, big_r, QC * n + 2)
                    until(dve, q_r, n)
                    dve.tensor_tensor(q[:, 0, :], bp[:, 1, :], cosT[:, 0, :], ALU.mult).then_inc(dve_s, 1)
                    dve.tensor_tensor(t[:, 0, :], bp[:, 2, :], sinT[:, 0, :], ALU.mult).then_inc(dve_s, 1)
                    dve.tensor_tensor(q[:, 1, :], bp[:, 2, :], cosT[:, 1, :], ALU.mult).then_inc(dve_s, 1)
                    dve.tensor_tensor(t[:, 1, :], bp[:, 1, :], sinT[:, 1, :], ALU.mult).then_inc(dve_s, 1)
                    until(dve, dve_s, done + 2)
                    dve.tensor_tensor(q[:, 0, :], q[:, 0, :], t[:, 0, :], ALU.add).then_inc(rot_r, 1)
                    until(dve, dve_s, done + 4)
                    dve.tensor_tensor(q[:, 1, :], q[:, 1, :], t[:, 1, :], ALU.add).then_inc(rot_r, 1)
                    until(dve, big_r, QC * n + 3)
                    half = P // 2
                    dve.tensor_tensor(q[:, 2, :], bp[:, 3, :], cosT[:, 2, :], ALU.mult).then_inc(dve_s, 1)
                    dve.tensor_tensor(t[0:half, 2, :], bp[half:P, 3, :], sinT[half:P, 2, :], ALU.mult).then_inc(dve_s, 1)
                    dve.tensor_tensor(t[half:P, 2, :], bp[0:half, 3, :], sinT[0:half, 2, :], ALU.mult).then_inc(dve_s, 1)
                    until(dve, dve_s, done + 7)
                    dve.tensor_tensor(q[:, 2, :], q[:, 2, :], t[:, 2, :], ALU.add).then_inc(rot_r, 1)
                    dve.engine_nop().then_inc(dve_s, 1)

                def keys(n):
                    until(dve, khi_r, n + 1)
                    dve.tensor_tensor(k3[0:R, :], ap[0:R, 2, :], k2[0:R, :].bitcast(F32),
                                      ALU.subtract).then_inc(klo_r, 1)
                    until(dve, q3_r, n + 1)
                    until(dve, q2_r, n + 1)
                    dve.tensor_tensor(q2[R:2 * R, :], ap[0:R, 1, :], q3[0:R, :].bitcast(F32),
                                      ALU.subtract).then_inc(qlo_r, 1)

                def step(n, h, b, parity, last, last_head):
                    for j in range(SJ):
                        until(dve, smax_r, SJ * n + j + 1)
                        dve.tensor_reduce(top[:, j:j + 1], ap[:, j, :], AX_X, ALU.max).then_inc(top_r, 1)
                    if not last:
                        queries(n + 1)
                        rotate(n + 1)
                    until(dve, chi_r, n + 1)
                    dve.tensor_tensor(c_lo[:], bp[:, 0, :], c_hi[:].bitcast(F32), ALU.subtract).then_inc(clo_r, 1)
                    until(dve, sum_r, n + 1)
                    until(dve, y_r, SJ * n + SJ - 1)
                    dve.reciprocal(gsum[:], ap[:, 0, 0:SJ]).then_inc(rec_r, 1)
                    until(dve, rec_r, 2 * n + 1)
                    dve.tensor_scalar(gsum[:], gsum[:], cst["tanhg"][:, 1:2], None, ALU.mult).then_inc(rec_r, 1)
                    if b == B - 1 and not last_head:
                        split_v(h + 1, 1 - parity)
                    if not last:
                        keys(n + 1)
                    if b == 2 and not last_head:
                        split_w(h + 1, 1 - parity)

                dve.wait_ge(tabs_in, 32)
                dve.memset(k3[R:R + 1, :].bitcast(F32), 1.0).then_inc(one_r, 1)
                split_w(0, 0)
                split_v(0, 0)
                queries(0)
                rotate(0)
                keys(0)
                heads(dve, step)

            @block.tensor
            def _(pe):
                def three(out, a_hi, a_lo, b_hi, b_lo, start=True, stop=True):
                    pe.matmul(out, a_hi, b_hi, start=start, stop=False)
                    pe.matmul(out, a_hi, b_lo, start=False, stop=False)
                    return pe.matmul(out, a_lo, b_hi, start=False, stop=stop)

                def queries(n, b, parity, chunks=range(DC)):
                    for c in chunks:
                        w = slice(KQ + c * P, KQ + (c + 1) * P)
                        mm = three(bp[:, 0, :], w_hi[parity][:, w], w_lo[parity][:, w],
                                   xT_hi[:, c, b * S:(b + 1) * S], xT_lo[:, c, b * S:(b + 1) * S], c == 0, c == DC - 1)
                    if c == DC - 1:
                        mm.then_inc(qh_r, 1)

                def big(n, parity):
                    until(pe, qhlo_r, n + 1)
                    for c in range(QC):
                        w = slice(KB + c * P, KB + (c + 1) * P)
                        three(bp[:, 1 + c, :], w_hi[parity][:, w], w_lo[parity][:, w], qh_hi[:],
                              qh_lo[:]).then_inc(big_r, 1)

                def keys(n, b, parity):
                    w = slice(KK, KK + P)
                    three(ap[:, 2, :], w_hi[parity][:, w], w_lo[parity][:, w], kvT_hi[:, b * S:(b + 1) * S],
                          kvT_lo[:, b * S:(b + 1) * S]).then_inc(k_r, 1)
                    for c in range(QC):
                        until(pe, rot_r, QC * n + c + 1)
                        mm = pe.matmul(ap[0:R, 1, :], wqr[parity][:, c, :], q[:, c, :], start=(c == 0),
                                       stop=(c == QC - 1))
                    mm.then_inc(q_r, 1)

                def values(h):
                    until(pe, raw_in, 32 * h + 32)
                    pe.matmul(ap[:, 3, :], rawv[:, 0:P], rawv[:, P:P + D], start=True, stop=True).then_inc(vp_r, 1)

                def step(n, h, b, parity, last, last_head):
                    until(pe, klo_r, n + 1)
                    until(pe, qlo_r, n + 1)
                    if b == 0:
                        until(pe, vlo_r, h + 1)
                    for j in range(SJ):
                        pe.matmul(ap[:, j, :], q3[0:R, j * P:(j + 1) * P], k2[0:R, :], start=True,
                                  stop=True).then_inc(smax_r, 1)
                    nb, np_ = nxt(b, parity)
                    until(pe, y_r, SJ * n)
                    if not last:
                        if b == B - 1:
                            until(pe, wlo_r, h + 2)
                            until(pe, wqr_s, 16 * h + 32)
                        queries(n + 1, nb, np_, range(DC - 1))
                    until(pe, y_r, SJ * n + SJ - 1)
                    until(pe, top_r, SJ * n + SJ)
                    for j in range(SJ):
                        mm = pe.transpose(bp[0:1, 1, j * P:(j + 1) * P], top[:, j:j + 1], cst["ident"][:])
                    mm.then_inc(row_r, 1)
                    if not last:
                        queries(n + 1, nb, np_, [DC - 1])
                    until(pe, m_r, n + 1)
                    for j in range(SJ):
                        pe.matmul(ap[:, j, :], k2[:, j * P:(j + 1) * P], q2[:], start=True, stop=False)
                        pe.matmul(ap[:, j, :], k3[:, j * P:(j + 1) * P], q3[:], start=False, stop=True).then_inc(sc_r, 1)
                    if not last:
                        big(n + 1, np_)
                    for j in range(SJ):
                        until(pe, e_r, SJ * n + j + 1)
                        mm = pe.matmul(bp[:, 0, :], kv[:, SJ * b + j, :], pT[:, j, :], start=(j == 0), stop=(j == SJ - 1))
                    mm.then_inc(ctx_r, 1)
                    until(pe, s4_r, n + 1)
                    for j in range(SJ):
                        mm = pe.matmul(ap[:, 0, j:j + 1], s4[:, j * P:(j + 1) * P], cst["ones"][:, 0:1], start=True,
                                       stop=True)
                    mm.then_inc(sum_r, 1)
                    if b == B - 1 and not last_head:
                        values(h + 1)
                    if not last:
                        keys(n + 1, nb, np_)
                    until(pe, clo_r, n + 1)
                    for j in range(SJ):
                        rows = slice(j * P, (j + 1) * P)
                        three(bp[:, j, :], c_hi[:, rows], c_lo[:, rows], v_hi[parity][:], v_lo[parity][:]).then_inc(out_r, 1)

                pe.wait_ge(wqr_s, 16)
                values(0)
                pe.wait_ge(one_r, 1)
                pe.wait_ge(wlo_r, 1)
                queries(0, 0, 0)
                big(0, 0)
                keys(0, 0, 0)
                heads(pe, step)


def second_attention_all(nc, cst, X, accs, ctx_in, cos_k, sin_k, ws_in, wqr_in, wr_in, cosT_in, sinT_in):
    with ExitStack() as ctx:
        def mem(name, shape, dt=F32):
            return ctx.enter_context(nc.sbuf_tensor(name, shape, dt))

        xT_hi, xT_lo = mem("xT_hi", [P, DC, T], F32R), mem("xT_lo", [P, DC, T], F32R)
        kvT_hi, kvT_lo = mem("kvT_hi", [P, T], F32R), mem("kvT_lo", [P, T], F32R)
        kv = mem("kv", [P, NT, C])
        add_and_transpose(nc, cst, X, accs, ctx_in, cos_k, sin_k, xT_hi, xT_lo, kv, kvT_hi, kvT_lo)
        second_layer_attention(nc, cst, X, ws_in, wqr_in, wr_in, cosT_in, sinT_in, xT_hi, xT_lo, kv, kvT_hi, kvT_lo)

E2, K2, CAP = 16, 2, 256
COLS2 = E2 * CAP // P
TILES2 = E2 * CAP // TILE + T // TILE


def second_layer_routing(nc, cst, X, gw_in, bias_in, xn_dram, tab_dram, table, slot, entry, acc, weights):
    with ExitStack() as ctx:
        def mem(name, shape, dt=F32):
            return ctx.enter_context(nc.sbuf_tensor("r_" + name, shape, dt))

        sem = semaphores(nc, ctx, "r_")

        M = NT * K2
        gw, bias = mem("gw", [P, DC, E2]), mem("bias", [P, E2])
        N, NTr = [mem(f"N{i}", [P, SJ, D]) for i in (0, 1)], mem("NT", [P, DC, S])
        stats, mv = mem("stats", [P, NT, 6]), mem("mv", [P, NT, 2])
        ve, rstd, nbias = mem("ve", [P, NT]), mem("rstd", [P, NT]), mem("nbias", [P, NT])
        lg, score, pick = mem("lg", [P, NT, E2]), mem("score", [P, NT, E2]), mem("pick", [P, NT, E2])
        u, w1, d, dz = mem("u", [P, NT, E2]), mem("w1", [P, NT, E2]), mem("d", [P, NT, E2]), mem("dz", [P, NT, E2])
        ln = mem("ln", [P, NT, E2])
        top8, idx8 = mem("top8", [P, NT, 8]), mem("idx8", [P, NT, 8], U32)
        idxf = mem("idxf", [P, NT, K2])
        hot, tmp = mem("hot", [P, M, E2]), mem("tmp", [P, M, E2])
        mask, pref = mem("mask", [P, NT, E2]), mem("pref", [P, NT, E2])
        pos, low, pos_i = mem("pos", [P, NT * E2]), mem("low", [P, NT * E2], I32), mem("pos_i", [P, NT * E2], I32)
        addr = mem("addr", [P, NT * E2])
        s_k, p_k, a_k, valid = mem("s_k", [P, M]), mem("p_k", [P, M]), mem("a_k", [P, M]), mem("valid", [P, M])
        wsum = mem("wsum", [P, NT])
        iota_e, e2, ids, spare = (mem("iota_e", [P, E2], I32), mem("e2", [P, NT, E2], I32),
                                  mem("ids", [P, NT, K2], I32), mem("spare", [P, NT, K2], I32))
        iota_ef, spare_f, weight1 = mem("iota_ef", [P, E2]), mem("spare_f", [P, M]), mem("weight1", [P, NT + SUB * 2])
        init, zeros = mem("init", [P, COLS2, 2], I32), mem("zeros", [P, D])
        trp = [ctx.enter_context(nc.psum_tensor(f"r_tr{c}", [P, S], F32)) for c in range(DC)]
        lgp = ctx.enter_context(nc.psum_tensor("r_logits_sum", [P, SJ, E2], F32))
        posp = ctx.enter_context(nc.psum_tensor("r_place_sum", [P, NT * E2], F32))
        rows_out = [sem(f"rows_out{i}") for i in (0, 1)]
        (c_in, var_r, rstd_r, nb_r, n_r, tr_r, keep_a, keep_v, lg_r, lgk_r, dve_s, iota_r, init_s,
         zeros_r, abs_r, u_r, w1_r, ln_r, sp_r, score_r, mask_r, pos_r) = (sem(n) for n in (
             "consts_in", "var", "rstd", "nbias", "rows_normal", "transposed", "kept_by_act", "kept_by_dve",
             "logits_made", "logits_kept", "dve", "iota", "tab_init", "zeros", "abs", "exp",
             "one_plus", "ln", "softplus", "score", "mask", "pos"))
        xnv = xn_dram[0:T, :].rearrange("(b j p) d -> b p j d", p=P, j=SJ)

        def sequences(eng, body):
            with eng.Fori(0, B // 2) as i:
                body(2 * i, 0)
                body(2 * i + 1, 1)

        with nc.Block() as block:
            @block.sync
            def _(sp):
                sp.dma_start(gw[:], gw_in).then_inc(c_in, 16)
                sp.dma_start(bias[:], bias_in.partition_broadcast(P)).then_inc(c_in, 16)
                sp.wait_ge(iota_r, 7)
                sp.dma_start(tab_dram[0:E2 * CAP, :].rearrange("(p c) w -> p c w", p=P), init[:]).then_inc(init_s, 16)
                sp.wait_ge(zeros_r, 1)
                sp.dma_start(xn_dram[T:T + P, :], zeros[:]).then_inc(init_s, 16)
                sp.dma_start(acc[0:T, :].rearrange("(n p) d -> p n d", p=P), X[:]).then_inc(init_s, 16)
                sp.dma_start(acc[T:T + P, :], zeros[:]).then_inc(init_s, 16)

                def step(b, parity):
                    until(sp, n_r, SJ * b + SJ)
                    sp.dma_start(xnv[ds(b, 1)].rearrange("a p j d -> (a p) j d"),
                                 N[parity][:]).then_inc(rows_out[parity], 16)

                sequences(sp, step)
                for e in (0, 1):
                    weights.load(sp, e, e)
                for sent in rows_out:
                    sp.wait_ge(sent, 16 * B // 2)
                sp.wait_ge(init_s, 64)

            @block.gpsimd
            def _(pool):
                pool.iota(iota_e[:], [[1, E2]], base=0, channel_multiplier=0).then_inc(iota_r, 1)
                pool.iota(e2[:], [[0, NT], [CAP // P, E2]], base=0, channel_multiplier=0).then_inc(iota_r, 1)
                pool.iota(ids[:], [[P, NT], [0, K2]], base=0, channel_multiplier=1).then_inc(iota_r, 1)
                pool.iota(spare[:], [[P, NT], [T, K2]], base=E2 * CAP, channel_multiplier=1).then_inc(iota_r, 1)
                pool.iota(init[:, :, 0], [[0, COLS2]], base=T, channel_multiplier=1).then_inc(iota_r, 1)
                pool.memset(init[:, :, 1], 0).then_inc(iota_r, 1)
                pool.iota(table[:, 0:NT, 0], [[P, NT]], base=0, channel_multiplier=1).then_inc(iota_r, 1)
                pool.memset(table[:, COLS2 + NT:COLS2 + NT + 2 * SUB, 0], 0).then_inc(iota_r, 1)
                pool.wait_ge(var_r, 1)
                pool.tensor_tensor(rstd[:], ve[:], cst["mhalf"][:], ALU.pow).then_inc(rstd_r, 1)

            @block.scalar
            def _(act):
                def rows(b):
                    for j in range(SJ):
                        t = SJ * b + j
                        act.activation(N[b % 2][:, j, :], X[:, t, :], ACT.Identity, bias=nbias[:, t:t + 1],
                                       scale=rstd[:, t:t + 1]).then_inc(n_r, 1)

                act.wait_ge(nb_r, 1)
                rows(0)
                rows(1)
                for b in range(B):
                    if b > 0:
                        act.wait_ge(lg_r, b)
                    for c in (0, 1):
                        act.wait_ge(tr_r, DC * b + c + 1)
                        act.activation(NTr[:, c, :], trp[c][:], ACT.Copy).then_inc(keep_a, 1)
                    if b + 2 < B:
                        act.wait_ge(tr_r, DC * b + DC)
                        act.wait_ge(rows_out[b % 2], 16 * (b // 2 + 1))
                        rows(b + 2)
                act.wait_ge(abs_r, 1)
                act.activation(u[:], u[:], ACT.Exp).then_inc(u_r, 1)
                act.wait_ge(w1_r, 1)
                act.activation(ln[:], w1[:], ACT.Ln).then_inc(ln_r, 1)
                act.wait_ge(sp_r, 1)
                act.activation(score[:], score[:], ACT.Sqrt).then_inc(score_r, 1)

            @block.tensor
            def _(pe):
                pe.wait_ge(c_in, 32)

                def step(b, parity):
                    until(pe, n_r, SJ * b + SJ)
                    until(pe, keep_v, 2 * b)
                    until(pe, keep_a, 2 * b)
                    for c in range(DC):
                        for j in range(SJ):
                            mm = pe.transpose(trp[c][:, j * P:(j + 1) * P], N[parity][:, j, c * P:(c + 1) * P],
                                              cst["ident"][:])
                        mm.then_inc(tr_r, 1)
                    until(pe, keep_a, 2 * b + 2)
                    until(pe, keep_v, 2 * b + 2)
                    until(pe, lgk_r, b)
                    for j in range(SJ):
                        for c in range(DC):
                            mm = pe.matmul(lgp[:, j, :], NTr[:, c, j * P:(j + 1) * P], gw[:, c, :],
                                           start=(c == 0), stop=(c == DC - 1))
                    mm.then_inc(lg_r, 1)

                sequences(pe, step)
                pe.wait_ge(mask_r, 1)
                pe.matmul(posp[:], cst["before"][:], mask[:].rearrange("p j e -> p (j e)"), start=True, stop=False)
                pe.matmul(posp[:], cst["ones"][:], pref[:].rearrange("p j e -> p (j e)"), start=False,
                          stop=True).then_inc(pos_r, 1)

            @block.vector
            def _(dve):
                dve.memset(zeros[:], 0.0).then_inc(zeros_r, 1)
                step = Steps(dve, dve_s)
                for t in range(NT):
                    step(dve.bn_stats(stats[:, t, :], X[:, t, :]))
                step.settle()
                for t in range(NT):
                    step(dve.bn_aggr(mv[:, t, :], stats[:, t, :]))
                step.settle()
                dve.tensor_scalar(ve[:], mv[:, :, 1], LN_EPS, None, ALU.add).then_inc(var_r, 1)
                dve.wait_ge(rstd_r, 1)
                dve.scalar_tensor_tensor(nbias[:], mv[:, :, 0], -1.0, rstd[:], ALU.mult, ALU.mult).then_inc(nb_r, 1)
                with dve.Fori(0, B) as b:
                    until(dve, lg_r, b)
                    for c in (2, 3):
                        until(dve, tr_r, DC * b + c + 1)
                        dve.tensor_copy(NTr[:, c, :], trp[c][:]).then_inc(keep_v, 1)
                    until(dve, lg_r, b + 1)
                    dve.tensor_copy(lg[:, ds(SJ * b, SJ), :], lgp[:]).then_inc(lgk_r, 1)
                dve.wait_ge(lgk_r, B)
                dve.wait_ge(iota_r, 8)
                dve.scalar_tensor_tensor(u[:], lg[:], -1.0, lg[:], ALU.mult, ALU.min).then_inc(abs_r, 1)
                dve.wait_ge(u_r, 1)
                dve.tensor_scalar(w1[:], u[:], 1.0, None, ALU.add).then_inc(w1_r, 1)
                dve.wait_ge(w1_r, 1)
                step(dve.tensor_scalar(d[:], w1[:], -1.0, None, ALU.add))
                step.settle()
                step(dve.tensor_scalar(dz[:], d[:], 0.0, None, ALU.is_equal))
                step.settle()
                step(dve.tensor_tensor(d[:], d[:], dz[:], ALU.add))
                step.settle()
                step(dve.reciprocal(d[:], d[:]))
                step(dve.tensor_tensor(dz[:], dz[:], u[:], ALU.mult))
                dve.wait_ge(ln_r, 1)
                step(dve.tensor_tensor(ln[:], ln[:], u[:], ALU.mult))
                step.settle()
                step(dve.tensor_tensor(ln[:], ln[:], d[:], ALU.mult))
                step.settle()
                step(dve.tensor_tensor(ln[:], ln[:], dz[:], ALU.add))
                step.settle()
                dve.scalar_tensor_tensor(score[:], lg[:], 0.0, ln[:], ALU.max, ALU.add).then_inc(sp_r, 1)
                dve.wait_ge(c_in, 32)
                dve.wait_ge(score_r, 1)
                step(dve.tensor_tensor(pick[:], score[:], over(bias[:], 1, NT), ALU.add))
                step.settle()
                for j in range(NT):
                    step(dve.max(top8[:, j, :], pick[:, j, :]))
                step.settle()
                for j in range(NT):
                    step(dve.max_index(idx8[:, j, :], top8[:, j, :], pick[:, j, :]))
                step(dve.tensor_copy(iota_ef[:], iota_e[:]))
                step(dve.tensor_copy(spare_f[:], spare[:].rearrange("p j k -> p (j k)")))
                step(dve.tensor_copy(weight1[:], cst["tanhg"][:, 3:4].to_broadcast([P, NT + 2 * SUB])))
                step.settle()
                step(dve.tensor_copy(idxf[:], idx8[:, :, 0:K2]))
                step(dve.tensor_copy(table[:, 0:NT, 1].bitcast(F32), weight1[:, 0:NT]))
                step(dve.tensor_copy(table[:, COLS2 + NT:, 1].bitcast(F32), weight1[:, NT:]))
                step.settle()
                step(dve.tensor_tensor(hot[:], over(idxf[:].rearrange("p j k -> p (j k)"), 2, E2),
                                       over(iota_ef[:], 1, M), ALU.is_equal))
                step.settle()
                step(dve.tensor_reduce(mask[:], hot[:].rearrange("p (j k) e -> p j e k", k=K2), AX_X, ALU.add))
                step(dve.memset(pref[:, 0, :], 0.0))
                step.settle()
                for j in range(NT - 1):
                    step(dve.tensor_tensor(pref[:, j + 1, :], pref[:, j, :], mask[:, j, :], ALU.add))
                    step.settle()
                dve.engine_nop().then_inc(mask_r, 1)

                def chosen(out, values):
                    step(dve.tensor_tensor(tmp[:].rearrange("p (j k) e -> p j k e", k=K2),
                                           hot[:].rearrange("p (j k) e -> p j k e", k=K2), over(values, 2, K2),
                                           ALU.mult))
                    step.settle()
                    step(dve.tensor_reduce(out, tmp[:], AX_X, ALU.add))
                    step.settle()

                def per_expert(ap):
                    return ap[:].rearrange("p (j e) -> p j e", e=E2)

                chosen(s_k[:], score[:])
                step(dve.tensor_reduce(wsum[:], s_k[:].rearrange("p (j k) -> p j k", k=K2), AX_X, ALU.add))
                step.settle()
                step(dve.reciprocal(wsum[:], wsum[:]))
                step.settle()
                step(dve.tensor_scalar(wsum[:], wsum[:], cst["tanhg"][:, 3:4], None, ALU.mult))
                dve.wait_ge(pos_r, 1)
                step(dve.tensor_copy(pos[:], posp[:]))
                step.settle()
                step(dve.tensor_copy(pos_i[:], pos[:]))
                chosen(p_k[:], per_expert(pos))
                step(dve.tensor_scalar(valid[:], p_k[:], float(CAP), None, ALU.is_lt))
                step(dve.tensor_scalar(low[:], pos_i[:], P - 1, COLS2.bit_length() - 1, ALU.bitwise_and,
                                       ALU.logical_shift_left))
                step(dve.tensor_scalar(pos_i[:], pos_i[:], P.bit_length() - 1, None, ALU.logical_shift_right))
                step.settle()
                step(dve.tensor_tensor(low[:], low[:], pos_i[:], ALU.add))
                step.settle()
                step(dve.tensor_tensor(addr[:], low[:], e2[:].rearrange("p j e -> p (j e)"), ALU.add))
                step.settle()
                chosen(a_k[:], per_expert(addr))
                step(dve.tensor_tensor(a_k[:], a_k[:], spare_f[:], ALU.subtract))
                step.settle()
                step(dve.tensor_tensor(a_k[:], a_k[:], valid[:], ALU.mult))
                step(dve.tensor_tensor(s_k[:], s_k[:], valid[:], ALU.mult))
                step.settle()
                step(dve.tensor_tensor(slot[:], a_k[:], spare_f[:], ALU.add))
                step(dve.tensor_tensor(entry[:, :, :, 1].bitcast(F32), s_k[:].rearrange("p (j k) -> p j k", k=K2),
                                       over(wsum[:], 2, K2), ALU.mult))
                step(dve.tensor_copy(entry[:, :, :, 0], ids[:]))


def store(nc, acc, out):
    with ExitStack() as ctx:
        out_s = semaphores(nc, ctx, "o_")("out")
        with nc.Block() as block:
            @block.sync
            def _(sp):
                sp.dma_start(out.rearrange("(p n) d -> p (n d)", p=P),
                             acc[0:T, :].rearrange("(p n) d -> p (n d)", p=P)).then_inc(out_s, 16)
                sp.wait_ge(out_s, 16)


def two_layers(nc, a, out):
    with ExitStack() as ctx:
        def mem(name, shape, dt=F32):
            return ctx.enter_context(nc.sbuf_tensor(name, shape, dt))

        def sem(name):
            return ctx.enter_context(nc.semaphore(name))

        def dram(name, shape, dt=F32):
            return nc.dram_tensor(name, shape, dt, kind="Internal").ap()

        cst = constants(nc, mem, sem, a["gates"])
        for name in ("a_table_out", "b_table_out", "e_rows_in", "e_rows_added0", "e_rows_added1", "f_rows_in",
                     "f_rows_added0", "f_rows_added1"):
            cst[name] = sem(name)
        X = mem("X", [P, NT, D])
        rows_a, rows_b = dram("rows_a", (T + P, D)), dram("rows_b", (T + P, D))
        sum_a, sum_b = [dram("sum_a0", (T + P, D)), dram("sum_a1", (T + P, D))], dram("sum_b", (T + P, D))
        tab_a, tab_b = dram("tab_a", (32 * T, 2), I32), dram("tab_b", (E2 * CAP + K2 * T, 2), I32)
        plan = dram("plan", (1, P), I32)
        with ExitStack() as first:
            def mem1(name, shape, dt=F32):
                return first.enter_context(nc.sbuf_tensor(name, shape, dt))

            weights = Weights(mem1, sem, "e_", a["gu_a"], a["dn_a"])
            running = mem1("running", [P, 32])
            first_layer_attention(nc, cst, X, a["x"], a["ctxT"], a["wkT"], a["b_k"], a["gamma"], a["beta"],
                                  a["gate_kernel"], rows_a, tab_a, running, sum_a, weights)
            bounds, cols = mem1("bounds", [1, 33], I32), mem1("cols", [1, P], I32)
            table = mem1("table_a", [P, 32 * T // P, 2], I32)
            plan_tiles(nc, cst, running, bounds, cols, plan, tab_a, table)
            experts(nc, cst, "e_", rows_a, sum_a, table, weights, CHUNKS_A, PIECES_A, bounds, cols,
                    97, [], 15, [30, 31])
        second_attention_all(nc, cst, X, sum_a, a["ctx"], a["cos_k"], a["sin_k"], a["heads"], a["heads_qr"],
                             a["heads_v"], a["cos_q"], a["sin_q"])
        table = mem("table_b", [P, COLS2 + NT + 2 * SUB, 2], I32)
        weights = Weights(mem, sem, "f_", a["gu_b"], a["dn_b"])
        slot, entry = mem("slot_b", [P, NT * K2], I32), mem("entry_b", [P, NT, K2, 2], I32)
        second_layer_routing(nc, cst, X, a["gate_w"], a["gate_b"], rows_b, tab_b, table, slot, entry, sum_b,
                             weights)
        experts(nc, cst, "f_", rows_b, [sum_b, sum_b], table, weights, CHUNKS_B, PIECES_B,
                [0] + list(range(T // TILE, TILES2 + 1)), None, TILES2, [0], E2 // 2 - 1, [E2 - 1, E2],
                (slot, entry, tab_b, NT))
        store(nc, sum_b, out)


def rope(np, length, dim):
    inv = (1.0 / 10000.0 ** (np.arange(0, dim, 2, dtype=np.float32) / np.float32(dim))).astype(np.float32)
    f = np.arange(length, dtype=np.float32)[:, None] * inv[None]
    return np.repeat(np.sin(f), 2, -1).astype(np.float32), np.repeat(np.cos(f), 2, -1).astype(np.float32)


def rope_tables(np, order):
    s, c = rope(np, S, Q)
    s, c = s.T[order].reshape(QC, P, S).copy(), c.T[order].reshape(QC, P, S)
    s[0] *= -1
    low = s[2, :P // 2].copy()
    s[2, :P // 2], s[2, P // 2:] = s[2, P // 2:], -low
    sk, ck = rope(np, S, C)
    sk[:, :C // 2] *= -1
    return (np.ascontiguousarray(c.transpose(1, 0, 2)), np.ascontiguousarray(s.transpose(1, 0, 2)),
            np.ascontiguousarray(ck.reshape(SJ, P, C).transpose(1, 0, 2)),
            np.ascontiguousarray(sk.reshape(SJ, P, C).transpose(1, 0, 2)))


def kernel(**inputs):
    import numpy as np
    import concourse.bacc as bacc
    from concourse.bass_utils import run_bass_kernel_spmd as run

    v = {k: np.asarray(a) for k, a in inputs.items()}

    def lay(a):
        return np.ascontiguousarray(a)

    def chunked(a):
        return lay(np.moveaxis(a.reshape(*a.shape[:-2], DC, P, a.shape[-1]), -3, -2))

    h = 192 - P
    order = np.concatenate([np.arange(0, P), np.arange(Q // 2, Q // 2 + P), np.arange(P, Q // 2),
                            np.arange(Q // 2 + P, Q)])
    g, u, d = v["L0_ffn_gate_proj"], v["L0_ffn_up_proj"], v["L0_ffn_down_proj"]
    dn_a = np.zeros((32, P, 2, D), np.float32)
    dn_a[:, :h, 0], dn_a[:, :, 1] = d[:, P:], d[:, :P]
    g1 = np.concatenate([v["L1_ffn_Ws1"][None], v["L1_ffn_W1"]]).transpose(0, 2, 1)
    u1 = np.concatenate([v["L1_ffn_Ws3"][None], v["L1_ffn_W3"]]).transpose(0, 2, 1)
    d1 = np.concatenate([v["L1_ffn_Ws2"][None], v["L1_ffn_W2"]]).transpose(0, 2, 1)
    dn_b = np.zeros((E2 + 1, 3 * P, D), np.float32)
    dn_b[:, :d1.shape[1]] = d1
    wq = v["L1_xattn_Wq"].reshape(H, P, DC, P).transpose(0, 3, 2, 1).reshape(H, P, D)
    wkr = v["L1_xattn_W_kr"]
    wo = v["L1_xattn_Wo"].reshape(D, H, P).transpose(1, 2, 0)
    cos_q, sin_q, cos_k, sin_k = rope_tables(np, order)
    arrays = {
        "x": lay(v["x"].reshape(T, D)),
        "ctx": lay(v["ctx_512"].reshape(T, C)),
        "ctxT": lay(v["ctx_512"].transpose(0, 2, 1)),
        "gates": lay(np.concatenate([v["g_xattn"], v["g_ffn"]])),
        "wkT": lay(v["L0_xattn_W_k"].T),
        "b_k": lay(v["L0_xattn_b_k"]),
        "gamma": lay(v["L0_xattn_ln_gamma"]),
        "beta": lay(v["L0_xattn_ln_beta"]),
        "gate_kernel": chunked(v["L0_ffn_gate_kernel"]),
        "gu_a": chunked(np.concatenate([g[..., P:], u[..., P:], g[..., :P], u[..., :P]], -1)),
        "dn_a": dn_a,
        "heads": lay(np.concatenate([wq, v["L1_xattn_w_kc_q"][..., order], wkr, wkr], 2)),
        "heads_qr": lay(v["L1_xattn_W_qr"][:, order].reshape(H, QC, P, R).transpose(0, 2, 1, 3)),
        "heads_v": lay(np.concatenate([v["L1_xattn_w_kc_kv"], wo], 2)),
        "cos_q": cos_q, "sin_q": sin_q, "cos_k": cos_k, "sin_k": sin_k,
        "gate_w": chunked(v["L1_ffn_gate_w"].T),
        "gate_b": lay(v["L1_ffn_gate_b"]),
        "gu_b": chunked(np.concatenate([m[..., i * P:(i + 1) * P] for i in range(3) for m in (g1, u1)], -1)),
        "dn_b": lay(dn_b.reshape(E2 + 1, 3, P, D).transpose(0, 2, 1, 3)),
    }
    nc = bacc.Bacc("TRN2", target_bir_lowering=False, num_devices=1)
    ins = {k: nc.dram_tensor("in_" + k, a.shape, mybir.dt.from_np(a.dtype), kind="ExternalInput").ap()
           for k, a in arrays.items()}
    out = nc.dram_tensor("out", (T, D), F32, kind="ExternalOutput").ap()
    two_layers(nc, ins, out)
    got = run(nc, [{"in_" + k: a for k, a in arrays.items()}], core_ids=[0])
    return got.results[0]["out"].reshape(B, S, D)
```
